# Optimizing a Trainium2 kernel written in Bass

```python
import numpy as np
import jax
import jax.numpy as jnp

def _softmax(x, axis=-1):
    return jax.nn.softmax(x, axis=axis)

def _gelu(x):
    return jax.nn.gelu(x, approximate=True)

def _silu(x):
    return jax.nn.silu(x)

def _sigmoid(x):
    return jax.nn.sigmoid(x)

def _layernorm(x, axis=-1, eps=1e-05):
    m = jnp.mean(x, axis=axis, keepdims=True)
    v = jnp.var(x, axis=axis, keepdims=True)
    return (x - m) / jnp.sqrt(v + eps)

def _scatter_add(tgt, idx, src, axis=0):
    return tgt.at[idx].add(src)

def _segment_sum(src, seg, n):
    return jax.ops.segment_sum(src, seg, n)
kernel_name = 'mk_seq_postln_d2_jaxref_r8_2b8775'

def setup_inputs(seed: int=0):
    np.random.seed(seed)
    _w = jnp.asarray

    def _L0_attn_setup():
        import jax, jax.numpy as jnp
        import numpy as np
        C = 8.0
        B, S, D = (4, 512, 256)
        key = jax.random.key(seed)
        k1, k2, k3, k4 = jax.random.split(key, 4)
        x = jax.random.normal(k1, (B, S, D), dtype=jnp.float32)
        std = 1.0 / np.sqrt(D)
        Wa = jax.random.normal(k2, (D, D), dtype=jnp.float32) * std
        Wx = jax.random.normal(k3, (D, D), dtype=jnp.float32) * std
        ba = jnp.zeros((D,), dtype=jnp.float32)
        bx = jnp.zeros((D,), dtype=jnp.float32)
        u = jax.random.uniform(k4, (D,), minval=0.9, maxval=0.999, dtype=jnp.float32)
        Lam = -jnp.log(u ** (-1.0 / C) - 1.0)
        return {'x': x, 'Wa': Wa, 'Wx': Wx, 'ba': ba, 'bx': bx, 'Lam': Lam}
    _L0_attn_in = _L0_attn_setup()

    def _L0_ffn_setup():
        import jax, jax.numpy as jnp
        import numpy as np
        COST_LAMBDA = 1e-07
        HID = [128, 256, 384, 512, 128, 256, 384, 512]
        TOP_K = 2

        def _gelu(v):
            return jax.nn.gelu(v, approximate=False)

        def _forward(x, down_w, down_b, up_w, up_b, router_w, router_b, shared_w1, shared_b1, shared_w2, shared_b2, core_w, core_b, expert_params):
            E = len(expert_params)
            h = x @ down_w + down_b
            cost = jnp.array([w1.shape[0] * w1.shape[1] + w2.shape[0] * w2.shape[1] for w1, _, w2, _ in expert_params], jnp.float32)
            logits = x @ router_w + router_b - COST_LAMBDA * cost
            probs = jax.nn.softmax(logits, axis=-1)
            topv, topi = jax.lax.top_k(probs, TOP_K)
            gate = jax.nn.softmax(topv, axis=-1)
            out = jnp.zeros_like(h)
            for k in range(TOP_K):
                mask = jax.nn.one_hot(topi[..., k], E, dtype=h.dtype)
                acc = jnp.zeros_like(h)
                for e, (w1, b1, w2, b2) in enumerate(expert_params):
                    hm = h * mask[..., e:e + 1]
                    acc = acc + (_gelu(_gelu(hm) @ w1 + b1) @ w2 + b2)
                out = out + acc * gate[..., k:k + 1]
            out = out + 0.1 * (_gelu(_gelu(h) @ shared_w1 + shared_b1) @ shared_w2 + shared_b2)
            out = out @ up_w + up_b
            out = out + (_gelu(x) @ core_w + core_b)
            return out
        key = jax.random.key(seed)
        ks = iter(jax.random.split(key, 80))

        def W(shape):
            return jax.random.normal(next(ks), shape, jnp.float32) * 0.02
        B, T, D, L = (4, 256, 256, 128)
        inp = {'x': jax.random.normal(next(ks), (B, T, D), jnp.float32)}
        inp['down_w'] = W((D, L))
        inp['down_b'] = jnp.zeros((L,), jnp.float32)
        inp['up_w'] = W((L, D))
        inp['up_b'] = jnp.zeros((D,), jnp.float32)
        inp['router_w'] = W((D, len(HID)))
        inp['router_b'] = jnp.zeros((len(HID),), jnp.float32)
        inp['shared_w1'] = W((L, L))
        inp['shared_b1'] = jnp.zeros((L,), jnp.float32)
        inp['shared_w2'] = W((L, L))
        inp['shared_b2'] = jnp.zeros((L,), jnp.float32)
        inp['core_w'] = W((D, D))
        inp['core_b'] = jnp.zeros((D,), jnp.float32)
        for e, h in enumerate(HID):
            inp[f'e{e}_w1'] = W((L, h))
            inp[f'e{e}_b1'] = jnp.zeros((h,), jnp.float32)
            inp[f'e{e}_w2'] = W((h, L))
            inp[f'e{e}_b2'] = jnp.zeros((L,), jnp.float32)
        return inp
    _L0_ffn_in = _L0_ffn_setup()

    def _L1_attn_setup():
        import jax, jax.numpy as jnp
        import numpy as np
        H = 16
        EPS_DEN = 1e-06

        def _decay_scan(x, decay, init):
            xT = jnp.moveaxis(x, 2, 0)

            def step(s, xt):
                s = decay * s + xt
                return (s, s)
            _, ys = jax.lax.scan(step, init, xT)
            return jnp.moveaxis(ys, 0, 2)

        def _phi(z):
            return jax.nn.elu(z) + 1.0

        def _reference_tuple_inner(x, w_qkv, w_out, decay_param):
            B, T, Hid = x.shape
            D = Hid // H
            qkv = x @ w_qkv
            q, k, v = jnp.split(qkv, 3, axis=-1)

            def to_bhtd(t):
                return t.reshape(B, T, H, D).transpose(0, 2, 1, 3)
            q = _phi(to_bhtd(q))
            k = _phi(to_bhtd(k))
            v = to_bhtd(v)
            decay = jax.nn.sigmoid(decay_param).reshape(1, H, 1)
            init = jnp.zeros((B, H, D), dtype=x.dtype)
            running_kv = _decay_scan(k * v, decay, init)
            running_ksum = _decay_scan(k, decay, init)
            den = jnp.clip(jnp.sum(q * running_ksum, axis=-1, keepdims=True), EPS_DEN, None)
            out = q * running_kv / den
            out = out.transpose(0, 2, 1, 3).reshape(B, T, Hid) @ w_out
            new_kv = running_kv[:, :, -1, :]
            new_ksum = running_ksum[:, :, -1, :]
            return (out, new_kv, new_ksum)
        key = jax.random.key(seed)
        k1, k2, k3 = jax.random.split(key, 3)
        x = jax.random.normal(k1, (2, 512, 256), dtype=jnp.float32)
        w_qkv = jax.random.normal(k2, (256, 768), dtype=jnp.float32) * 0.02
        w_out = jax.random.normal(k3, (256, 256), dtype=jnp.float32) * 0.02
        decay_param = jnp.full((H,), 0.95, dtype=jnp.float32)
        return {'x': x, 'w_qkv': w_qkv, 'w_out': w_out, 'decay_param': decay_param}
    _L1_attn_in = _L1_attn_setup()

    def _L1_ffn_setup():
        import jax, jax.numpy as jnp
        import numpy as np
        B, S, D, H = (4, 256, 256, 1024)

        def fwht(x):
            orig_shape = x.shape
            n = orig_shape[-1]
            x = x.reshape(-1, n)
            h = 1
            while h < n:
                xb = x.reshape(-1, n // (2 * h), 2, h)
                a = xb[:, :, 0, :]
                b = xb[:, :, 1, :]
                x = jnp.stack([a + b, a - b], axis=2).reshape(-1, n)
                h *= 2
            scale = jnp.asarray(1.0 / np.sqrt(n), dtype=x.dtype)
            return (x * scale).reshape(orig_shape)
        key = jax.random.key(seed)
        kx, k1, k2, k3 = jax.random.split(key, 4)
        x = jax.random.normal(kx, (B, S, D), dtype=jnp.float32)
        W1 = jax.random.normal(k1, (H, D), dtype=jnp.float32) * (1.0 / np.sqrt(D))
        W2 = jax.random.normal(k2, (D, H), dtype=jnp.float32) * (1.0 / np.sqrt(H))
        W3 = jax.random.normal(k3, (H, D), dtype=jnp.float32) * (1.0 / np.sqrt(D))
        return {'x': x, 'W1': W1, 'W2': W2, 'W3': W3}
    _L1_ffn_in = _L1_ffn_setup()
    _d = {'L0_attn_x': _L0_attn_in['x'], 'L0_attn_Wa': _L0_attn_in['Wa'], 'L0_attn_Wx': _L0_attn_in['Wx'], 'L0_attn_ba': _L0_attn_in['ba'], 'L0_attn_bx': _L0_attn_in['bx'], 'L0_attn_Lam': _L0_attn_in['Lam'], 'L0_ffn_down_w': _L0_ffn_in['down_w'], 'L0_ffn_down_b': _L0_ffn_in['down_b'], 'L0_ffn_up_w': _L0_ffn_in['up_w'], 'L0_ffn_up_b': _L0_ffn_in['up_b'], 'L0_ffn_router_w': _L0_ffn_in['router_w'], 'L0_ffn_router_b': _L0_ffn_in['router_b'], 'L0_ffn_shared_w1': _L0_ffn_in['shared_w1'], 'L0_ffn_shared_b1': _L0_ffn_in['shared_b1'], 'L0_ffn_shared_w2': _L0_ffn_in['shared_w2'], 'L0_ffn_shared_b2': _L0_ffn_in['shared_b2'], 'L0_ffn_core_w': _L0_ffn_in['core_w'], 'L0_ffn_core_b': _L0_ffn_in['core_b'], 'L0_ffn_e0_w1': _L0_ffn_in['e0_w1'], 'L0_ffn_e0_b1': _L0_ffn_in['e0_b1'], 'L0_ffn_e0_w2': _L0_ffn_in['e0_w2'], 'L0_ffn_e0_b2': _L0_ffn_in['e0_b2'], 'L0_ffn_e1_w1': _L0_ffn_in['e1_w1'], 'L0_ffn_e1_b1': _L0_ffn_in['e1_b1'], 'L0_ffn_e1_w2': _L0_ffn_in['e1_w2'], 'L0_ffn_e1_b2': _L0_ffn_in['e1_b2'], 'L0_ffn_e2_w1': _L0_ffn_in['e2_w1'], 'L0_ffn_e2_b1': _L0_ffn_in['e2_b1'], 'L0_ffn_e2_w2': _L0_ffn_in['e2_w2'], 'L0_ffn_e2_b2': _L0_ffn_in['e2_b2'], 'L0_ffn_e3_w1': _L0_ffn_in['e3_w1'], 'L0_ffn_e3_b1': _L0_ffn_in['e3_b1'], 'L0_ffn_e3_w2': _L0_ffn_in['e3_w2'], 'L0_ffn_e3_b2': _L0_ffn_in['e3_b2'], 'L0_ffn_e4_w1': _L0_ffn_in['e4_w1'], 'L0_ffn_e4_b1': _L0_ffn_in['e4_b1'], 'L0_ffn_e4_w2': _L0_ffn_in['e4_w2'], 'L0_ffn_e4_b2': _L0_ffn_in['e4_b2'], 'L0_ffn_e5_w1': _L0_ffn_in['e5_w1'], 'L0_ffn_e5_b1': _L0_ffn_in['e5_b1'], 'L0_ffn_e5_w2': _L0_ffn_in['e5_w2'], 'L0_ffn_e5_b2': _L0_ffn_in['e5_b2'], 'L0_ffn_e6_w1': _L0_ffn_in['e6_w1'], 'L0_ffn_e6_b1': _L0_ffn_in['e6_b1'], 'L0_ffn_e6_w2': _L0_ffn_in['e6_w2'], 'L0_ffn_e6_b2': _L0_ffn_in['e6_b2'], 'L0_ffn_e7_w1': _L0_ffn_in['e7_w1'], 'L0_ffn_e7_b1': _L0_ffn_in['e7_b1'], 'L0_ffn_e7_w2': _L0_ffn_in['e7_w2'], 'L0_ffn_e7_b2': _L0_ffn_in['e7_b2'], 'L1_attn_w_qkv': _L1_attn_in['w_qkv'], 'L1_attn_w_out': _L1_attn_in['w_out'], 'L1_attn_decay_param': _L1_attn_in['decay_param'], 'L1_ffn_W1': _L1_ffn_in['W1'], 'L1_ffn_W2': _L1_ffn_in['W2'], 'L1_ffn_W3': _L1_ffn_in['W3']}
    _x0 = _d['L0_attn_x']
    _d['L0_attn_x'] = jax.random.normal(jax.random.fold_in(jax.random.key(seed), 1), (8, 256, 256), dtype=_x0.dtype)
    del _x0
    return _d

def reference(L0_attn_x, L0_attn_Wa, L0_attn_Wx, L0_attn_ba, L0_attn_bx, L0_attn_Lam, L0_ffn_down_w, L0_ffn_down_b, L0_ffn_up_w, L0_ffn_up_b, L0_ffn_router_w, L0_ffn_router_b, L0_ffn_shared_w1, L0_ffn_shared_b1, L0_ffn_shared_w2, L0_ffn_shared_b2, L0_ffn_core_w, L0_ffn_core_b, L0_ffn_e0_w1, L0_ffn_e0_b1, L0_ffn_e0_w2, L0_ffn_e0_b2, L0_ffn_e1_w1, L0_ffn_e1_b1, L0_ffn_e1_w2, L0_ffn_e1_b2, L0_ffn_e2_w1, L0_ffn_e2_b1, L0_ffn_e2_w2, L0_ffn_e2_b2, L0_ffn_e3_w1, L0_ffn_e3_b1, L0_ffn_e3_w2, L0_ffn_e3_b2, L0_ffn_e4_w1, L0_ffn_e4_b1, L0_ffn_e4_w2, L0_ffn_e4_b2, L0_ffn_e5_w1, L0_ffn_e5_b1, L0_ffn_e5_w2, L0_ffn_e5_b2, L0_ffn_e6_w1, L0_ffn_e6_b1, L0_ffn_e6_w2, L0_ffn_e6_b2, L0_ffn_e7_w1, L0_ffn_e7_b1, L0_ffn_e7_w2, L0_ffn_e7_b2, L1_attn_w_qkv, L1_attn_w_out, L1_attn_decay_param, L1_ffn_W1, L1_ffn_W2, L1_ffn_W3):

    def _L0_attn_ref(x, Wa, Wx, ba, bx, Lam):
        import jax, jax.numpy as jnp
        import numpy as np
        C = 8.0
        B, S, D = (4, 512, 256)
        r = jax.nn.sigmoid(jnp.einsum('bsd,hd->bsh', x, Wa) + ba)
        i = jax.nn.sigmoid(jnp.einsum('bsd,hd->bsh', x, Wx) + bx)
        log_a = -C * jax.nn.softplus(-Lam) * r
        a = jnp.exp(log_a)
        u = jnp.sqrt(1.0 - a ** 2) * (i * x)
        a_t = jnp.moveaxis(a, 1, 0)
        u_t = jnp.moveaxis(u, 1, 0)

        def step(h, au):
            at, ut = au
            h = at * h + ut
            return (h, h)
        h0 = jnp.zeros((x.shape[0], x.shape[2]), dtype=x.dtype)
        _, y = jax.lax.scan(step, h0, (a_t, u_t))
        return jnp.moveaxis(y, 0, 1)

    def _L0_ffn_ref(x, down_w, down_b, up_w, up_b, router_w, router_b, shared_w1, shared_b1, shared_w2, shared_b2, core_w, core_b, e0_w1, e0_b1, e0_w2, e0_b2, e1_w1, e1_b1, e1_w2, e1_b2, e2_w1, e2_b1, e2_w2, e2_b2, e3_w1, e3_b1, e3_w2, e3_b2, e4_w1, e4_b1, e4_w2, e4_b2, e5_w1, e5_b1, e5_w2, e5_b2, e6_w1, e6_b1, e6_w2, e6_b2, e7_w1, e7_b1, e7_w2, e7_b2):
        import jax, jax.numpy as jnp
        import numpy as np
        COST_LAMBDA = 1e-07
        HID = [128, 256, 384, 512, 128, 256, 384, 512]
        TOP_K = 2

        def _gelu(v):
            return jax.nn.gelu(v, approximate=False)

        def _forward(x, down_w, down_b, up_w, up_b, router_w, router_b, shared_w1, shared_b1, shared_w2, shared_b2, core_w, core_b, expert_params):
            E = len(expert_params)
            h = x @ down_w + down_b
            cost = jnp.array([w1.shape[0] * w1.shape[1] + w2.shape[0] * w2.shape[1] for w1, _, w2, _ in expert_params], jnp.float32)
            logits = x @ router_w + router_b - COST_LAMBDA * cost
            probs = jax.nn.softmax(logits, axis=-1)
            topv, topi = jax.lax.top_k(probs, TOP_K)
            gate = jax.nn.softmax(topv, axis=-1)
            out = jnp.zeros_like(h)
            for k in range(TOP_K):
                mask = jax.nn.one_hot(topi[..., k], E, dtype=h.dtype)
                acc = jnp.zeros_like(h)
                for e, (w1, b1, w2, b2) in enumerate(expert_params):
                    hm = h * mask[..., e:e + 1]
                    acc = acc + (_gelu(_gelu(hm) @ w1 + b1) @ w2 + b2)
                out = out + acc * gate[..., k:k + 1]
            out = out + 0.1 * (_gelu(_gelu(h) @ shared_w1 + shared_b1) @ shared_w2 + shared_b2)
            out = out @ up_w + up_b
            out = out + (_gelu(x) @ core_w + core_b)
            return out
        ep = [(e0_w1, e0_b1, e0_w2, e0_b2), (e1_w1, e1_b1, e1_w2, e1_b2), (e2_w1, e2_b1, e2_w2, e2_b2), (e3_w1, e3_b1, e3_w2, e3_b2), (e4_w1, e4_b1, e4_w2, e4_b2), (e5_w1, e5_b1, e5_w2, e5_b2), (e6_w1, e6_b1, e6_w2, e6_b2), (e7_w1, e7_b1, e7_w2, e7_b2)]
        return _forward(x, down_w, down_b, up_w, up_b, router_w, router_b, shared_w1, shared_b1, shared_w2, shared_b2, core_w, core_b, ep)

    def _L1_attn_ref(x, w_qkv, w_out, decay_param):
        import jax, jax.numpy as jnp
        import numpy as np
        H = 16
        EPS_DEN = 1e-06

        def _decay_scan(x, decay, init):
            xT = jnp.moveaxis(x, 2, 0)

            def step(s, xt):
                s = decay * s + xt
                return (s, s)
            _, ys = jax.lax.scan(step, init, xT)
            return jnp.moveaxis(ys, 0, 2)

        def _phi(z):
            return jax.nn.elu(z) + 1.0

        def _reference_tuple_inner(x, w_qkv, w_out, decay_param):
            B, T, Hid = x.shape
            D = Hid // H
            qkv = x @ w_qkv
            q, k, v = jnp.split(qkv, 3, axis=-1)

            def to_bhtd(t):
                return t.reshape(B, T, H, D).transpose(0, 2, 1, 3)
            q = _phi(to_bhtd(q))
            k = _phi(to_bhtd(k))
            v = to_bhtd(v)
            decay = jax.nn.sigmoid(decay_param).reshape(1, H, 1)
            init = jnp.zeros((B, H, D), dtype=x.dtype)
            running_kv = _decay_scan(k * v, decay, init)
            running_ksum = _decay_scan(k, decay, init)
            den = jnp.clip(jnp.sum(q * running_ksum, axis=-1, keepdims=True), EPS_DEN, None)
            out = q * running_kv / den
            out = out.transpose(0, 2, 1, 3).reshape(B, T, Hid) @ w_out
            new_kv = running_kv[:, :, -1, :]
            new_ksum = running_ksum[:, :, -1, :]
            return (out, new_kv, new_ksum)
        return _reference_tuple_inner(x, w_qkv, w_out, decay_param)[0]

    def _L1_ffn_ref(x, W1, W2, W3):
        import jax, jax.numpy as jnp
        import numpy as np
        B, S, D, H = (4, 256, 256, 1024)

        def fwht(x):
            orig_shape = x.shape
            n = orig_shape[-1]
            x = x.reshape(-1, n)
            h = 1
            while h < n:
                xb = x.reshape(-1, n // (2 * h), 2, h)
                a = xb[:, :, 0, :]
                b = xb[:, :, 1, :]
                x = jnp.stack([a + b, a - b], axis=2).reshape(-1, n)
                h *= 2
            scale = jnp.asarray(1.0 / np.sqrt(n), dtype=x.dtype)
            return (x * scale).reshape(orig_shape)
        up_gate = jnp.einsum('bsd,hd->bsh', x, W1)
        up_lin = jnp.einsum('bsd,hd->bsh', x, W3)
        hidden = jax.nn.silu(up_gate) * up_lin
        hidden = fwht(hidden)
        out = jnp.einsum('bsh,dh->bsd', hidden, W2)
        return out
    x = L0_attn_x
    x = _layernorm(x + _L0_attn_ref(x, L0_attn_Wa, L0_attn_Wx, L0_attn_ba, L0_attn_bx, L0_attn_Lam), axis=-1)
    x = _layernorm(x + _L0_ffn_ref(x, L0_ffn_down_w, L0_ffn_down_b, L0_ffn_up_w, L0_ffn_up_b, L0_ffn_router_w, L0_ffn_router_b, L0_ffn_shared_w1, L0_ffn_shared_b1, L0_ffn_shared_w2, L0_ffn_shared_b2, L0_ffn_core_w, L0_ffn_core_b, L0_ffn_e0_w1, L0_ffn_e0_b1, L0_ffn_e0_w2, L0_ffn_e0_b2, L0_ffn_e1_w1, L0_ffn_e1_b1, L0_ffn_e1_w2, L0_ffn_e1_b2, L0_ffn_e2_w1, L0_ffn_e2_b1, L0_ffn_e2_w2, L0_ffn_e2_b2, L0_ffn_e3_w1, L0_ffn_e3_b1, L0_ffn_e3_w2, L0_ffn_e3_b2, L0_ffn_e4_w1, L0_ffn_e4_b1, L0_ffn_e4_w2, L0_ffn_e4_b2, L0_ffn_e5_w1, L0_ffn_e5_b1, L0_ffn_e5_w2, L0_ffn_e5_b2, L0_ffn_e6_w1, L0_ffn_e6_b1, L0_ffn_e6_w2, L0_ffn_e6_b2, L0_ffn_e7_w1, L0_ffn_e7_b1, L0_ffn_e7_w2, L0_ffn_e7_b2), axis=-1)
    x = _layernorm(x + _L1_attn_ref(x, L1_attn_w_qkv, L1_attn_w_out, L1_attn_decay_param), axis=-1)
    x = _layernorm(x + _L1_ffn_ref(x, L1_ffn_W1, L1_ffn_W2, L1_ffn_W3), axis=-1)
    return x

_drawn_inputs = setup_inputs


def setup_inputs(seed=0):
    import zlib

    import numpy as np

    out = dict(_drawn_inputs(seed))
    spreads = {'L0_attn_ba': (0.0, 0.8),
     'L0_attn_bx': (0.0, 0.455),
     'L0_ffn_down_b': (0.0, 0.8),
     'L0_ffn_up_b': (0.0, 0.1),
     'L0_ffn_router_b': (0.0, 0.8),
     'L0_ffn_shared_b1': (0.0, 2.0),
     'L0_ffn_shared_b2': (0.0, 2.0),
     'L0_ffn_core_b': (0.0, 0.1),
     'L0_ffn_e0_b1': (0.0, 0.8),
     'L0_ffn_e0_b2': (0.0, 0.323),
     'L0_ffn_e1_b1': (0.0, 0.8),
     'L0_ffn_e1_b2': (0.0, 0.315),
     'L0_ffn_e2_b1': (0.0, 0.8),
     'L0_ffn_e2_b2': (0.0, 0.309),
     'L0_ffn_e3_b1': (0.0, 0.8),
     'L0_ffn_e3_b2': (0.0, 0.359),
     'L0_ffn_e4_b1': (0.0, 0.8),
     'L0_ffn_e4_b2': (0.0, 0.297),
     'L0_ffn_e5_b1': (0.0, 0.8),
     'L0_ffn_e5_b2': (0.0, 0.354),
     'L0_ffn_e6_b1': (0.0, 0.8),
     'L0_ffn_e6_b2': (0.0, 0.283),
     'L0_ffn_e7_b1': (0.0, 0.8),
     'L0_ffn_e7_b2': (0.0, 0.327),
     'L1_attn_decay_param': (0.949999988079071, 0.6)}
    factors = {'L0_ffn_down_w': 8.0,
     'L0_ffn_router_w': 8.0,
     'L0_ffn_shared_w1': 8.0,
     'L0_ffn_shared_w2': 8.0,
     'L0_ffn_e0_w1': 8.0,
     'L0_ffn_e0_w2': 8.0,
     'L0_ffn_e1_w1': 8.0,
     'L0_ffn_e1_w2': 8.0,
     'L0_ffn_e2_w1': 8.0,
     'L0_ffn_e2_w2': 8.0,
     'L0_ffn_e3_w1': 8.0,
     'L0_ffn_e3_w2': 8.0,
     'L0_ffn_e4_w1': 8.0,
     'L0_ffn_e4_w2': 8.0,
     'L0_ffn_e5_w1': 8.0,
     'L0_ffn_e5_w2': 8.0,
     'L0_ffn_e6_w1': 8.0,
     'L0_ffn_e6_w2': 8.0,
     'L0_ffn_e7_w1': 8.0,
     'L0_ffn_e7_w2': 8.0,
     'L1_attn_w_qkv': 8.0,
     'L1_attn_w_out': 8.0}
    for name, (base, spread) in spreads.items():
        noise = np.random.default_rng([zlib.crc32(name.encode()), seed]).standard_normal(out[name].shape)
        drawn = base * np.exp(spread * noise) if base else spread * noise
        out[name] = jnp.asarray(drawn.astype(out[name].dtype))
    for name, factor in factors.items():
        out[name] = (out[name] * factor).astype(out[name].dtype)
    return out
```

```python
import concourse.bass as bass
from concourse import mybir
from contextlib import ExitStack

HID = [128, 256, 384, 512, 128, 256, 384, 512]
E = len(HID)
D = 256
L = 128
FF = 1024
SEQ = 256
CHUNK = 512
CT = D // 128
NB = CHUNK // 128
HEADS, HEAD = 16, 16
FT = FF // 128
TILES = [(-1, 0)] + [(e, j) for e in range(E) for j in range(HID[e] // 128)]
NT = len(TILES)
LAG = 3
EPS = 1e-5
COST = [1e-7 * 2 * L * h for h in HID]

_at = 0


def _cols(n):
    global _at
    _at += n
    return _at - n


WA = _cols(CT * D)
WX = _cols(CT * D)
DOWN = _cols(CT * L)
ROUTER = _cols(CT * E)
SW1 = _cols(L)
SW2 = _cols(L)
CORE = _cols(CT * D)
UP = _cols(D)
EXPERTS = _at
EW1, EW2 = [], []
for _h in HID:
    EW1.append(_cols(_h))
    EW2.append(_cols(_h))
QKV = _cols(CT * 3 * D)
WOUT = _cols(CT * D)
W1 = _cols(CT * FF)
W3 = _cols(CT * FF)
W2 = _cols(FT * D)
WCOLS = _at
PIECE = 512
EXPERT_PIECES = (QKV - EXPERTS) // PIECE
ATTN_PIECES = (W1 - QKV) // PIECE
FFN_PIECES = (W2 - W1) // PIECE
PIECES = EXPERT_PIECES + ATTN_PIECES + FFN_PIECES

V_BA, V_BX, V_LAM, V_DOWN, V_S1, V_S2, V_E1, V_E2, V_DEC = 0, 2, 4, 6, 7, 8, 9, 9 + NT - 1, 9 + NT - 1 + E
VCOLS = V_DEC + CT
C_ID, C_HAD, C_HEAD, C_REV, C_COST = 0, 128, 256, 256 + CT * HEADS, 256 + CT * HEADS + NB * E
CCOLS = C_COST + NB * E


def program(nc, x_in, weights, vectors, rows, consts, out):
    f32, f32r = mybir.dt.float32, mybir.dt.float32r
    ALU, ACT, AX = mybir.AluOpType, mybir.ActivationFunctionType, mybir.AxisListType
    chunks = x_in.shape[1] // CHUNK
    x_chunks = x_in.rearrange("(c p) (k t) -> k p c t", p=128, t=CHUNK)
    out_chunks = out.rearrange("(k b p) n -> k p b n", b=NB, p=128)
    gates_dram = nc.dram_tensor("gates_scratch", (chunks, E, CHUNK), f32, kind="Internal").ap()

    with ExitStack() as ctx:
        def sb(name, shape, dt=f32):
            return ctx.enter_context(nc.sbuf_tensor(name, shape, dt))

        wh = sb("weights_hi", [128, WCOLS], f32r)
        wl = sb("weights_lo", [128, WCOLS], f32r)
        xy = sb("x_then_y", [128, CT, CHUNK])
        chan_h = sb("chan_hi", [128, CT, CHUNK], f32r)
        chan_l = sb("chan_lo", [128, CT, CHUNK], f32r)
        mid_h = sb("mid_hi", [128, CT, CHUNK], f32r)
        mid_l = sb("mid_lo", [128, CT, CHUNK], f32r)
        ffn_h = sb("ffn_hi", [128, CT, CHUNK], f32r)
        ffn_l = sb("ffn_lo", [128, CT, CHUNK], f32r)
        tok = sb("tok", [128, NB, D])
        tok3 = sb("tok3", [128, NB, D])
        gate = sb("gate_rows", [128, 2, CHUNK])
        ac = sb("gate_attn_work", [128, 7, CHUNK])
        hid = sb("hidden", [128, 5, CHUNK])
        sh = sb("hidden_hi", [128, 4, CHUNK], f32r)
        sl = sb("hidden_lo", [128, 4, CHUNK], f32r)
        cst = sb("consts", [128, CCOLS])
        vec = sb("vectors", [128, VCOLS])
        bias_uc = sb("bias_up_core", [128, D])
        bias_r = sb("bias_router", [128, NB * E])
        half_b = sb("half_gate_bias", [128, 2 * CT])
        c2 = sb("half_log_decay", [128, CT])
        nc2 = sb("neg_half_log_decay", [128, CT])
        ser = sb("softplus_work", [128, 5, CT])
        s2b = sb("shared_bias_tenth", [128, 1])
        decay = sb("attn_decay", [128, CT])
        b1g = sb("gelu_of_bias", [128, NT - 1])
        b1s = sb("gelu_of_bias_split", [128, NT - 1, 2], f32r)
        idle2 = sb("idle_parts", [128, 2 * E])
        idle = sb("idle_expert", [128, E])
        idle_sum = sb("idle_sum", [128, 2])
        neg_half = sb("neg_half", [128, NB])
        rt = sb("routing", [128, 9, NB * E])
        r4 = sb("routing_per_token", [128, 12, NB])
        gt = hid[0:NB * E, 3, 0:128]
        lg = hid[0:E, 4, :]
        rden = sb("denominators", [128, NB * HEADS])
        st = [sb(f"ln{i}_stats", [128, NB, 6]) for i in range(4)]
        mv = [sb(f"ln{i}_mean_var", [128, NB, 2]) for i in range(4)]
        rs = [sb(f"ln{i}_rstd", [128, 2, NB]) for i in range(4)]
        ident = cst[:, C_ID:C_ID + 128]
        R = [ctx.enter_context(nc.psum_tensor(f"R{i}", [128, CHUNK], f32)) for i in range(6)]
        M = [ctx.enter_context(nc.psum_tensor(f"M{i}", [128, CHUNK], f32)) for i in range(2)]

        class Signal:

            def __init__(self, name, per=1, by=1):
                self.sem, self.per, self.by = ctx.enter_context(nc.semaphore(name)), per, by

            def nth(self, k, i=0):
                return (k * self.per + i + 1) * self.by

        def later(k):
            return not isinstance(k, int) or k > 0

        def more_chunks(k):
            return not isinstance(k, int) or k < chunks - 1

        wait_carried = Signal("wait_carried")

        def apart(eng):
            eng.sem_inc(wait_carried.sem, 1)

        S = Signal
        x_loaded, gates_stored = S("x_loaded", 1, 16), S("gates_stored", 1, 16)
        row_loaded = [S(f"gate_row_loaded{i}", E // 2, 16) for i in range(2)]
        out_stored = S("out_stored", 1, 16)
        small_loaded, w0_loaded, w1_loaded = S("small_loaded", 1, 16), S("w_gates_loaded", 1, 16), S("w_dense_loaded", 1, 16)
        rows_loaded, vec_loaded = S("rows_loaded", 1, 16), S("vec_loaded", 1, 16)
        piece_loaded = [S(f"piece_loaded{i}", 1, 16) for i in range(2)]
        w2_loaded = S("w2_loaded", 1, 16)
        dense_hi, dense_lo = S("dense_hi"), S("dense_lo")
        exp_hi, exp_lo = S("expert_w_hi"), S("expert_w_lo")
        att_hi, att_lo = S("attn_w_hi"), S("attn_w_lo")
        ffn_w_hi, ffn_w_lo = S("ffn_w_hi"), S("ffn_w_lo")
        had_step, had_z, had_hi, had_lo = S("had_step"), S("had_z"), S("had_hi"), S("had_lo")
        setup_act, setup_dve, idle_z = S("setup_act"), S("setup_dve"), S("idle_z")
        x_hi, x_lo, gate_z = S("x_hi"), S("x_lo"), S("gate_z", 4)
        tanh_r, tanh_i, a_exp, a_tanh, a_sq = (S(n, CT) for n in ("tanh_r", "tanh_i", "a_exp", "a_tanh", "a_square"))
        a_cut, w_ready, w_root = S("a_cut"), S("w_ready", CT), S("w_root")
        ix_ready, u_ready, h_ready, y_ready = S("ix_ready"), S("u_ready"), S("h_ready"), S("y_ready")
        y_turned, x1_turned = S("y_turned", 2), S("x1_turned", 2)
        x1_hi, x1_lo, resid1 = S("x1_hi", 2), S("x1_lo", 2), S("resid1")
        ln_stats = [S(f"ln{i}_stats_s", NB) for i in range(4)]
        ln_mv = [S(f"ln{i}_mv_s", NB) for i in range(4)]
        ln_var = [S(f"ln{i}_var_s") for i in range(4)]
        ln_rstd = [S(f"ln{i}_rstd_s") for i in range(4)]
        ln_done = [S(f"ln{i}_done", NB) for i in range(4)]
        logit_z, logit_copied, logit_turned = S("logit_z"), S("logit_copied"), S("logit_turned")
        ROUTE = 22
        route, route_exp, route_tanh = S("route", ROUTE), S("route_exp"), S("route_tanh")
        gate_turned, gate_copied = S("gate_turned"), S("gate_copied")
        down_z, h_act, h_hi, h_lo = S("down_z"), S("h_act"), S("h_hi"), S("h_lo")
        x1_sum, g1_act, g1_hi, g1_lo = S("x1_sum"), S("g1_act"), S("g1_hi"), S("g1_lo")
        hid_z, hid_act, hid_hi, hid_lo, hid_used = (S(n, NT) for n in ("hid_z", "hid_act", "hid_hi", "hid_lo", "hid_used"))
        combined, summed = S("combined", E + 1), S("summed", E)
        m_hi, m_lo, moe_out, y2_ready = S("m_hi"), S("m_lo"), S("moe_out", 2), S("y2_ready", 2)
        x2_turned, x2_hi, x2_lo = S("x2_turned", 2), S("x2_hi", 2), S("x2_lo", 2)
        qkv_z = S("qkv_z", 6)
        k_exp, k_min, k_phi, kv_ready, q_exp, q_min, q_phi = (S(n, CT) for n in ("k_exp", "k_min", "k_phi", "kv_ready", "q_exp", "q_min", "q_phi"))
        scanned, qk_ready, num_ready = S("scanned", 4 * CT), S("qk_ready", CT), S("num_ready", CT)
        den_z, den_copied, den_turned, den_max, den_inv, den_wide = (S(n) for n in ("den_z", "den_copied", "den_turned", "den_max", "den_inv", "den_wide"))
        inv_turned, o_ready, o_hi, o_lo = S("inv_turned", 2), S("o_ready", 2), S("o_hi"), S("o_lo")
        attn_out, y3_ready = S("attn_out", 2), S("y3_ready", 2)
        x3_turned, x3_hi, x3_lo = S("x3_turned", 2), S("x3_hi", 2), S("x3_lo", 2)
        ff_z, ff_tanh, ff_silu, ff_hid, ff_hi, ff_lo, ff_used = (S(n, FT) for n in ("ff_z", "ff_tanh", "ff_silu", "ff_hid", "ff_hi", "ff_lo", "ff_used"))
        y4_ready = S("y4_ready", 2)

        block = ctx.enter_context(nc.Block())

        def last_tile(o):
            return max(t for t, (e, _) in enumerate(TILES) if e == o - 1)

        @block.sync
        def _(sp):
            def piece(n):
                if n >= 2:
                    m = n - 2
                    if m < EXPERT_PIECES:
                        sp.wait_ge(exp_lo.sem, exp_lo.nth(m))
                    elif m < EXPERT_PIECES + ATTN_PIECES:
                        sp.wait_ge(att_lo.sem, att_lo.nth(m - EXPERT_PIECES))
                    else:
                        sp.wait_ge(ffn_w_lo.sem, ffn_w_lo.nth(m - EXPERT_PIECES - ATTN_PIECES))
                c = EXPERTS + n * PIECE
                sp.dma_start(tok3[:].rearrange("p b n -> p (b n)")[:, (n % 2) * PIECE:(n % 2 + 1) * PIECE],
                             weights[:, c:c + PIECE]).then_inc(piece_loaded[n % 2].sem, 16)

            def load_x(k):
                if later(k):
                    sp.wait_ge(y_turned.sem, y_turned.nth(k - 1, 1))
                sp.dma_start(xy[:], x_chunks[k]).then_inc(x_loaded.sem, 16)

            def store_gates(k):
                sp.wait_ge(gate_copied.sem, gate_copied.nth(k))
                sp.dma_start(gates_dram[k].rearrange("e (b t) -> (e b) t", t=128), gt).then_inc(gates_stored.sem, 16)

            def gate_row(k, e):
                sp.wait_ge(gates_stored.sem, gates_stored.nth(k))
                if e < 2:
                    sp.wait_ge(resid1.sem, resid1.nth(k))
                    sp.wait_ge(x1_turned.sem, x1_turned.nth(k, 1))
                else:
                    sp.wait_ge(combined.sem, combined.nth(k, e + 1 - 2))
                sp.dma_start(gate[:, e % 2, :], gates_dram[k][e].partition_broadcast(128)).then_inc(row_loaded[e % 2].sem, 16)

            def store_out(k):
                sp.wait_ge(ln_done[3].sem, ln_done[3].nth(k, NB - 1))
                sp.dma_start(out_chunks[k], hid[:, 3:5, :].rearrange("p a (b n) -> p (a b) n", n=D)).then_inc(out_stored.sem, 16)

            flat = hid[:].rearrange("p a n -> p (a n)")
            sp.dma_start(flat[:, 0:DOWN], weights[:, 0:DOWN]).then_inc(w0_loaded.sem, 16)
            sp.dma_start(xy[:], x_chunks[0]).then_inc(x_loaded.sem, 16)
            sp.dma_start(flat[:, DOWN:EXPERTS], weights[:, DOWN:EXPERTS]).then_inc(w1_loaded.sem, 16)
            piece(0)
            piece(1)
            load_done = EXPERT_PIECES
            for n in range(2, 6):
                piece(n)
            load_x(1)
            store_gates(0)
            gate_row(0, 0)
            gate_row(0, 1)
            for n in range(6, load_done):
                piece(n)
            n = load_done
            for e in range(2, E):
                gate_row(0, e)
                if n < EXPERT_PIECES + ATTN_PIECES:
                    piece(n)
                    n += 1
            sp.wait_ge(hid_lo.sem, hid_lo.nth(0, NT - 1))
            sp.wait_ge(m_lo.sem, m_lo.nth(0))
            sp.dma_start(flat[:, 0:FT * D], weights[:, W2:WCOLS]).then_inc(w2_loaded.sem, 16)
            for n in range(n, PIECES - 2):
                piece(n)
            load_x(2)
            piece(PIECES - 2)
            piece(PIECES - 1)
            store_gates(1)
            gate_row(1, 0)
            gate_row(1, 1)

            sp.sem_inc(out_stored.sem, 16)

            def a_round(r, more):
                for e in range(2, E):
                    gate_row(r, e)
                if more == 2:
                    load_x(r + 2)
                if more:
                    store_gates(r + 1)
                    gate_row(r + 1, 0)
                    gate_row(r + 1, 1)
                store_out(r - 1)

            a_round(1, 2)
            with sp.Fori(2, chunks - 1) as r:
                a_round(r, 1)
            a_round(chunks - 1, 0)
            store_out(chunks - 1)
            sp.wait_ge(out_stored.sem, out_stored.nth(chunks))
            sp.wait_ge(gates_stored.sem, gates_stored.nth(chunks - 1))

        @block.tensor
        def _(pe):
            def product(out, a, b, start=True, stop=True, shared=False):
                (ah, al), (bh, bl) = a, b
                pe.matmul(out, ah, bh, start=start, stop=False, skip_group_check=shared)
                pe.matmul(out, ah, bl, start=False, stop=False, skip_group_check=shared)
                return pe.matmul(out, al, bh, start=False, stop=stop, skip_group_check=shared)

            def w(c, n=128):
                return wh[:, c:c + n], wl[:, c:c + n]

            def two(h, l, i, lo=0, n=CHUNK):
                return h[:, i, lo:lo + n], l[:, i, lo:lo + n]

            def gates(k, c, after):
                pe.wait_ge(x_lo.sem, x_lo.nth(k))
                for g, base in enumerate((WA, WX)):
                    if c == 0:
                        after(g)
                    else:
                        pe.wait_ge((tanh_r, tanh_i)[g].sem, (tanh_r, tanh_i)[g].nth(k, c - 1))
                    for kt in range(CT):
                        last = product(M[g][:], w(base + kt * D + c * 128), two(chan_h, chan_l, kt), kt == 0, kt == CT - 1)
                    last.then_inc(gate_z.sem, 1)

            def to_tokens(src, done):
                for b in range(NB):
                    for c in range(CT):
                        last = pe.transpose(M[b // 2][:, (b % 2) * D + c * 128:(b % 2) * D + (c + 1) * 128],
                                            src[:, c, b * 128:(b + 1) * 128], ident)
                    if b % 2:
                        last.then_inc(done.sem, 1)

            def to_channels(src, done):
                for c in range(CT):
                    for b in range(NB):
                        last = pe.transpose(M[c][:, b * 128:(b + 1) * 128], src[:, b, c * 128:(c + 1) * 128], ident)
                    last.then_inc(done.sem, 1)

            gate_tok = gate[:].rearrange("p a (b n) -> p (a b) n", n=D)

            def turn_y(k, after):
                pe.wait_ge(y_ready.sem, y_ready.nth(k))
                after()
                to_tokens(xy, y_turned)

            def turn_x1(k, after):
                pe.wait_ge(ln_done[0].sem, ln_done[0].nth(k, NB - 1))
                after()
                to_channels(gate_tok, x1_turned)

            def logits(k, after):
                pe.wait_ge(x1_lo.sem, x1_lo.nth(k, CT - 1))
                after()
                for kt in range(CT):
                    last = product(M[0][:], w(ROUTER + kt * E), two(chan_h, chan_l, kt), kt == 0, kt == CT - 1)
                last.then_inc(logit_z.sem, 1)

            def turn_logits(k):
                pe.wait_ge(logit_copied.sem, logit_copied.nth(k))
                apart(pe)
                for b in range(NB):
                    last = pe.transpose(M[0][:, b * E:(b + 1) * E], lg[:, b * 128:(b + 1) * 128], ident[0:E, 0:E])
                last.then_inc(logit_turned.sem, 1)

            def turn_gates(k, after):
                pe.wait_ge(route.sem, route.nth(k, ROUTE - 1))
                after()
                pe.transpose(M[1][0:NB * E, 0:128], rt[:, 8, :], ident).then_inc(gate_turned.sem, 1)

            def down(k, after):
                pe.wait_ge(x1_lo.sem, x1_lo.nth(k, CT - 1))
                after()
                for kt in range(CT):
                    last = product(M[1][:], w(DOWN + kt * L), two(chan_h, chan_l, kt), kt == 0, kt == CT - 1)
                last.then_inc(down_z.sem, 1)

            def idle_experts():
                pe.wait_ge(setup_dve.sem, setup_dve.nth(IDLE_SPLIT))
                for t, (e, j) in enumerate(TILES[1:]):
                    if j == 0:
                        pe.wait_ge(exp_lo.sem, exp_lo.nth((EW2[e] + HID[e] - EXPERTS - 1) // PIECE))
                    pe.matmul(R[3][:, 2 * e:2 * e + 2], wh[:, EW2[e] + j * 128:EW2[e] + (j + 1) * 128], b1s[:, t, :],
                              start=j == 0, stop=False)
                    last = pe.matmul(R[3][:, 2 * e:2 * e + 2], wl[:, EW2[e] + j * 128:EW2[e] + (j + 1) * 128], b1s[:, t, :],
                                     start=False, stop=j == HID[e] // 128 - 1)
                last.then_inc(idle_z.sem, 1)

            def first(k, t):
                e, j = TILES[t]
                if t == 0:
                    pe.wait_ge(h_lo.sem, h_lo.nth(k))
                if t < 3:
                    if later(k):
                        pe.wait_ge(ff_hid.sem, ff_hid.nth(k - 1, FT - 1))
                else:
                    pe.wait_ge(hid_act.sem, hid_act.nth(k, t - 3))
                product(R[t % 3][:], w(SW1 if e < 0 else EW1[e] + j * 128), two(sh, sl, 3)).then_inc(hid_z.sem, 1)

            def second(k, t):
                e, j = TILES[t]
                o = e + 1
                pe.wait_ge(hid_lo.sem, hid_lo.nth(k, t))
                if j == 0:
                    if o < 3:
                        if later(k):
                            pe.wait_ge(y4_ready.sem, y4_ready.nth(k - 1, 1))
                        if isinstance(k, int) and k == 0 and o == 0:
                            pe.wait_ge(setup_dve.sem, setup_dve.nth(IDLE_COPIED))
                    else:
                        pe.wait_ge(combined.sem, combined.nth(k, o - 3))
                n = 1 if e < 0 else HID[e] // 128
                product(R[3 + o % 3][:], w(SW2 if e < 0 else EW2[e] + j * 128), two(sh, sl, t % 3), j == 0, j == n - 1)\
                    .then_inc(hid_used.sem, 1)

            def moe_product(k, after):
                pe.wait_ge(g1_lo.sem, g1_lo.nth(k))
                after()
                for b in range(NB):
                    for kt in range(CT):
                        product(M[b // 2][:, (b % 2) * D:(b % 2 + 1) * D], two(mid_h, mid_l, kt, b * 128, 128),
                                w(CORE + kt * D, D), b % 2 == 0 and kt == 0, False, shared=True)
                pe.wait_ge(m_lo.sem, m_lo.nth(k))
                for b in range(NB):
                    last = product(M[b // 2][:, (b % 2) * D:(b % 2 + 1) * D], two(sh, sl, 3, b * 128, 128), w(UP, D),
                                   False, True, shared=True)
                    if b % 2:
                        last.then_inc(moe_out.sem, 1)

            def turn_x2(k, after):
                pe.wait_ge(ln_done[1].sem, ln_done[1].nth(k, NB - 1))
                after()
                to_channels(tok, x2_turned)

            def qkv(k, bank, which, c, after):
                pe.wait_ge(x2_lo.sem, x2_lo.nth(k, CT - 1))
                after()
                for kt in range(CT):
                    last = product(M[bank][:], w(QKV + kt * 3 * D + which * D + c * 128), two(mid_h, mid_l, kt), kt == 0, kt == CT - 1)
                last.then_inc(qkv_z.sem, 1)

            def denominators(k):
                if more_chunks(k):
                    pe.wait_ge(gate_copied.sem, gate_copied.nth(k + 1))
                pe.wait_ge(k_phi.sem, k_phi.nth(k, 1))
                for c in range(CT):
                    pe.wait_ge(qk_ready.sem, qk_ready.nth(k, c))
                    last = pe.matmul(M[1][0:HEADS, :], cst[:, C_HEAD + c * HEADS:C_HEAD + (c + 1) * HEADS], ac[:, 3 + c, :],
                                     start=c == 0, stop=c == CT - 1)
                last.then_inc(den_z.sem, 1)

            def turn_denominators(k):
                pe.wait_ge(den_copied.sem, den_copied.nth(k))
                pe.wait_ge(q_phi.sem, q_phi.nth(k, 1))
                apart(pe)
                for b in range(NB):
                    last = pe.transpose(M[0][:, b * HEADS:(b + 1) * HEADS], ac[0:HEADS, 2, b * 128:(b + 1) * 128],
                                        ident[0:HEADS, 0:HEADS])
                last.then_inc(den_turned.sem, 1)

            def turn_inverses(k):
                pe.wait_ge(den_wide.sem, den_wide.nth(k))
                wide = ac[:, 0:2, :].rearrange("p a (b n) -> p (a b) n", n=D)
                to_channels(wide, inv_turned)

            def attention_product(k):
                pe.wait_ge(o_lo.sem, o_lo.nth(k))
                for b in range(NB):
                    if b % 2 == 0:
                        pe.wait_ge(o_ready.sem, o_ready.nth(k, b // 2))
                    for kt in range(CT):
                        last = product(M[b // 2][:, (b % 2) * D:(b % 2 + 1) * D], two(mid_h, mid_l, kt, b * 128, 128),
                                       w(WOUT + kt * D, D), kt == 0, kt == CT - 1)
                    if b % 2:
                        last.then_inc(attn_out.sem, 1)

            def turn_x3(k, after):
                pe.wait_ge(ln_done[2].sem, ln_done[2].nth(k, NB - 1))
                after()
                to_channels(tok3, x3_turned)

            def ffn_first(r, j, tail=False):
                if j == 0:
                    if later(r):
                        pe.wait_ge(x3_lo.sem, x3_lo.nth(r - 1, CT - 1))
                p = 2 * (j % 2)
                if j < 2:
                    if not tail:
                        pe.wait_ge(hid_act.sem, hid_act.nth(r, NT - 1))
                        pe.wait_ge(combined.sem, combined.nth(r, E))
                pe.wait_ge(ff_hid.sem, ff_hid.nth(r, j - 2))
                for g, base in enumerate((W1, W3)):
                    for kt in range(CT):
                        last = product(R[p + g][:], w(base + kt * FF + j * 128), two(ffn_h, ffn_l, kt), kt == 0, kt == CT - 1)
                last.then_inc(ff_z.sem, 1)

            def ffn_second(r, j):
                pe.wait_ge(ff_lo.sem, ff_lo.nth(r, j))
                if j == 0:
                    if later(r):
                        pe.wait_ge(y4_ready.sem, y4_ready.nth(r - 1, 1))
                for b in range(NB):
                    last = product(R[4 + b // 2][:, (b % 2) * D:(b % 2 + 1) * D], two(sh, sl, j % 3, b * 128, 128),
                                   w(W2 + j * D, D), j == 0 and b % 2 == 0, j == FT - 1, shared=True)
                last.then_inc(ff_used.sem, 1)

            def experts(r):
                more = more_chunks(r)
                for t in range(NT + LAG):
                    if t < NT:
                        first(r, t)
                    if t == 2 and later(r):
                        def after():
                            if later(r):
                                pe.wait_ge(y3_ready.sem, y3_ready.nth(r - 1, 1))
                            pe.wait_ge(h_act.sem, h_act.nth(r))
                        turn_x3(r - 1, after)
                    if more and t == 8:
                        def after(g):
                            pe.wait_ge(h_act.sem, h_act.nth(r))
                            if later(r):
                                pe.wait_ge(x3_lo.sem, x3_lo.nth(r - 1, CT - 1))
                        gates(r + 1, 0, after)
                    if more and t == 10:
                        gates(r + 1, 1, None)
                    if t >= LAG:
                        second(r, t - LAG)

                def after():
                    if more:
                        pe.wait_ge(tanh_r.sem, tanh_r.nth(r + 1, 1))
                        pe.wait_ge(tanh_i.sem, tanh_i.nth(r + 1, 1))
                    else:
                        pe.wait_ge(h_act.sem, h_act.nth(r))
                        if later(r):
                            pe.wait_ge(x3_lo.sem, x3_lo.nth(r - 1, CT - 1))
                moe_product(r, after)

            def rest(r, ffn):
                more = more_chunks(r)

                def ff(j):
                    if ffn:
                        ffn_first(r, j)
                        if j:
                            ffn_second(r, j - 1)
                ff(0)
                if more:
                    turn_y(r + 1, lambda: pe.wait_ge(y2_ready.sem, y2_ready.nth(r, 1)))
                ff(1)

                def after():
                    pe.wait_ge(y2_ready.sem, y2_ready.nth(r, 1))
                    if more:
                        pe.wait_ge(ln_done[0].sem, ln_done[0].nth(r + 1, NB - 1))
                turn_x2(r, after)
                if more:
                    turn_x1(r + 1, lambda: pe.wait_ge(x2_lo.sem, x2_lo.nth(r, 1)))

                def after():
                    if more:
                        pe.wait_ge(x1_lo.sem, x1_lo.nth(r + 1, 1))
                    pe.wait_ge(x2_lo.sem, x2_lo.nth(r, 1))
                qkv(r, 0, 1, 0, after)
                ff(2)
                qkv(r, 1, 2, 0, after)
                if more:
                    logits(r + 1, lambda: pe.wait_ge(k_phi.sem, k_phi.nth(r)))
                qkv(r, 1, 0, 0, lambda: pe.wait_ge(kv_ready.sem, kv_ready.nth(r)))
                if more:
                    turn_logits(r + 1)
                ff(3)
                qkv(r, 1, 1, 1, lambda: pe.wait_ge(q_phi.sem, q_phi.nth(r)))

                def after():
                    pe.wait_ge(k_phi.sem, k_phi.nth(r))
                    if more:
                        pe.wait_ge(route.sem, route.nth(r + 1))
                qkv(r, 0, 2, 1, after)
                if more:
                    turn_gates(r + 1, lambda: pe.wait_ge(k_phi.sem, k_phi.nth(r, 1)))
                ff(4)
                qkv(r, 0, 0, 1, lambda: pe.wait_ge(kv_ready.sem, kv_ready.nth(r, 1)))
                ff(5)
                denominators(r)
                ff(6)
                turn_denominators(r)
                ff(7)
                pe.wait_ge(den_max.sem, den_max.nth(r))
                turn_inverses(r)
                if ffn:
                    ffn_second(r, FT - 1)
                attention_product(r)
                if more:
                    down(r + 1, lambda: pe.wait_ge(y3_ready.sem, y3_ready.nth(r, 1)))

            pe.wait_ge(small_loaded.sem, 16)
            pe.wait_ge(dense_lo.sem, dense_lo.nth(0))
            gates(0, 0, lambda g: None)
            gates(0, 1, None)

            def after():
                pe.wait_ge(tanh_r.sem, tanh_r.nth(0, 1))
                pe.wait_ge(tanh_i.sem, tanh_i.nth(0, 1))
            turn_y(0, after)
            turn_x1(0, lambda: pe.wait_ge(ln_done[0].sem, ln_done[0].nth(0, NB - 1)))
            pe.wait_ge(dense_lo.sem, dense_lo.nth(1))
            logits(0, lambda: None)
            down(0, lambda: None)
            turn_logits(0)
            turn_gates(0, lambda: pe.wait_ge(h_act.sem, h_act.nth(0)))
            idle_experts()
            pe.wait_ge(gate_copied.sem, gate_copied.nth(0))
            experts(0)
            pe.wait_ge(had_step.sem, had_step.nth(5))
            for q in range(4):
                pe.matmul(R[q][:], cst[:, C_HAD:C_HAD + 128], hid[:, q, :], start=True, stop=True).then_inc(had_z.sem, 1)
            pe.wait_ge(att_lo.sem, att_lo.nth(ATTN_PIECES - 1))
            rest(0, False)
            pe.sem_inc(ff_z.sem, FT)
            pe.sem_inc(ff_used.sem, FT)
            pe.wait_ge(ffn_w_lo.sem, ffn_w_lo.nth(FFN_PIECES - 1))
            pe.wait_ge(had_lo.sem, had_lo.nth(3))
            with pe.Fori(1, chunks - 1) as r:
                experts(r)
                rest(r, True)
            experts(chunks - 1)
            rest(chunks - 1, True)

            def after():
                pe.wait_ge(y3_ready.sem, y3_ready.nth(chunks - 1, 1))
            turn_x3(chunks - 1, after)
            for j in range(FT):
                ffn_first(chunks, j, tail=True)
                if j:
                    ffn_second(chunks, j - 1)
            ffn_second(chunks, FT - 1)

        @block.scalar
        def _(act):
            def gates(k, c):
                if c == 0:
                    if later(k):
                        act.wait_ge(y_ready.sem, y_ready.nth(k - 1))
                    if later(k - 1):
                        act.wait_ge(inv_turned.sem, inv_turned.nth(k - 2, 1))
                        act.wait_ge(o_lo.sem, o_lo.nth(k - 2))
                    if later(k):
                        act.wait_ge(g1_lo.sem, g1_lo.nth(k - 1))
                    if later(k):
                        act.wait_ge(h_lo.sem, h_lo.nth(k - 1))
                act.wait_ge(gate_z.sem, gate_z.nth(k, 2 * c))
                act.activation(ac[:, c, :], M[0][:], ACT.Tanh, bias=half_b[:, c:c + 1], scale=0.5).then_inc(tanh_r.sem, 1)
                act.wait_ge(gate_z.sem, gate_z.nth(k, 2 * c + 1))
                act.activation(ac[:, 2 + c, :], M[1][:], ACT.Tanh, bias=half_b[:, CT + c:CT + c + 1], scale=0.5).then_inc(tanh_i.sem, 1)

            def decays(k, c):
                act.wait_ge(tanh_r.sem, tanh_r.nth(k, c))
                act.activation(ac[:, 4 + c, :], ac[:, c, :], ACT.Exp, bias=c2[:, c:c + 1], scale=c2[:, c:c + 1]).then_inc(a_exp.sem, 1)
                act.wait_ge(a_exp.sem, a_exp.nth(k, c))
                act.activation(ac[:, c, :], ac[:, c, :], ACT.Tanh, bias=nc2[:, c:c + 1], scale=nc2[:, c:c + 1]).then_inc(a_tanh.sem, 1)
                if c:
                    act.wait_ge(w_ready.sem, w_ready.nth(k, c - 1))
                act.activation(ac[:, 6, :], ac[:, 4 + c, :], ACT.Square).then_inc(a_sq.sem, 1)

            def root(k):
                act.wait_ge(w_ready.sem, w_ready.nth(k, CT - 1))
                act.activation(ac[:, 0:2, :], ac[:, 0:2, :], ACT.Sqrt).then_inc(w_root.sem, 1)

            def x1_high(k):
                for c in range(CT):
                    act.wait_ge(x1_turned.sem, x1_turned.nth(k, c))
                    act.wait_ge(gate_z.sem, gate_z.nth(k, 3))
                    act.activation(chan_h[:, c, :], M[c][:], ACT.Copy).then_inc(x1_hi.sem, 1)

            def logit_copy(k):
                act.wait_ge(logit_z.sem, logit_z.nth(k))
                if later(k):
                    act.wait_ge(m_lo.sem, m_lo.nth(k - 1))
                act.activation(lg, M[0][0:E, :], ACT.Copy).then_inc(logit_copied.sem, 1)

            def route_e(k):
                act.wait_ge(route.sem, route.nth(k, 2))
                act.activation(rt[:, 2, :], rt[:, 1, :], ACT.Exp).then_inc(route_exp.sem, 1)

            def route_t(k):
                act.wait_ge(route.sem, route.nth(k, 16))
                act.activation(r4[:, 6, :], r4[:, 5, :], ACT.Tanh, scale=-0.5).then_inc(route_tanh.sem, 1)

            def gate_copy(k):
                act.wait_ge(gate_turned.sem, gate_turned.nth(k))
                if later(k):
                    act.wait_ge(m_lo.sem, m_lo.nth(k - 1))
                act.activation(gt, M[1][0:NB * E, 0:128], ACT.Copy).then_inc(gate_copied.sem, 1)

            def h_gelu(k):
                act.wait_ge(down_z.sem, down_z.nth(k))
                if later(k):
                    act.wait_ge(inv_turned.sem, inv_turned.nth(k - 1, 1))
                act.wait_ge(y_ready.sem, y_ready.nth(k))
                act.activation(ac[:, 0, :], M[1][:], ACT.Gelu, bias=vec[:, V_DOWN:V_DOWN + 1]).then_inc(h_act.sem, 1)

            def g1_gelu(k):
                act.wait_ge(x1_sum.sem, x1_sum.nth(k))
                act.activation(ac[:, 5:7, :], ac[:, 5:7, :], ACT.Gelu).then_inc(g1_act.sem, 1)

            def hidden(k, t):
                act.wait_ge(hid_z.sem, hid_z.nth(k, t))
                if t < 3:
                    if later(k):
                        act.wait_ge(ff_lo.sem, ff_lo.nth(k - 1, FT - 1))
                else:
                    act.wait_ge(hid_lo.sem, hid_lo.nth(k, t - 3))
                b = vec[:, V_S1:V_S1 + 1] if t == 0 else vec[:, V_E1 + t - 1:V_E1 + t]
                act.activation(hid[:, t % 3, :], R[t % 3][:], ACT.Gelu, bias=b).then_inc(hid_act.sem, 1)

            def x2_high(k):
                for c in range(CT):
                    act.wait_ge(x2_turned.sem, x2_turned.nth(k, c))
                    act.activation(mid_h[:, c, :], M[c][:], ACT.Copy).then_inc(x2_hi.sem, 1)

            def key_exp(k, c):
                act.wait_ge(qkv_z.sem, qkv_z.nth(k, 3 * c))
                if c == 0:
                    if more_chunks(k):
                        act.wait_ge(y_ready.sem, y_ready.nth(k + 1))
                else:
                    act.wait_ge(scanned.sem, scanned.nth(k, 4 * c - 1))
                act.activation(ac[:, 0, :], M[c][:], ACT.Exp).then_inc(k_exp.sem, 1)

            def query_exp(k, c):
                act.wait_ge(qkv_z.sem, qkv_z.nth(k, 3 * c + 2))
                if c:
                    act.wait_ge(num_ready.sem, num_ready.nth(k, c - 1))
                act.activation(ac[:, 2, :], M[1 - c][:], ACT.Exp).then_inc(q_exp.sem, 1)

            def den_copy(k):
                act.wait_ge(den_z.sem, den_z.nth(k))
                act.wait_ge(num_ready.sem, num_ready.nth(k, CT - 1))
                act.activation(ac[0:HEADS, 2, :], M[1][0:HEADS, :], ACT.Copy).then_inc(den_copied.sem, 1)

            def den_expand(k):
                act.wait_ge(den_inv.sem, den_inv.nth(k))
                act.wait_ge(scanned.sem, scanned.nth(k, 4 * CT - 1))
                act.activation(ac[:, 0:2, :].rearrange("p a (n d) -> p (a n) d", d=HEAD),
                               rden[:].unsqueeze(2).broadcast_to([128, NB * HEADS, HEAD]), ACT.Copy).then_inc(den_wide.sem, 1)

            def x3_high(k):
                for c in range(CT):
                    act.wait_ge(x3_turned.sem, x3_turned.nth(k, c))
                    act.wait_ge(ff_z.sem, ff_z.nth(k, FT - 1))
                    act.activation(ffn_h[:, c, :], M[c][:], ACT.Copy).then_inc(x3_hi.sem, 1)

            def ffn(r, j, tail=False):
                act.wait_ge(ff_z.sem, ff_z.nth(r, j))
                if j < 3 and not tail:
                    act.wait_ge(hid_lo.sem, hid_lo.nth(r, NT - 1))
                act.wait_ge(ff_lo.sem, ff_lo.nth(r, j - 3))
                act.activation(hid[:, j % 3, :], R[2 * (j % 2)][:], ACT.Tanh, scale=0.5).then_inc(ff_tanh.sem, 1)

            def experts(r, attn_weights=False):
                more = more_chunks(r)
                for t in range(NT):
                    hidden(r, t)
                    if t == 1:
                        g1_gelu(r)
                    if t == 3 and later(r):
                        x3_high(r - 1)
                    if attn_weights and t >= 12 and t % 2 == 0 and (t - 12) // 2 < ATTN_PIECES:
                        attn_split((t - 12) // 2)
                    if more:
                        if t == 8:
                            gates(r + 1, 0)
                        if t == 10:
                            gates(r + 1, 1)
                        if t == 11:
                            decays(r + 1, 0)
                        if t == 13:
                            decays(r + 1, 1)
                        if t == 15:
                            root(r + 1)

            def rest(r, has_ffn):
                more = more_chunks(r)

                def ff(j):
                    if has_ffn:
                        ffn(r, j)
                ff(0)
                ff(1)
                x2_high(r)
                if more:
                    x1_high(r + 1)
                key_exp(r, 0)
                ff(2)
                if more:
                    logit_copy(r + 1)
                query_exp(r, 0)
                if more:
                    route_e(r + 1)
                ff(3)
                key_exp(r, 1)
                if more:
                    route_t(r + 1)
                    gate_copy(r + 1)
                ff(4)
                query_exp(r, 1)
                ff(5)
                den_copy(r)
                ff(6)
                ff(7)
                den_expand(r)
                if more:
                    h_gelu(r + 1)

            flat = hid[:].rearrange("p a n -> p (a n)")
            raw = tok3[:].rearrange("p b n -> p (b n)")

            def attn_split(n):
                m = EXPERT_PIECES + n
                c = QKV + n * PIECE
                act.wait_ge(piece_loaded[m % 2].sem, 16 * (m // 2 + 1))
                act.activation(wh[:, c:c + PIECE], raw[:, (m % 2) * PIECE:(m % 2 + 1) * PIECE], ACT.Copy).then_inc(att_hi.sem, 1)

            act.dma_start(vec[:], vectors).then_inc(vec_loaded.sem, 16)
            act.dma_start(cst[:], consts).then_inc(small_loaded.sem, 16)
            act.dma_start(ac[:, 0:2, :].rearrange("p a n -> p (a n)")[:, 0:rows.shape[0]], rows.partition_broadcast(128)).then_inc(rows_loaded.sem, 16)
            act.wait_ge(vec_loaded.sem, 16)
            act.activation(ser[:, 0, :], vec[:, V_LAM:V_LAM + CT], ACT.Abs).then_inc(setup_act.sem, 1)
            act.wait_ge(setup_act.sem, setup_act.nth(0))
            act.activation(ser[:, 1, :], ser[:, 0, :], ACT.Exp, scale=-1.0).then_inc(setup_act.sem, 1)
            act.activation(decay[:, :], vec[:, V_DEC:V_DEC + CT], ACT.Tanh, scale=0.5).then_inc(setup_act.sem, 1)
            act.wait_ge(w0_loaded.sem, 16)
            act.activation(wh[:, 0:DOWN], flat[:, 0:DOWN], ACT.Copy).then_inc(dense_hi.sem, 1)
            act.wait_ge(w1_loaded.sem, 16)
            act.activation(wh[:, DOWN:EXPERTS], flat[:, DOWN:EXPERTS], ACT.Copy).then_inc(dense_hi.sem, 1)
            act.wait_ge(setup_dve.sem, setup_dve.nth(SET_ROWS))
            act.wait_ge(setup_dve.sem, setup_dve.nth(SET_C2))
            gates(0, 0)
            gates(0, 1)
            decays(0, 0)
            decays(0, 1)
            root(0)
            x1_high(0)
            logit_copy(0)
            route_e(0)
            route_t(0)
            act.activation(b1g[:, :], vec[:, V_E1:V_E1 + NT - 1], ACT.Gelu).then_inc(setup_act.sem, 1)
            h_gelu(0)
            gate_copy(0)
            experts(0, attn_weights=True)
            for q in range(4):
                act.wait_ge(had_z.sem, had_z.nth(q))
                act.activation(wh[:, W2 + q * PIECE:W2 + (q + 1) * PIECE], R[q][:], ACT.Copy).then_inc(had_hi.sem, 1)
            rest(0, False)
            act.sem_inc(ff_tanh.sem, FT)
            with act.Fori(1, chunks - 1) as r:
                experts(r)
                rest(r, True)
            experts(chunks - 1)
            rest(chunks - 1, True)
            x3_high(chunks - 1)
            for j in range(FT):
                ffn(chunks, j, tail=True)

        @block.vector
        def _(dve):
            def split_x(k):
                dve.wait_ge(x_loaded.sem, x_loaded.nth(k))
                if later(k):
                    dve.wait_ge(down_z.sem, down_z.nth(k - 1))
                if later(k):
                    dve.wait_ge(x1_sum.sem, x1_sum.nth(k - 1))
                dve.tensor_copy(chan_h[:], xy[:]).then_inc(x_hi.sem, 1)
                dve.wait_ge(x_hi.sem, x_hi.nth(k))
                dve.tensor_tensor(chan_l[:], xy[:], chan_h[:].bitcast(f32), ALU.subtract).then_inc(x_lo.sem, 1)

            def roots(k, c):
                dve.wait_ge(a_sq.sem, a_sq.nth(k, c))
                dve.wait_ge(a_tanh.sem, a_tanh.nth(k, c))
                dve.scalar_tensor_tensor(out=ac[:, c, :], in0=ac[:, 6, :], scalar=1.0, in1=ac[:, c, :], op0=ALU.add, op1=ALU.mult)\
                    .then_inc(w_ready.sem, 1)

            def recurrence(k):
                dve.wait_ge(a_sq.sem, a_sq.nth(k, CT - 1))
                dve.memset(ac[:, 4:6, :].rearrange("p a (s t) -> p (a s) t", t=SEQ)[:, :, 0:1], 0.0).then_inc(a_cut.sem, 1)
                dve.wait_ge(tanh_i.sem, tanh_i.nth(k, CT - 1))
                dve.scalar_tensor_tensor(out=ac[:, 2:4, :], in0=ac[:, 2:4, :], scalar=1.0, in1=xy[:], op0=ALU.add, op1=ALU.mult)\
                    .then_inc(ix_ready.sem, 1)
                dve.wait_ge(w_root.sem, w_root.nth(k))
                dve.wait_ge(ix_ready.sem, ix_ready.nth(k))
                dve.scalar_tensor_tensor(out=ac[:, 2:4, :], in0=ac[:, 0:2, :], scalar=0.5, in1=ac[:, 2:4, :], op0=ALU.mult, op1=ALU.mult)\
                    .then_inc(u_ready.sem, 1)
                dve.wait_ge(u_ready.sem, u_ready.nth(k))
                dve.wait_ge(a_cut.sem, a_cut.nth(k))
                dve.tensor_tensor_scan(ac[:, 0:2, :].rearrange("p a n -> p (a n)"), ac[:, 4:6, :].rearrange("p a n -> p (a n)"),
                                       ac[:, 2:4, :].rearrange("p a n -> p (a n)"), 0.0, ALU.mult, ALU.add).then_inc(h_ready.sem, 1)
                dve.wait_ge(h_ready.sem, h_ready.nth(k))
                dve.tensor_tensor(xy[:], ac[:, 0:2, :], xy[:], ALU.add).then_inc(y_ready.sem, 1)

            def norm(i, k, src, dst, ready):
                for b in range(NB):
                    ready(b)
                    dve.bn_stats(st[i][:, b, :], src(b)).then_inc(ln_stats[i].sem, 1)
                dve.wait_ge(ln_stats[i].sem, ln_stats[i].nth(k, NB - 1))
                apart(dve)
                for b in range(NB):
                    dve.bn_aggr(mv[i][:, b, :], st[i][:, b, :]).then_inc(ln_mv[i].sem, 1)

            def normed(i, k, src, dst):
                dve.wait_ge(ln_rstd[i].sem, ln_rstd[i].nth(k))
                for b in range(NB):
                    dve.tensor_scalar(dst(b), src(b), mv[i][:, b, 0:1], rs[i][:, 1, b:b + 1], ALU.subtract, ALU.mult)\
                        .then_inc(ln_done[i].sem, 1)

            def in_m(b):
                return M[b // 2][:, (b % 2) * D:(b % 2 + 1) * D]

            gate_tok = gate[:].rearrange("p a (b n) -> p (a b) n", n=D)

            def x1_stats(k):
                norm(0, k, in_m, None, lambda b: dve.wait_ge(y_turned.sem, y_turned.nth(k, b // 2)))

            def x1_norm(k):
                if later(k):
                    dve.wait_ge(combined.sem, combined.nth(k - 1, E))
                normed(0, k, in_m, lambda b: gate_tok[:, b, :])

            def x1_low(k):
                for c in range(CT):
                    dve.wait_ge(x1_hi.sem, x1_hi.nth(k, c))
                    dve.tensor_tensor(chan_l[:, c, :], M[c][:], chan_h[:, c, :].bitcast(f32), ALU.subtract).then_inc(x1_lo.sem, 1)

            def grid(ap):
                return ap.rearrange("p (b e) -> p b e", e=E)

            def over(ap):
                return ap.unsqueeze(2).broadcast_to([128, NB, E])

            def routing(k, part):
                at = [0 if part == 0 else 3 if part == 1 else 17]

                def step(ins):
                    ins.then_inc(route.sem, 1)
                    dve.wait_ge(route.sem, route.nth(k, at[0]))
                    at[0] += 1

                shifted, expd, t0, k1, l2, k2, t1, first = (grid(rt[:, i, :]) for i in range(1, 9))
                rev = grid(cst[:, C_REV:C_REV + NB * E])
                m1, i1, m2, i2, z, d, th, g1, g2, rz, e2 = (r4[:, i, :] for i in (0, 1, 2, 3, 4, 5, 6, 7, 8, 9, 10))
                if part == 0:
                    dve.wait_ge(logit_turned.sem, logit_turned.nth(k))
                    if later(k):
                        dve.wait_ge(gate_turned.sem, gate_turned.nth(k - 1))
                    step(dve.tensor_tensor(rt[:, 0, :], M[0][:, 0:NB * E], bias_r[:, :], ALU.add))
                    step(dve.reduce_max(m1, grid(rt[:, 0, :]), AX.X))
                    step(dve.tensor_tensor(shifted, grid(rt[:, 0, :]), over(m1), ALU.subtract))
                elif part == 1:
                    step(dve.scalar_tensor_tensor(out=rt[:, 3, :], in0=rt[:, 1, :], scalar=0.0, in1=cst[:, C_REV:C_REV + NB * E], op0=ALU.is_ge, op1=ALU.mult))
                    step(dve.reduce_max(i1, t0, AX.X))
                    step(dve.tensor_tensor(k1, rev, over(i1), ALU.is_equal))
                    step(dve.scalar_tensor_tensor(out=rt[:, 5, :], in0=rt[:, 4, :], scalar=-3e38, in1=rt[:, 1, :], op0=ALU.mult, op1=ALU.add))
                    step(dve.reduce_max(m2, l2, AX.X))
                    step(dve.tensor_tensor(t0, l2, over(m2), ALU.is_equal))
                    step(dve.tensor_tensor(t0, t0, rev, ALU.mult))
                    step(dve.reduce_max(i2, t0, AX.X))
                    step(dve.tensor_tensor(k2, rev, over(i2), ALU.is_equal))
                    dve.wait_ge(route_exp.sem, route_exp.nth(k))
                    step(dve.reduce_sum(z, expd, AX.X))
                    step(dve.reciprocal(rz, z))
                    step(dve.tensor_tensor(t1, expd, k2, ALU.mult))
                    step(dve.reduce_sum(e2, t1, AX.X))
                    step(dve.scalar_tensor_tensor(out=d, in0=e2, scalar=-1.0, in1=rz, op0=ALU.add, op1=ALU.mult))
                else:
                    dve.wait_ge(route_tanh.sem, route_tanh.nth(k))
                    step(dve.tensor_scalar(g1, th, 0.5, 0.5, ALU.mult, ALU.add))
                    step(dve.tensor_scalar(g2, th, -0.5, 0.5, ALU.mult, ALU.add))
                    step(dve.tensor_tensor(k1, k1, over(g1), ALU.mult))
                    step(dve.tensor_tensor(k2, k2, over(g2), ALU.mult))
                    step(dve.tensor_tensor(rt[:, 8, :].rearrange("p (e b) -> p b e", b=NB), k1, k2, ALU.add))

            def split_h(k):
                dve.wait_ge(h_act.sem, h_act.nth(k))
                if later(k):
                    dve.wait_ge(moe_out.sem, moe_out.nth(k - 1, 1))
                dve.tensor_copy(sh[:, 3, :], ac[:, 0, :]).then_inc(h_hi.sem, 1)
                dve.wait_ge(h_hi.sem, h_hi.nth(k))
                dve.tensor_tensor(sl[:, 3, :], ac[:, 0, :], sh[:, 3, :].bitcast(f32), ALU.subtract).then_inc(h_lo.sem, 1)

            def split_g1(k):
                dve.wait_ge(g1_act.sem, g1_act.nth(k))
                if later(k):
                    dve.wait_ge(attn_out.sem, attn_out.nth(k - 1, 1))
                dve.tensor_copy(mid_h[:], ac[:, 5:7, :]).then_inc(g1_hi.sem, 1)
                dve.wait_ge(g1_hi.sem, g1_hi.nth(k))
                dve.tensor_tensor(mid_l[:], ac[:, 5:7, :], mid_h[:].bitcast(f32), ALU.subtract).then_inc(g1_lo.sem, 1)

            def hidden_high(k, t):
                dve.wait_ge(hid_act.sem, hid_act.nth(k, t))
                if t < 3:
                    if later(k):
                        dve.wait_ge(ff_used.sem, ff_used.nth(k - 1, FT - 1))
                else:
                    dve.wait_ge(hid_used.sem, hid_used.nth(k, t - 3))
                dve.tensor_copy(sh[:, t % 3, :], hid[:, t % 3, :]).then_inc(hid_hi.sem, 1)

            def combine(k, o):
                dve.wait_ge(hid_used.sem, hid_used.nth(k, last_tile(o)))
                if o == 0:
                    if later(k):
                        dve.wait_ge(out_stored.sem, out_stored.nth(k - 1))
                    dve.wait_ge(gates_stored.sem, gates_stored.nth(k))
                    dve.tensor_scalar(hid[:, 3, :], R[3][:], 0.1, s2b[:, 0:1], ALU.mult, ALU.add).then_inc(combined.sem, 1)
                    return
                e = o - 1
                dve.wait_ge(row_loaded[e % 2].sem, row_loaded[e % 2].nth(k, e // 2))
                if o > 1:
                    dve.wait_ge(summed.sem, summed.nth(k, e - 1))
                else:
                    dve.wait_ge(combined.sem, combined.nth(k))
                dve.scalar_tensor_tensor(out=hid[:, 4, :], in0=R[3 + o % 3][:], scalar=idle[:, e:e + 1], in1=gate[:, e % 2, :],
                                         op0=ALU.subtract, op1=ALU.mult).then_inc(combined.sem, 1)
                dve.wait_ge(combined.sem, combined.nth(k, o))
                dve.tensor_tensor(hid[:, 3, :], hid[:, 3, :], hid[:, 4, :], ALU.add).then_inc(summed.sem, 1)

            def mixture(k):
                dve.wait_ge(summed.sem, summed.nth(k, E - 1))
                dve.wait_ge(hid_z.sem, hid_z.nth(k, NT - 1))
                dve.tensor_scalar(sh[:, 3, :], hid[:, 3, :], idle_sum[:, 0:1], None, ALU.add).then_inc(m_hi.sem, 1)
                dve.wait_ge(m_hi.sem, m_hi.nth(k))
                dve.scalar_tensor_tensor(out=sl[:, 3, :], in0=hid[:, 3, :], scalar=idle_sum[:, 0:1], in1=sh[:, 3, :].bitcast(f32),
                                         op0=ALU.add, op1=ALU.subtract).then_inc(m_lo.sem, 1)

            def flat2(t, i):
                return t[:, 2 * i:2 * i + 2, :].rearrange("p b n -> p (b n)")

            def x2_stats(k):
                for i in range(2):
                    dve.wait_ge(moe_out.sem, moe_out.nth(k, i))
                    dve.wait_ge(resid1.sem, resid1.nth(k))
                    dve.tensor_tensor(flat2(tok, i), M[i][:], flat2(tok, i), ALU.add).then_inc(y2_ready.sem, 1)
                norm(1, k, lambda b: tok[:, b, :], None, lambda b: dve.wait_ge(y2_ready.sem, y2_ready.nth(k, b // 2)))

            def x2_norm(k):
                normed(1, k, lambda b: tok[:, b, :], lambda b: tok[:, b, :])

            def x2_low(k):
                for c in range(CT):
                    dve.wait_ge(x2_hi.sem, x2_hi.nth(k, c))
                    dve.tensor_tensor(mid_l[:, c, :], M[c][:], mid_h[:, c, :].bitcast(f32), ALU.subtract).then_inc(x2_lo.sem, 1)

            def elu1(k, c, exp, low, phi, slot, bank):
                dve.wait_ge(exp.sem, exp.nth(k, c))
                dve.tensor_scalar(ac[:, slot, :], ac[:, slot, :], 1.0, None, ALU.min).then_inc(low.sem, 1)
                dve.wait_ge(low.sem, low.nth(k, c))
                dve.scalar_tensor_tensor(out=ac[:, slot, :], in0=bank[:], scalar=0.0, in1=ac[:, slot, :], op0=ALU.max, op1=ALU.add)\
                    .then_inc(phi.sem, 1)

            def keys(k, c):
                elu1(k, c, k_exp, k_min, k_phi, 0, M[c])
                dve.wait_ge(k_phi.sem, k_phi.nth(k, c))
                dve.wait_ge(qkv_z.sem, qkv_z.nth(k, 3 * c + 1))
                dve.tensor_tensor(ac[:, 1, :], M[1 - c][:], ac[:, 0, :], ALU.mult).then_inc(kv_ready.sem, 1)
                dve.wait_ge(kv_ready.sem, kv_ready.nth(k, c))
                for what, dst in ((0, 3 + c), (1, 5 + c)):
                    for s in range(CHUNK // SEQ):
                        at = slice(s * SEQ, (s + 1) * SEQ)
                        dve.tensor_tensor_scan(ac[:, dst, at], decay[:, c:c + 1].broadcast_to([128, SEQ]), ac[:, what, at], 0.0,
                                               ALU.mult, ALU.add).then_inc(scanned.sem, 1)

            def queries(k, c):
                elu1(k, c, q_exp, q_min, q_phi, 2, M[1 - c])

            def inverses(k):
                dve.wait_ge(den_turned.sem, den_turned.nth(k))
                dve.tensor_scalar(rden[:, :], M[0][:, 0:NB * HEADS], 1e-6, None, ALU.max).then_inc(den_max.sem, 1)
                dve.wait_ge(den_max.sem, den_max.nth(k))
                dve.reciprocal(rden[:, :], rden[:, :]).then_inc(den_inv.sem, 1)

            def attention(k):
                for c in range(CT):
                    dve.wait_ge(inv_turned.sem, inv_turned.nth(k, c))
                    dve.wait_ge(num_ready.sem, num_ready.nth(k, c))
                    dve.tensor_tensor(ac[:, 5 + c, :], M[c][:], ac[:, 5 + c, :], ALU.mult).then_inc(o_ready.sem, 1)
                dve.wait_ge(o_ready.sem, o_ready.nth(k, CT - 1))
                dve.wait_ge(qkv_z.sem, qkv_z.nth(k, 5))
                dve.tensor_copy(mid_h[:], ac[:, 5:7, :]).then_inc(o_hi.sem, 1)
                dve.wait_ge(o_hi.sem, o_hi.nth(k))
                dve.tensor_tensor(mid_l[:], ac[:, 5:7, :], mid_h[:].bitcast(f32), ALU.subtract).then_inc(o_lo.sem, 1)

            def x3_stats(k):
                if isinstance(k, int) and k == 0:
                    dve.wait_ge(ffn_w_lo.sem, ffn_w_lo.nth(FFN_PIECES - 1))
                for i in range(2):
                    dve.wait_ge(attn_out.sem, attn_out.nth(k, i))
                    dve.wait_ge(y4_ready.sem, y4_ready.nth(k, 1))
                    dve.tensor_tensor(flat2(tok3, i), M[i][:], flat2(tok, i), ALU.add).then_inc(y3_ready.sem, 1)
                norm(2, k, lambda b: tok3[:, b, :], None, lambda b: dve.wait_ge(y3_ready.sem, y3_ready.nth(k, b // 2)))

            def x3_norm(k):
                normed(2, k, lambda b: tok3[:, b, :], lambda b: tok3[:, b, :])

            def x3_low(k):
                for c in range(CT):
                    dve.wait_ge(x3_hi.sem, x3_hi.nth(k, c))
                    dve.tensor_tensor(ffn_l[:, c, :], M[c][:], ffn_h[:, c, :].bitcast(f32), ALU.subtract).then_inc(x3_lo.sem, 1)

            def ffn(r, j, tail=False):
                dve.wait_ge(ff_tanh.sem, ff_tanh.nth(r, j))
                p = 2 * (j % 2)
                h = hid[:, j % 3, :]
                dve.scalar_tensor_tensor(out=h, in0=h, scalar=1.0, in1=R[p][:], op0=ALU.add, op1=ALU.mult).then_inc(ff_silu.sem, 1)
                dve.wait_ge(ff_silu.sem, ff_silu.nth(r, j))
                dve.tensor_tensor(h, R[p + 1][:], h, ALU.mult).then_inc(ff_hid.sem, 1)
                dve.wait_ge(ff_hid.sem, ff_hid.nth(r, j))
                if j < 3 and not tail:
                    dve.wait_ge(hid_used.sem, hid_used.nth(r, NT - 1))
                dve.wait_ge(ff_used.sem, ff_used.nth(r, j - 3))
                dve.tensor_copy(sh[:, j % 3, :], h).then_inc(ff_hi.sem, 1)

            y4 = hid[:, 3:5, :].rearrange("p a (b n) -> p (a b) n", n=D)

            def out_stats(r, tail=False):
                for i in range(2):
                    dve.wait_ge(ff_used.sem, ff_used.nth(r, FT - 1))
                    if tail:
                        if later(r):
                            dve.wait_ge(out_stored.sem, out_stored.nth(r - 1))
                    else:
                        dve.wait_ge(m_lo.sem, m_lo.nth(r))
                        if more_chunks(r):
                            dve.wait_ge(logit_turned.sem, logit_turned.nth(r + 1))
                            dve.wait_ge(gates_stored.sem, gates_stored.nth(r + 1))
                    dve.tensor_tensor(hid[:, 3 + i, :], R[4 + i][:], flat2(tok3, i), ALU.add).then_inc(y4_ready.sem, 1)
                norm(3, r - 1, lambda b: y4[:, b, :], None, lambda b: dve.wait_ge(y4_ready.sem, y4_ready.nth(r, b // 2)))

            def out_norm(r):
                normed(3, r - 1, lambda b: y4[:, b, :], lambda b: y4[:, b, :])

            raw = tok3[:].rearrange("p b n -> p (b n)")
            flat = hid[:].rearrange("p a n -> p (a n)")

            def attn_split(n):
                m = EXPERT_PIECES + n
                c = QKV + n * PIECE
                dve.wait_ge(att_hi.sem, att_hi.nth(n))
                dve.tensor_tensor(wl[:, c:c + PIECE], raw[:, (m % 2) * PIECE:(m % 2 + 1) * PIECE], wh[:, c:c + PIECE].bitcast(f32),
                                  ALU.subtract).then_inc(att_lo.sem, 1)

            def experts(r, attn_weights=False):
                more = more_chunks(r)
                done = 0
                for t in range(NT + LAG):
                    if t < NT:
                        hidden_high(r, t)
                    if t == 1:
                        split_g1(r)
                    if t == 4 and later(r):
                        x3_low(r - 1)
                    if attn_weights and t >= 12 and t % 2 == 0 and (t - 12) // 2 < ATTN_PIECES:
                        attn_split((t - 12) // 2)
                    if t - LAG >= 1 and done <= E and last_tile(done) <= t - LAG - 1:
                        combine(r, done)
                        done += 1
                    if more:
                        if t == 6:
                            split_x(r + 1)
                        if t == 12:
                            roots(r + 1, 0)
                        if t == 14:
                            roots(r + 1, 1)
                        if t == 17:
                            recurrence(r + 1)
                while done <= E:
                    combine(r, done)
                    done += 1
                mixture(r)

            def rest(r, has_ffn):
                more = more_chunks(r)

                def ff(j):
                    if has_ffn:
                        ffn(r, j)
                x2_stats(r)
                if more:
                    x1_stats(r + 1)
                ff(0)
                x2_norm(r)
                if more:
                    x1_norm(r + 1)
                ff(1)
                x2_low(r)
                if more:
                    x1_low(r + 1)
                keys(r, 0)
                ff(2)
                if more:
                    routing(r + 1, 0)
                queries(r, 0)
                if more:
                    routing(r + 1, 1)
                ff(3)
                keys(r, 1)
                if more:
                    routing(r + 1, 2)
                ff(4)
                queries(r, 1)
                ff(5)
                ff(6)
                inverses(r)
                ff(7)
                attention(r)
                if has_ffn:
                    out_stats(r)
                else:
                    dve.sem_inc(y4_ready.sem, 2)
                x3_stats(r)
                if has_ffn:
                    out_norm(r)
                if more:
                    split_h(r + 1)
                x3_norm(r)

            n = [0]

            def link(ins):
                ins.then_inc(setup_dve.sem, 1)
                dve.wait_ge(setup_dve.sem, setup_dve.nth(n[0]))
                n[0] += 1
                return n[0] - 1

            link(dve.memset(neg_half[:, :], -0.5))
            dve.wait_ge(setup_act.sem, setup_act.nth(1))
            e_, ratio, sq, acc = ser[:, 1, :], ser[:, 2, :], ser[:, 3, :], ser[:, 4, :]
            link(dve.tensor_scalar(ratio, e_, 2.0, None, ALU.add))
            link(dve.reciprocal(ratio, ratio))
            link(dve.tensor_tensor(ratio, ratio, e_, ALU.mult))
            link(dve.tensor_tensor(sq, ratio, ratio, ALU.mult))
            link(dve.tensor_scalar(acc, sq, 1.0 / 17, None, ALU.mult))
            for d in (15, 13, 11, 9, 7, 5, 3):
                link(dve.scalar_tensor_tensor(out=acc, in0=acc, scalar=1.0 / d, in1=sq, op0=ALU.add, op1=ALU.mult))
            link(dve.scalar_tensor_tensor(out=acc, in0=acc, scalar=1.0, in1=ratio, op0=ALU.add, op1=ALU.mult))
            link(dve.tensor_scalar(sq, vec[:, V_LAM:V_LAM + CT], -1.0, 0.0, ALU.mult, ALU.max))
            link(dve.scalar_tensor_tensor(out=sq, in0=acc, scalar=2.0, in1=sq, op0=ALU.mult, op1=ALU.add))
            link(dve.tensor_scalar(c2[:, :], sq, -4.0, None, ALU.mult))
            link(dve.tensor_scalar(nc2[:, :], sq, 4.0, None, ALU.mult))
            link(dve.tensor_scalar(half_b[:, :], vec[:, V_BA:V_BA + 2 * CT], 0.5, None, ALU.mult))
            assert link(dve.tensor_scalar(s2b[:, :], vec[:, V_S2:V_S2 + 1], 0.1, None, ALU.mult)) == SET_C2
            dve.wait_ge(setup_act.sem, setup_act.nth(2))
            link(dve.tensor_scalar(decay[:, :], decay[:, :], 0.5, 0.5, ALU.mult, ALU.add))
            dve.wait_ge(rows_loaded.sem, 16)
            dve.wait_ge(small_loaded.sem, 16)
            rw = ac[:, 0:2, :].rearrange("p a n -> p (a n)")
            link(dve.tensor_tensor(bias_uc[:, :], rw[:, 0:D], rw[:, D:2 * D], ALU.add))
            assert link(dve.tensor_tensor(bias_r[:, :], rw[:, 2 * D:2 * D + NB * E], cst[:, C_COST:C_COST + NB * E], ALU.subtract)) == SET_ROWS
            split_x(0)
            for i, (a, b) in enumerate(((0, DOWN), (DOWN, EXPERTS))):
                dve.wait_ge(dense_hi.sem, dense_hi.nth(i))
                dve.tensor_tensor(wl[:, a:b], flat[:, a:b], wh[:, a:b].bitcast(f32), ALU.subtract).then_inc(dense_lo.sem, 1)
            roots(0, 0)
            roots(0, 1)
            recurrence(0)
            x1_stats(0)
            x1_norm(0)
            x1_low(0)
            routing(0, 0)
            routing(0, 1)
            routing(0, 2)
            dve.wait_ge(setup_act.sem, setup_act.nth(3))
            link(dve.tensor_copy(b1s[:, :, 0], b1g[:, :]))
            assert link(dve.tensor_tensor(b1s[:, :, 1], b1g[:, :], b1s[:, :, 0].bitcast(f32), ALU.subtract)) == IDLE_SPLIT
            split_h(0)
            dve.wait_ge(idle_z.sem, idle_z.nth(0))
            assert link(dve.tensor_copy(idle2[:, :], R[3][:, 0:2 * E])) == IDLE_COPIED
            parts = idle2[:, :].rearrange("p (e two) -> p e two", two=2)
            link(dve.tensor_tensor(idle[:, :], parts[:, :, 0], parts[:, :, 1], ALU.add))
            link(dve.reduce_sum(idle_sum[:, 0:1], idle[:, :], AX.X))
            link(dve.reduce_sum(idle_sum[:, 1:2], vec[:, V_E2:V_E2 + E], AX.X))
            link(dve.tensor_tensor(idle_sum[:, 0:1], idle_sum[:, 0:1], idle_sum[:, 1:2], ALU.add))
            experts(0, attn_weights=True)
            dve.wait_ge(w2_loaded.sem, 16)
            n_had = 0
            for s in (1, 2, 4):
                v = hid[:, 0:4, :].rearrange("p a (c n) -> p (a c) n", n=D).rearrange("p (g two s) n -> p g two (s n)", two=2, s=s)
                a, b = v[:, :, 0, :], v[:, :, 1, :]
                dve.tensor_tensor(b, a, b, ALU.subtract).then_inc(had_step.sem, 1)
                dve.wait_ge(had_step.sem, had_step.nth(n_had))
                dve.scalar_tensor_tensor(out=a, in0=a, scalar=2.0, in1=b, op0=ALU.mult, op1=ALU.subtract).then_inc(had_step.sem, 1)
                dve.wait_ge(had_step.sem, had_step.nth(n_had + 1))
                n_had += 2
            for q in range(4):
                dve.wait_ge(had_hi.sem, had_hi.nth(q))
                c = W2 + q * PIECE
                dve.tensor_tensor(wl[:, c:c + PIECE], R[q][:], wh[:, c:c + PIECE].bitcast(f32), ALU.subtract).then_inc(had_lo.sem, 1)
            rest(0, False)
            for sig in (ff_silu, ff_hid, ff_hi):
                dve.sem_inc(sig.sem, FT)
            with dve.Fori(1, chunks - 1) as r:
                experts(r)
                rest(r, True)
            experts(chunks - 1)
            rest(chunks - 1, True)
            x3_low(chunks - 1)
            for j in range(FT):
                ffn(chunks, j, tail=True)
            out_stats(chunks, tail=True)
            out_norm(chunks)

        @block.gpsimd
        def _(pool):
            def rstd(i, k):
                pool.wait_ge(ln_mv[i].sem, ln_mv[i].nth(k, NB - 1))
                if later(k):
                    pool.wait_ge(ln_done[i].sem, ln_done[i].nth(k - 1, NB - 1))
                apart(pool)
                pool.tensor_scalar(rs[i][:, 0, :], mv[i][:, :, 1], EPS, None, ALU.add).then_inc(ln_var[i].sem, 1)
                pool.wait_ge(ln_var[i].sem, ln_var[i].nth(k))
                pool.tensor_tensor(rs[i][:, 1, :], rs[i][:, 0, :], neg_half[:, :], ALU.pow).then_inc(ln_rstd[i].sem, 1)

            gate_tok = gate[:].rearrange("p a (b n) -> p (a b) n", n=D)

            def residual1(k):
                pool.wait_ge(ln_done[0].sem, ln_done[0].nth(k, NB - 1))
                if later(k):
                    pool.wait_ge(y3_ready.sem, y3_ready.nth(k - 1, 1))
                pool.tensor_tensor(tok[:], gate_tok, bias_uc[:].unsqueeze(1).broadcast_to([128, NB, D]), ALU.add).then_inc(resid1.sem, 1)

            def x1_whole(k):
                pool.wait_ge(x1_lo.sem, x1_lo.nth(k, CT - 1))
                if later(k):
                    pool.wait_ge(o_lo.sem, o_lo.nth(k - 1))
                pool.wait_ge(y_ready.sem, y_ready.nth(k))
                pool.tensor_tensor(ac[:, 5:7, :], chan_h[:].bitcast(f32), chan_l[:].bitcast(f32), ALU.add).then_inc(x1_sum.sem, 1)

            def hidden_low(k, t):
                pool.wait_ge(hid_hi.sem, hid_hi.nth(k, t))
                pool.tensor_tensor(sl[:, t % 3, :], hid[:, t % 3, :], sh[:, t % 3, :].bitcast(f32), ALU.subtract).then_inc(hid_lo.sem, 1)

            def ffn_low(r, j):
                pool.wait_ge(ff_hi.sem, ff_hi.nth(r, j))
                pool.tensor_tensor(sl[:, j % 3, :], hid[:, j % 3, :], sh[:, j % 3, :].bitcast(f32), ALU.subtract).then_inc(ff_lo.sem, 1)

            def numerators(k, c):
                pool.wait_ge(q_phi.sem, q_phi.nth(k, c))
                pool.wait_ge(scanned.sem, scanned.nth(k, 4 * c + 3))
                pool.tensor_tensor(ac[:, 3 + c, :], ac[:, 2, :], ac[:, 3 + c, :], ALU.mult).then_inc(qk_ready.sem, 1)
                pool.tensor_tensor(ac[:, 5 + c, :], ac[:, 2, :], ac[:, 5 + c, :], ALU.mult).then_inc(num_ready.sem, 1)

            raw = tok3[:].rearrange("p b n -> p (b n)")

            def split_piece(m, hi, lo, c, n):
                slot = raw[:, (m % 2) * PIECE:(m % 2 + 1) * PIECE]
                pool.wait_ge(piece_loaded[m % 2].sem, 16 * (m // 2 + 1))
                pool.tensor_scalar(wh[:, c:c + PIECE], slot, 1.0, None, ALU.mult).then_inc(hi.sem, 1)
                pool.wait_ge(hi.sem, hi.nth(n))
                pool.tensor_tensor(wl[:, c:c + PIECE], slot, wh[:, c:c + PIECE].bitcast(f32), ALU.subtract).then_inc(lo.sem, 1)

            def expert_piece(n):
                split_piece(n, exp_hi, exp_lo, EXPERTS + n * PIECE, n)

            def ffn_piece(n):
                split_piece(EXPERT_PIECES + ATTN_PIECES + n, ffn_w_hi, ffn_w_lo, W1 + n * PIECE, n)

            def experts(r):
                x1_whole(r)
                for t in range(NT):
                    hidden_low(r, t)
                    if t == 0 and later(r):
                        rstd(2, r - 1)

            def rest(r, has_ffn):
                more = more_chunks(r)

                def ff(j):
                    if has_ffn:
                        ffn_low(r, j)
                    else:
                        ffn_piece(j)
                rstd(1, r)
                if more:
                    rstd(0, r + 1)
                ff(0)
                ff(1)
                ff(2)
                numerators(r, 0)
                ff(3)
                ff(4)
                numerators(r, 1)
                ff(5)
                ff(6)
                ff(7)
                if has_ffn:
                    rstd(3, r - 1)
                rstd(2, r)
                if more:
                    residual1(r + 1)

            for n in range(6):
                expert_piece(n)
            rstd(0, 0)
            residual1(0)
            for n in range(6, EXPERT_PIECES):
                expert_piece(n)
            x1_whole(0)
            for t in range(NT):
                hidden_low(0, t)
            rest(0, False)
            pool.sem_inc(ff_lo.sem, FT)
            with pool.Fori(1, chunks - 1) as r:
                x1_whole(r)
                for t in range(NT):
                    hidden_low(r, t)
                rest(r, True)
            x1_whole(chunks - 1)
            for t in range(NT):
                hidden_low(chunks - 1, t)
            rest(chunks - 1, True)
            for j in range(FT):
                ffn_low(chunks, j)
            rstd(3, chunks - 1)


SET_C2 = 19
SET_ROWS = 22
IDLE_SPLIT = 24
IDLE_COPIED = 25


def kernel(**inputs):
    import numpy as np
    import concourse.bacc as bacc
    from concourse import mybir
    from concourse.bass_utils import run_bass_kernel_spmd as run

    g = {n: np.asarray(a) for n, a in inputs.items()}
    x = g["L0_attn_x"]
    batch, seq, d = x.shape

    def rows_first(a):
        k, n = a.shape
        return a.reshape(k // 128, 128, n).transpose(1, 0, 2).reshape(128, -1)

    parts = [g["L0_attn_Wa"].T, g["L0_attn_Wx"].T, g["L0_ffn_down_w"], g["L0_ffn_router_w"], g["L0_ffn_shared_w1"],
             g["L0_ffn_shared_w2"], g["L0_ffn_core_w"], g["L0_ffn_up_w"]]
    for e in range(E):
        parts += [g[f"L0_ffn_e{e}_w1"], g[f"L0_ffn_e{e}_w2"]]
    parts += [g["L1_attn_w_qkv"], g["L1_attn_w_out"], g["L1_ffn_W1"].T, g["L1_ffn_W3"].T, g["L1_ffn_W2"].T]
    weights = np.concatenate([rows_first(a) for a in parts], axis=1)

    cols = [g["L0_attn_ba"], g["L0_attn_bx"], g["L0_attn_Lam"], g["L0_ffn_down_b"], g["L0_ffn_shared_b1"], g["L0_ffn_shared_b2"]]
    cols += [g[f"L0_ffn_e{e}_b1"] for e in range(E)] + [g[f"L0_ffn_e{e}_b2"] for e in range(E)]
    cols += [np.repeat(g["L1_attn_decay_param"], HEAD)]
    vectors = np.concatenate([a.reshape(-1, 128).T for a in cols], axis=1)
    rows = np.concatenate([g["L0_ffn_up_b"], g["L0_ffn_core_b"], np.tile(g["L0_ffn_router_b"], NB)])

    had = np.array([[1.0]])
    while had.shape[0] < 128:
        had = np.block([[had, had], [had, -had]])
    head = np.zeros((128, CT, HEADS))
    for p in range(128):
        for c in range(CT):
            head[p, c, (c * 128 + p) // HEAD] = 1.0
    consts = np.concatenate([np.eye(128), had / (2 * FF ** 0.5), head.reshape(128, -1),
                             np.tile(np.arange(E, 0, -1.0), (128, NB)), np.tile(np.array(COST), (128, NB))], axis=1).astype(np.float32)

    arrays = {"x_t": x.reshape(batch * seq, d).T, "weights": weights, "vectors": vectors, "rows": rows, "consts": consts}
    arrays = {n: np.ascontiguousarray(a) for n, a in arrays.items()}
    nc = bacc.Bacc("TRN2", target_bir_lowering=False, num_devices=1)
    aps = [nc.dram_tensor("in_" + n, a.shape, mybir.dt.from_np(a.dtype), kind="ExternalInput").ap() for n, a in arrays.items()]
    out = nc.dram_tensor("out", (batch * seq, d), mybir.dt.float32, kind="ExternalOutput").ap()
    program(nc, *aps, out)
    r = run(nc, [{"in_" + n: a for n, a in arrays.items()}], core_ids=[0])
    return r.results[0]["out"].reshape(batch, seq, d)
```

```python
import concourse.bass as bass
from concourse import mybir
from contextlib import ExitStack

HID = [128, 256, 384, 512, 128, 256, 384, 512]
E = len(HID)
D = 256
L = 128
FF = 1024
SEQ = 256
CHUNK = 512
CT = D // 128
NB = CHUNK // 128
HEADS, HEAD = 16, 16
FT = FF // 128
TILES = [(-1, 0)] + [(e, j) for e in range(E) for j in range(HID[e] // 128)]
NT = len(TILES)
AHEAD = 6
LAG = 3
X3_TILE = 6
GATE_TILES = (9, 11)
GATES_TURN = 5
ROOT_TILE = 15
CORE_TILES = (13, 18)
SUMS_TILE = 8
HAD_STEPS = 3
EPS = 1e-5
COST = [1e-7 * 2 * L * h for h in HID]

_at = 0


def _cols(n):
    global _at
    _at += n
    return _at - n


WA = _cols(CT * D)
WX = _cols(CT * D)
DOWN = _cols(CT * L)
ROUTER = _cols(CT * E)
SW1 = _cols(L)
SW2 = _cols(L)
CORE = _cols(CT * D)
UP = _cols(D)
EXPERTS = _at
EW1, EW2 = [], []
for _h in HID:
    EW1.append(_cols(_h))
    EW2.append(_cols(_h))
QKV = _cols(CT * 3 * D)
WOUT = _cols(CT * D)
W1 = _cols(CT * FF)
W3 = _cols(CT * FF)
W2 = _cols(FT * D)
WCOLS = _at
PIECE = 512
PIECES = (W2 - EXPERTS) // PIECE
EARLY = (W1 - EXPERTS) // PIECE
W2_PIECES = FT * D // PIECE
SLOTS = 8

V_BA, V_BX, V_LAM, V_DOWN, V_S1, V_S2, V_E1, V_E2, V_DEC = 0, 2, 4, 6, 7, 8, 9, 9 + NT - 1, 9 + NT - 1 + E
VCOLS = V_DEC + CT
C_ID, C_HAD, C_HEAD, C_REV, C_COST = 0, 128, 256, 256 + CT * HEADS, 256 + CT * HEADS + NB * E
CCOLS = C_COST + NB * E


def program(nc, x_in, weights, vectors, rows, consts, out):
    f32, f32r = mybir.dt.float32, mybir.dt.float32r
    ALU, ACT, AX = mybir.AluOpType, mybir.ActivationFunctionType, mybir.AxisListType
    chunks = x_in.shape[1] // CHUNK
    x_chunks = x_in.rearrange("(c p) (k t) -> k p c t", p=128, t=CHUNK)
    out_chunks = out.rearrange("(k b p) n -> k p b n", b=NB, p=128)
    gates_dram = nc.dram_tensor("gates_scratch", (chunks, E, CHUNK), f32, kind="Internal").ap()

    with ExitStack() as ctx:
        def sb(name, shape, dt=f32):
            return ctx.enter_context(nc.sbuf_tensor(name, shape, dt))

        def before(name, shape):
            with nc.sbuf_tensor(name, shape, f32) as t:
                return t

        wh = sb("weights_hi", [128, WCOLS], f32r)
        wl = sb("weights_lo", [128, WCOLS], f32r)
        xy = sb("x_then_y", [128, CT, CHUNK])
        chan_h = sb("chan_hi", [128, CT, CHUNK], f32r)
        chan_l = sb("chan_lo", [128, CT, CHUNK], f32r)
        mid_raw = before("mid_raw", [128, 2 * CT, CHUNK])
        mid_h = sb("mid_hi", [128, CT, CHUNK], f32r)
        mid_l = sb("mid_lo", [128, CT, CHUNK], f32r)
        w2_raw = before("w2_raw", [128, FT * D])
        ffn_h = sb("ffn_hi", [128, CT, CHUNK], f32r)
        ffn_l = sb("ffn_lo", [128, CT, CHUNK], f32r)
        tok = sb("tok", [128, NB, D])
        tok3 = sb("tok3", [128, NB, D])
        gate = sb("gate_rows", [128, 2, CHUNK])
        ac = sb("gate_attn_work", [128, 7, CHUNK])
        hid = sb("hidden", [128, 5, CHUNK])
        sh = sb("hidden_hi", [128, 4, CHUNK], f32r)
        sl = sb("hidden_lo", [128, 3, CHUNK], f32r)
        h_raw = before("h_raw", [128, CHUNK])
        sl3 = sb("input_lo", [128, CHUNK], f32r)
        cst = sb("consts", [128, CCOLS])
        vec = sb("vectors", [128, VCOLS])
        bias_uc = sb("bias_up_core", [128, D])
        bias_r = sb("bias_router", [128, NB * E])
        half_b = sb("half_gate_bias", [128, 2 * CT])
        c2 = sb("half_log_decay", [128, CT])
        nc2 = sb("neg_half_log_decay", [128, CT])
        ser = sb("softplus_work", [128, 5, CT])
        s2b = sb("shared_bias_tenth", [128, 1])
        decay = sb("attn_decay", [128, CT])
        b1g = sb("gelu_of_bias", [128, NT - 1])
        b1s = sb("gelu_of_bias_split", [128, NT - 1, 2], f32r)
        idle2 = sb("idle_parts", [128, 2 * E])
        idle = sb("idle_expert", [128, E])
        idle_sum = sb("idle_sum", [128, 2])
        neg_half = sb("neg_half", [128, NB])
        rt = sb("routing", [128, 9, NB * E])
        r4 = sb("routing_per_token", [128, 12, NB])
        gt = hid[0:NB * E, 3, 0:128]
        lg = hid[0:E, 4, :]
        rden = sb("denominators", [128, NB * HEADS])
        st = [sb(f"ln{i}_stats", [128, NB, 6]) for i in range(4)]
        mv = [sb(f"ln{i}_mean_var", [128, NB, 2]) for i in range(4)]
        rs = [sb(f"ln{i}_rstd", [128, 4, NB]) for i in range(4)]
        ident = cst[:, C_ID:C_ID + 128]
        R = [ctx.enter_context(nc.psum_tensor(f"R{i}", [128, CHUNK], f32)) for i in range(6)]
        M = [ctx.enter_context(nc.psum_tensor(f"M{i}", [128, CHUNK], f32)) for i in range(2)]

        class Signal:

            def __init__(self, name, per=1, by=1):
                self.sem, self.per, self.by = ctx.enter_context(nc.semaphore(name)), per, by

            def nth(self, k, i=0):
                return (k * self.per + i + 1) * self.by

        def later(k):
            return not isinstance(k, int) or k > 0

        def more_chunks(k):
            return not isinstance(k, int) or k < chunks - 1

        wait_carried = Signal("wait_carried")

        def apart(eng):
            eng.sem_inc(wait_carried.sem, 1)

        S = Signal
        x_loaded, gates_stored = S("x_loaded", 1, 16), S("gates_stored", 1, 16)
        row_loaded = [S(f"gate_row_loaded{i}", E // 2, 16) for i in range(2)]
        out_stored = S("out_stored", 1, 16)
        small_loaded, w0_loaded, w1_loaded = S("small_loaded", 1, 16), S("w_gates_loaded", 1, 16), S("w_dense_loaded", 1, 16)
        rows_loaded, vec_loaded = S("rows_loaded", 1, 16), S("vec_loaded", 1, 16)
        piece_loaded = [S(f"piece_loaded{i}", 1, 16) for i in range(SLOTS)]
        w2_loaded = S("w2_loaded", 1, 16)
        dense_hi, dense_lo = S("dense_hi"), S("dense_lo")
        piece_hi, piece_lo = S("piece_hi"), S("piece_lo")
        had_step, had_z, had_hi, had_lo = S("had_step"), S("had_z"), S("had_hi"), S("had_lo")
        setup_act, setup_dve, idle_z = S("setup_act"), S("setup_dve"), S("idle_z", 2)
        x_hi, x_lo, gate_z = S("x_hi", CT), S("x_lo", CT), S("gate_z", 4)
        tanh_r, tanh_i, a_exp, a_tanh, a_sq = (S(n, CT) for n in ("tanh_r", "tanh_i", "a_exp", "a_tanh", "a_square"))
        a_cut, w_ready, w_root = S("a_cut", CT), S("w_ready", CT), S("w_root")
        ix_ready, u_ready, state_ready, y_ready = (S(n, CT) for n in ("ix_ready", "u_ready", "state_ready", "y_ready"))
        y_turned, y_copied, x1_turned = (S(n, 2) for n in ("y_turned", "y_copied", "x1_turned"))
        x1_hi, x1_lo, resid1 = S("x1_hi", 2), S("x1_lo", 2), S("resid1", 2)
        ln_stats = [S(f"ln{i}_stats_s", NB) for i in range(4)]
        ln_mv = [S(f"ln{i}_mv_s", NB) for i in range(4)]
        ln_var = [S(f"ln{i}_var_s", 2) for i in range(4)]
        ln_rstd = [S(f"ln{i}_rstd_s") for i in range(4)]
        ln_shift = [S(f"ln{i}_shift_s") for i in range(4)]
        ln_done = [S(f"ln{i}_done", NB) for i in range(4)]
        logit_z, logit_copied, logit_turned = S("logit_z"), S("logit_copied"), S("logit_turned")
        ROUTE = 22
        route, route_exp, route_tanh = S("route", ROUTE), S("route_exp"), S("route_tanh")
        gate_turned, gate_copied = S("gate_turned"), S("gate_copied")
        down_z, down_copied, h_act, h_hi, h_lo = (S(n) for n in ("down_z", "down_copied", "h_act", "h_hi", "h_lo"))
        x1_sum, g1_act, g1_hi, g1_lo = S("x1_sum"), S("g1_act", CT), S("g1_hi", CT), S("g1_lo", CT)
        hid_z, hid_act, hid_hi, hid_lo, hid_used = (S(n, NT) for n in ("hid_z", "hid_act", "hid_hi", "hid_lo", "hid_used"))
        combined, summed = S("combined", E + 1), S("summed", E)
        m_hi, m_lo, moe_out, y2_ready = S("m_hi"), S("m_lo"), S("moe_out", 2), S("y2_ready", 2)
        x2_turned, x2_hi, x2_lo = S("x2_turned", 2), S("x2_hi", 2), S("x2_lo", 2)
        k_z, v_z, q_z = (S(n, CT) for n in ("k_z", "v_z", "q_z"))
        k_exp, k_min, k_phi, kv_ready, q_exp, q_min, q_phi = (S(n, CT) for n in ("k_exp", "k_min", "k_phi", "kv_ready", "q_exp", "q_min", "q_phi"))
        scanned, qk_ready, num_ready = S("scanned", 4 * CT), S("qk_ready", CT), S("num_ready", CT)
        den_z, den_copied, den_turned, den_max, den_inv, den_wide = (S(n) for n in ("den_z", "den_copied", "den_turned", "den_max", "den_inv", "den_wide"))
        inv_turned, o_ready, o_hi, o_lo = (S(n, CT) for n in ("inv_turned", "o_ready", "o_hi", "o_lo"))
        attn_out, y3_ready = S("attn_out", 2), S("y3_ready", 2)
        x3_turned, x3_hi, x3_lo = S("x3_turned", 2), S("x3_hi", 2), S("x3_lo", 2)
        ff_z, ff_tanh, ff_silu, ff_hid, ff_hi, ff_lo, ff_used = (S(n, FT) for n in ("ff_z", "ff_tanh", "ff_silu", "ff_hid", "ff_hi", "ff_lo", "ff_used"))
        y4_ready = S("y4_ready", 2)

        def raw_piece(m):
            if m < SLOTS and m >= 2:
                if m < 2 + 2 * CT:
                    return mid_raw[:, m - 2, :]
                return tok[:, (m % 2) * 2:(m % 2) * 2 + 2, :].rearrange("p b n -> p (b n)")
            return tok3[:, (m % 2) * 2:(m % 2) * 2 + 2, :].rearrange("p b n -> p (b n)")

        def piece_signal(m):
            if m < SLOTS:
                return piece_loaded[m], 16
            return piece_loaded[m % 2], 16 * ((m - SLOTS) // 2 + 2)

        block = ctx.enter_context(nc.Block())

        def last_tile(o):
            return max(t for t, (e, _) in enumerate(TILES) if e == o - 1)

        @block.sync
        def _(sp):
            def piece(m):
                if m >= SLOTS:
                    sp.wait_ge(piece_lo.sem, piece_lo.nth(m - (SLOTS if m < SLOTS + 2 else 2)))
                c = EXPERTS + m * PIECE
                sp.dma_start(raw_piece(m), weights[:, c:c + PIECE]).then_inc(piece_signal(m)[0].sem, 16)

            def load_x(k):
                if later(k):
                    sp.wait_ge(y_turned.sem, y_turned.nth(k - 1, 1))
                    apart(sp)
                sp.dma_start(xy[:], x_chunks[k]).then_inc(x_loaded.sem, 16)

            def store_gates(k):
                sp.wait_ge(gate_copied.sem, gate_copied.nth(k))
                sp.dma_start(gates_dram[k].rearrange("e (b t) -> (e b) t", t=128), gt).then_inc(gates_stored.sem, 16)

            def gate_row(k, e):
                if e == 0:
                    sp.wait_ge(gates_stored.sem, gates_stored.nth(k))
                    apart(sp)
                    sp.wait_ge(x1_turned.sem, x1_turned.nth(k, 1))
                    apart(sp)
                    sp.wait_ge(resid1.sem, resid1.nth(k, 1))
                elif e >= 2:
                    sp.wait_ge(combined.sem, combined.nth(k, e + 1 - 2))
                sp.dma_start(gate[:, e % 2, :], gates_dram[k][e].partition_broadcast(128)).then_inc(row_loaded[e % 2].sem, 16)

            flat = hid[:].rearrange("p a n -> p (a n)")
            sp.dma_start(flat[:, 0:DOWN], weights[:, 0:DOWN]).then_inc(w0_loaded.sem, 16)
            sp.dma_start(xy[:], x_chunks[0]).then_inc(x_loaded.sem, 16)
            sp.dma_start(flat[:, DOWN:EXPERTS], weights[:, DOWN:EXPERTS]).then_inc(w1_loaded.sem, 16)
            for m in range(SLOTS):
                piece(m)
            sp.dma_start(w2_raw[:], weights[:, W2:WCOLS]).then_inc(w2_loaded.sem, 16)
            for m in range(SLOTS, EARLY):
                piece(m)
            load_x(1)
            store_gates(0)
            for e in range(E):
                gate_row(0, e)
            for m in range(EARLY, PIECES):
                piece(m)
            store_gates(1)
            with sp.Fori(1, chunks - 1) as r:
                load_x(r + 1)
                for e in range(E):
                    gate_row(r, e)
                store_gates(r + 1)
            for e in range(E):
                gate_row(chunks - 1, e)
            sp.wait_ge(out_stored.sem, out_stored.nth(chunks))
            sp.wait_ge(gates_stored.sem, gates_stored.nth(chunks - 1))

        @block.tensor
        def _(pe):
            def product(out, a, b, start=True, stop=True, shared=False):
                (ah, al), (bh, bl) = a, b
                pe.matmul(out, ah, bh, start=start, stop=False, skip_group_check=shared)
                pe.matmul(out, ah, bl, start=False, stop=False, skip_group_check=shared)
                return pe.matmul(out, al, bh, start=False, stop=stop, skip_group_check=shared)

            def w(c, n=128):
                return wh[:, c:c + n], wl[:, c:c + n]

            def two(h, l, i, lo=0, n=CHUNK):
                return h[:, i, lo:lo + n], l[:, i, lo:lo + n]

            def gates(k, c):
                pe.wait_ge(x_lo.sem, x_lo.nth(k, CT - 1))
                for g, base in enumerate((WA, WX)):
                    if c:
                        pe.wait_ge((tanh_r, tanh_i)[g].sem, (tanh_r, tanh_i)[g].nth(k, c - 1))
                    for kt in range(CT):
                        last = product(M[g][:], w(base + kt * D + c * 128), two(chan_h, chan_l, kt), kt == 0, kt == CT - 1)
                    last.then_inc(gate_z.sem, 1)

            def to_tokens(src, done):
                for b in range(NB):
                    for c in range(CT):
                        last = pe.transpose(M[b // 2][:, (b % 2) * D + c * 128:(b % 2) * D + (c + 1) * 128],
                                            src[:, c, b * 128:(b + 1) * 128], ident)
                    if b % 2:
                        last.then_inc(done.sem, 1)

            def to_channels(src, done):
                for c in range(CT):
                    for b in range(NB):
                        last = pe.transpose(M[c][:, b * 128:(b + 1) * 128], src[:, b, c * 128:(c + 1) * 128], ident)
                    last.then_inc(done.sem, 1)

            gate_tok = gate[:].rearrange("p a (b n) -> p (a b) n", n=D)

            def turn_y(k):
                pe.wait_ge(y_ready.sem, y_ready.nth(k, CT - 1))
                to_tokens(xy, y_turned)

            def turn_x1(k):
                pe.wait_ge(ln_done[0].sem, ln_done[0].nth(k, NB - 1))
                to_channels(gate_tok, x1_turned)

            def logits(k):
                pe.wait_ge(x1_lo.sem, x1_lo.nth(k, CT - 1))
                for kt in range(CT):
                    last = product(M[1][:], w(ROUTER + kt * E), two(chan_h, chan_l, kt), kt == 0, kt == CT - 1)
                last.then_inc(logit_z.sem, 1)

            def turn_logits(k):
                pe.wait_ge(logit_copied.sem, logit_copied.nth(k))
                apart(pe)
                for b in range(NB):
                    last = pe.transpose(M[1][:, b * E:(b + 1) * E], lg[:, b * 128:(b + 1) * 128], ident[0:E, 0:E])
                last.then_inc(logit_turned.sem, 1)

            def turn_gates(k):
                pe.wait_ge(route.sem, route.nth(k, ROUTE - 1))
                pe.transpose(M[0][0:NB * E, 0:128], rt[:, 8, :], ident).then_inc(gate_turned.sem, 1)

            def down(k):
                pe.wait_ge(x1_lo.sem, x1_lo.nth(k, CT - 1))
                for kt in range(CT):
                    last = product(M[1][:], w(DOWN + kt * L), two(chan_h, chan_l, kt), kt == 0, kt == CT - 1)
                last.then_inc(down_z.sem, 1)

            def idle_experts(some):
                pe.wait_ge(setup_dve.sem, setup_dve.nth(IDLE_SPLIT))
                for t, (e, j) in enumerate(TILES[1:]):
                    if e not in some:
                        continue
                    if j == 0:
                        pe.wait_ge(piece_lo.sem, piece_lo.nth((EW2[e] + HID[e] - EXPERTS - 1) // PIECE))
                    pe.matmul(R[5][:, 2 * e:2 * e + 2], wh[:, EW2[e] + j * 128:EW2[e] + (j + 1) * 128], b1s[:, t, :],
                              start=j == 0, stop=False)
                    last = pe.matmul(R[5][:, 2 * e:2 * e + 2], wl[:, EW2[e] + j * 128:EW2[e] + (j + 1) * 128], b1s[:, t, :],
                                     start=False, stop=j == HID[e] // 128 - 1)
                last.then_inc(idle_z.sem, 1)

            def first(k, t):
                e, j = TILES[t]
                if t == 0:
                    pe.wait_ge(h_lo.sem, h_lo.nth(k))
                if t < 3:
                    if later(k):
                        pe.wait_ge(ff_hid.sem, ff_hid.nth(k - 1, FT - 1))
                else:
                    pe.wait_ge(hid_act.sem, hid_act.nth(k, t - 3))
                product(R[t % 3][:], w(SW1 if e < 0 else EW1[e] + j * 128), (sh[:, 3, :], sl3[:])).then_inc(hid_z.sem, 1)

            def second(k, t):
                e, j = TILES[t]
                o = e + 1
                pe.wait_ge(hid_lo.sem, hid_lo.nth(k, t))
                if j == 0:
                    if o < 3:
                        if later(k):
                            pe.wait_ge(y4_ready.sem, y4_ready.nth(k - 1, 1))
                        if isinstance(k, int) and k == 0 and o == 2:
                            pe.wait_ge(setup_dve.sem, setup_dve.nth(IDLE_COPIED))
                    else:
                        pe.wait_ge(combined.sem, combined.nth(k, o - 3))
                n = 1 if e < 0 else HID[e] // 128
                product(R[3 + o % 3][:], w(SW2 if e < 0 else EW2[e] + j * 128), two(sh, sl, t % 3), j == 0, j == n - 1)\
                    .then_inc(hid_used.sem, 1)

            def core_product(k, half):
                pe.wait_ge(g1_lo.sem, g1_lo.nth(k, CT - 1))
                for b in (2 * half, 2 * half + 1):
                    for kt in range(CT):
                        product(M[half][:, (b % 2) * D:(b % 2 + 1) * D], two(mid_h, mid_l, kt, b * 128, 128),
                                w(CORE + kt * D, D), b % 2 == 0 and kt == 0, False, shared=True)

            def up_product(k):
                pe.wait_ge(m_lo.sem, m_lo.nth(k))
                for b in range(NB):
                    last = product(M[b // 2][:, (b % 2) * D:(b % 2 + 1) * D], (sh[:, 3, b * 128:(b + 1) * 128], sl3[:, b * 128:(b + 1) * 128]), w(UP, D),
                                   False, True, shared=True)
                    if b % 2:
                        last.then_inc(moe_out.sem, 1)

            def turn_x2(k):
                pe.wait_ge(ln_done[1].sem, ln_done[1].nth(k, NB - 1))
                to_channels(tok, x2_turned)

            def qkv(k, which, c):
                bank = which // 2
                for kt in range(CT):
                    last = product(M[bank][:], w(QKV + kt * 3 * D + which * D + c * 128), two(mid_h, mid_l, kt), kt == 0, kt == CT - 1)
                last.then_inc((q_z, k_z, v_z)[which].sem, 1)

            def denominators(k):
                for c in range(CT):
                    pe.wait_ge(qk_ready.sem, qk_ready.nth(k, c))
                    last = pe.matmul(M[0][0:HEADS, :], cst[:, C_HEAD + c * HEADS:C_HEAD + (c + 1) * HEADS], ac[:, 3 + c, :],
                                     start=c == 0, stop=c == CT - 1)
                last.then_inc(den_z.sem, 1)

            def turn_denominators(k):
                pe.wait_ge(den_copied.sem, den_copied.nth(k))
                apart(pe)
                for b in range(NB):
                    last = pe.transpose(M[1][:, b * HEADS:(b + 1) * HEADS], ac[0:HEADS, 2, b * 128:(b + 1) * 128],
                                        ident[0:HEADS, 0:HEADS])
                last.then_inc(den_turned.sem, 1)

            def turn_inverses(k):
                pe.wait_ge(den_wide.sem, den_wide.nth(k))
                wide = ac[:, 0:2, :].rearrange("p a (b n) -> p (a b) n", n=D)
                to_channels(wide, inv_turned)

            def attention_product(k):
                pe.wait_ge(o_lo.sem, o_lo.nth(k, CT - 1))
                for b in range(NB):
                    for kt in range(CT):
                        last = product(M[b // 2][:, (b % 2) * D:(b % 2 + 1) * D], two(mid_h, mid_l, kt, b * 128, 128),
                                       w(WOUT + kt * D, D), kt == 0, kt == CT - 1)
                    if b % 2:
                        last.then_inc(attn_out.sem, 1)

            def turn_x3(k):
                pe.wait_ge(ln_done[2].sem, ln_done[2].nth(k, NB - 1))
                pe.wait_ge(y3_ready.sem, y3_ready.nth(k, 1))
                to_channels(tok3, x3_turned)

            def ffn_first(r, j, tail=False):
                if j == 0:
                    if later(r):
                        pe.wait_ge(x3_lo.sem, x3_lo.nth(r - 1, CT - 1))
                p = 2 * (j % 2)
                if j < 2:
                    if not tail:
                        pe.wait_ge(hid_act.sem, hid_act.nth(r, NT - 1))
                        pe.wait_ge(combined.sem, combined.nth(r, E - 2))
                pe.wait_ge(ff_hid.sem, ff_hid.nth(r, j - 2))
                for g, base in enumerate((W1, W3)):
                    for kt in range(CT):
                        last = product(R[p + g][:], w(base + kt * FF + j * 128), two(ffn_h, ffn_l, kt), kt == 0, kt == CT - 1)
                last.then_inc(ff_z.sem, 1)

            def ffn_second(r, j, tail=False):
                pe.wait_ge(ff_lo.sem, ff_lo.nth(r, j))
                if j == 0:
                    if later(r):
                        pe.wait_ge(y4_ready.sem, y4_ready.nth(r - 1, 1))
                    if not tail:
                        pe.wait_ge(combined.sem, combined.nth(r, E))
                for b in range(NB):
                    last = product(R[4 + b // 2][:, (b % 2) * D:(b % 2 + 1) * D], two(sh, sl, j % 3, b * 128, 128),
                                   w(W2 + j * D, D), j == 0 and b % 2 == 0, j == FT - 1, shared=True)
                last.then_inc(ff_used.sem, 1)

            def experts(r):
                more = more_chunks(r)
                for t in range(NT + LAG):
                    if t < NT:
                        first(r, t)
                    if t == X3_TILE and later(r):
                        turn_x3(r - 1)
                    if t == 2 and not later(r):
                        idle_experts(range(5, E))
                    if t == GATES_TURN and not later(r):
                        turn_gates(0)
                        pe.wait_ge(gate_copied.sem, gate_copied.nth(0))
                    if t in GATE_TILES and more:
                        if t == GATE_TILES[0] and later(r):
                            pe.wait_ge(x3_lo.sem, x3_lo.nth(r - 1, CT - 1))
                        gates(r + 1, GATE_TILES.index(t))
                    if t in CORE_TILES:
                        half = CORE_TILES.index(t)
                        if more:
                            pe.wait_ge((tanh_r, tanh_i)[half].sem, (tanh_r, tanh_i)[half].nth(r + 1, CT - 1))
                        else:
                            pe.wait_ge(x3_lo.sem, x3_lo.nth(r - 1, CT - 1))
                        core_product(r, half)
                    if t >= LAG:
                        second(r, t - LAG)

            def rest(r, has_ffn):
                more = more_chunks(r)

                def ff(j):
                    if has_ffn:
                        ffn_first(r, j)
                        if 2 <= j < FT - 3:
                            ffn_second(r, j - 2)
                    elif j < W2_PIECES:
                        pe.wait_ge(had_step.sem, had_step.nth(2 * HAD_STEPS - 1))
                        pe.wait_ge(hid_act.sem, hid_act.nth(r, NT - 1))
                        pe.wait_ge(combined.sem, combined.nth(r, E))
                        pe.matmul(R[j][:], cst[:, C_HAD:C_HAD + 128], w2_raw[:, j * PIECE:(j + 1) * PIECE], start=True, stop=True)\
                            .then_inc(had_z.sem, 1)
                    elif j == FT - 1:
                        pe.sem_inc(ff_z.sem, FT)
                        pe.sem_inc(ff_used.sem, FT)
                ff(0)
                up_product(r)
                ff(1)
                pe.wait_ge(y2_ready.sem, y2_ready.nth(r, 1))
                if more:
                    turn_y(r + 1)
                ff(2)
                if more:
                    pe.wait_ge(y_copied.sem, y_copied.nth(r + 1, 1))
                turn_x2(r)
                ff(3)
                pe.wait_ge(x2_lo.sem, x2_lo.nth(r, 1))
                if more:
                    turn_x1(r + 1)
                ff(4)
                if more:
                    pe.wait_ge(x1_lo.sem, x1_lo.nth(r + 1, 1))
                qkv(r, 1, 0)
                qkv(r, 2, 0)
                ff(5)
                pe.wait_ge(k_phi.sem, k_phi.nth(r))
                qkv(r, 0, 0)
                pe.wait_ge(kv_ready.sem, kv_ready.nth(r))
                if more:
                    logits(r + 1)
                if has_ffn:
                    ffn_second(r, FT - 5)
                if more:
                    turn_logits(r + 1)
                pe.wait_ge(q_phi.sem, q_phi.nth(r))
                qkv(r, 1, 1)
                if more:
                    pe.wait_ge(route.sem, route.nth(r + 1))
                qkv(r, 2, 1)
                if has_ffn:
                    ffn_second(r, FT - 4)
                pe.wait_ge(k_phi.sem, k_phi.nth(r, 1))
                qkv(r, 0, 1)
                pe.wait_ge(kv_ready.sem, kv_ready.nth(r, 1))
                if more:
                    down(r + 1)
                ff(6)
                pe.wait_ge(q_phi.sem, q_phi.nth(r, 1))
                denominators(r)
                if has_ffn:
                    ffn_second(r, FT - 3)
                if more:
                    pe.wait_ge(down_copied.sem, down_copied.nth(r + 1))
                turn_denominators(r)
                ff(7)
                if more:
                    turn_gates(r + 1)
                    pe.wait_ge(gate_copied.sem, gate_copied.nth(r + 1))
                pe.wait_ge(den_max.sem, den_max.nth(r))
                turn_inverses(r)
                if has_ffn:
                    ffn_second(r, FT - 2)
                    ffn_second(r, FT - 1)
                attention_product(r)

            pe.wait_ge(small_loaded.sem, 16)
            pe.wait_ge(dense_lo.sem, dense_lo.nth(0))
            gates(0, 0)
            gates(0, 1)
            pe.wait_ge(tanh_r.sem, tanh_r.nth(0, 1))
            pe.wait_ge(tanh_i.sem, tanh_i.nth(0, 1))
            turn_y(0)
            idle_experts(range(0, 5))
            pe.wait_ge(y_copied.sem, y_copied.nth(0, 1))
            turn_x1(0)
            pe.wait_ge(dense_lo.sem, dense_lo.nth(1))
            down(0)
            pe.wait_ge(down_copied.sem, down_copied.nth(0))
            logits(0)
            turn_logits(0)
            experts(0)
            pe.wait_ge(piece_lo.sem, piece_lo.nth(EARLY - 1))
            rest(0, False)
            pe.wait_ge(piece_lo.sem, piece_lo.nth(PIECES - 1))
            pe.wait_ge(had_lo.sem, had_lo.nth(3))
            with pe.Fori(1, chunks - 1) as r:
                experts(r)
                rest(r, True)
            experts(chunks - 1)
            rest(chunks - 1, True)
            turn_x3(chunks - 1)
            for j in range(FT):
                ffn_first(chunks, j, tail=True)
                if j >= 2:
                    ffn_second(chunks, j - 2, tail=True)
            ffn_second(chunks, FT - 2, tail=True)
            ffn_second(chunks, FT - 1, tail=True)

        @block.scalar
        def _(act):
            def gates(k, c):
                if c == 0:
                    if later(k):
                        act.wait_ge(y_ready.sem, y_ready.nth(k - 1, CT - 1))
                    if later(k - 1):
                        act.wait_ge(inv_turned.sem, inv_turned.nth(k - 2, 1))
                        act.wait_ge(o_lo.sem, o_lo.nth(k - 2, CT - 1))
                act.wait_ge(gate_z.sem, gate_z.nth(k, 2 * c))
                act.activation(ac[:, c, :], M[0][:], ACT.Tanh, bias=half_b[:, c:c + 1], scale=0.5).then_inc(tanh_r.sem, 1)
                act.wait_ge(gate_z.sem, gate_z.nth(k, 2 * c + 1))
                act.activation(ac[:, 2 + c, :], M[1][:], ACT.Tanh, bias=half_b[:, CT + c:CT + c + 1], scale=0.5).then_inc(tanh_i.sem, 1)

            def decays(k, c):
                act.wait_ge(tanh_r.sem, tanh_r.nth(k, c))
                if c == 0 and later(k):
                    act.wait_ge(summed.sem, summed.nth(k - 1))
                    act.wait_ge(g1_lo.sem, g1_lo.nth(k - 1, CT - 1))
                act.activation(ac[:, 4 + c, :], ac[:, c, :], ACT.Exp, bias=c2[:, c:c + 1], scale=c2[:, c:c + 1]).then_inc(a_exp.sem, 1)

            def decay_parts(k, c):
                act.wait_ge(a_exp.sem, a_exp.nth(k, c))
                act.activation(ac[:, c, :], ac[:, c, :], ACT.Tanh, bias=nc2[:, c:c + 1], scale=nc2[:, c:c + 1]).then_inc(a_tanh.sem, 1)
                if c:
                    act.wait_ge(w_ready.sem, w_ready.nth(k, c - 1))
                act.activation(ac[:, 6, :], ac[:, 4 + c, :], ACT.Square).then_inc(a_sq.sem, 1)

            def root(k):
                act.wait_ge(w_ready.sem, w_ready.nth(k, CT - 1))
                act.activation(ac[:, 0:2, :], ac[:, 0:2, :], ACT.Sqrt).then_inc(w_root.sem, 1)

            def x_high(k, c):
                act.wait_ge(x_loaded.sem, x_loaded.nth(k))
                if later(k):
                    act.wait_ge(down_z.sem, down_z.nth(k - 1))
                    act.wait_ge(logit_z.sem, logit_z.nth(k - 1))
                    act.wait_ge(x1_sum.sem, x1_sum.nth(k - 1))
                act.activation(chan_h[:, c, :], xy[:, c, :], ACT.Copy).then_inc(x_hi.sem, 1)

            def normed(i, k, src, dst):
                act.wait_ge(ln_shift[i].sem, ln_shift[i].nth(k))
                for b in range(NB):
                    act.activation(dst(b), src(b), ACT.Identity, bias=rs[i][:, 3, b:b + 1], scale=rs[i][:, 1, b:b + 1])\
                        .then_inc(ln_done[i].sem, 1)

            def y_copy(k):
                if later(k):
                    act.wait_ge(combined.sem, combined.nth(k - 1, E))
                for i in range(2):
                    act.wait_ge(y_turned.sem, y_turned.nth(k, i))
                    act.activation(gate[:, i, :], M[i][:], ACT.Copy).then_inc(y_copied.sem, 1)

            def x1_norm(k):
                normed(0, k, lambda b: gate_tok[:, b, :], lambda b: gate_tok[:, b, :])

            def x2_norm(k):
                normed(1, k, lambda b: tok[:, b, :], lambda b: tok[:, b, :])

            def x3_norm(k):
                normed(2, k, lambda b: tok3[:, b, :], lambda b: tok3[:, b, :])

            y4 = hid[:, 3:5, :].rearrange("p a (b n) -> p (a b) n", n=D)
            gate_tok = gate[:].rearrange("p a (b n) -> p (a b) n", n=D)

            def out_norm(r):
                normed(3, r - 1, lambda b: y4[:, b, :], lambda b: y4[:, b, :])
                act.wait_ge(ln_done[3].sem, ln_done[3].nth(r - 1, NB - 1))
                apart(act)
                act.dma_start(out_chunks[r - 1], y4).then_inc(out_stored.sem, 16)

            def x1_high(k):
                for c in range(CT):
                    act.wait_ge(x1_turned.sem, x1_turned.nth(k, c))
                    act.wait_ge(gate_z.sem, gate_z.nth(k, 3))
                    act.activation(chan_h[:, c, :], M[c][:], ACT.Copy).then_inc(x1_hi.sem, 1)

            def logit_copy(k):
                act.wait_ge(logit_z.sem, logit_z.nth(k))
                if later(k):
                    act.wait_ge(m_lo.sem, m_lo.nth(k - 1))
                act.activation(lg, M[1][0:E, :], ACT.Copy).then_inc(logit_copied.sem, 1)

            def route_e(k):
                act.wait_ge(route.sem, route.nth(k, 2))
                act.activation(rt[:, 2, :], rt[:, 1, :], ACT.Exp).then_inc(route_exp.sem, 1)

            def route_t(k):
                act.wait_ge(route.sem, route.nth(k, 16))
                act.activation(r4[:, 6, :], r4[:, 5, :], ACT.Tanh, scale=-0.5).then_inc(route_tanh.sem, 1)

            def gate_copy(k):
                act.wait_ge(gate_turned.sem, gate_turned.nth(k))
                if later(k):
                    act.wait_ge(m_lo.sem, m_lo.nth(k - 1))
                act.activation(gt, M[0][0:NB * E, 0:128], ACT.Copy).then_inc(gate_copied.sem, 1)

            def down_copy(k):
                act.wait_ge(down_z.sem, down_z.nth(k))
                if later(k):
                    act.wait_ge(moe_out.sem, moe_out.nth(k - 1, 1))
                act.activation(h_raw[:], M[1][:], ACT.Identity, bias=vec[:, V_DOWN:V_DOWN + 1]).then_inc(down_copied.sem, 1)

            def h_gelu(k):
                act.wait_ge(down_copied.sem, down_copied.nth(k))
                act.activation(sh[:, 3, :], h_raw[:], ACT.Gelu).then_inc(h_hi.sem, 1)
                act.wait_ge(h_hi.sem, h_hi.nth(k))
                act.activation(h_raw[:], h_raw[:], ACT.Gelu).then_inc(h_act.sem, 1)

            def g1_gelu(k, c):
                act.wait_ge(x1_sum.sem, x1_sum.nth(k))
                act.activation(ac[:, 5 + c, :], ac[:, 5 + c, :], ACT.Gelu).then_inc(g1_act.sem, 1)

            def hidden(k, t):
                act.wait_ge(hid_z.sem, hid_z.nth(k, t))
                if t < 3:
                    if later(k):
                        act.wait_ge(ff_lo.sem, ff_lo.nth(k - 1, FT - 1))
                else:
                    act.wait_ge(hid_lo.sem, hid_lo.nth(k, t - 3))
                b = vec[:, V_S1:V_S1 + 1] if t == 0 else vec[:, V_E1 + t - 1:V_E1 + t]
                act.activation(hid[:, t % 3, :], R[t % 3][:], ACT.Gelu, bias=b).then_inc(hid_act.sem, 1)

            def x2_high(k):
                for c in range(CT):
                    act.wait_ge(x2_turned.sem, x2_turned.nth(k, c))
                    act.activation(mid_h[:, c, :], M[c][:], ACT.Copy).then_inc(x2_hi.sem, 1)

            def key_exp(k, c):
                act.wait_ge(k_z.sem, k_z.nth(k, c))
                if c == 0:
                    if more_chunks(k):
                        act.wait_ge(y_ready.sem, y_ready.nth(k + 1, CT - 1))
                else:
                    act.wait_ge(scanned.sem, scanned.nth(k, 4 * c - 1))
                act.activation(ac[:, 0, :], M[0][:], ACT.Exp).then_inc(k_exp.sem, 1)

            def query_exp(k, c):
                act.wait_ge(q_z.sem, q_z.nth(k, c))
                if c:
                    act.wait_ge(num_ready.sem, num_ready.nth(k, c - 1))
                act.activation(ac[:, 2, :], M[0][:], ACT.Exp).then_inc(q_exp.sem, 1)

            def den_copy(k):
                act.wait_ge(den_z.sem, den_z.nth(k))
                act.wait_ge(num_ready.sem, num_ready.nth(k, CT - 1))
                act.activation(ac[0:HEADS, 2, :], M[0][0:HEADS, :], ACT.Copy).then_inc(den_copied.sem, 1)

            def den_expand(k):
                act.wait_ge(den_inv.sem, den_inv.nth(k))
                act.wait_ge(scanned.sem, scanned.nth(k, 4 * CT - 1))
                act.activation(ac[:, 0:2, :].rearrange("p a (n d) -> p (a n) d", d=HEAD),
                               rden[:].unsqueeze(2).broadcast_to([128, NB * HEADS, HEAD]), ACT.Copy).then_inc(den_wide.sem, 1)

            def o_high(k, c):
                act.wait_ge(o_ready.sem, o_ready.nth(k, c))
                act.wait_ge(q_z.sem, q_z.nth(k, CT - 1))
                act.wait_ge(v_z.sem, v_z.nth(k, CT - 1))
                act.activation(mid_h[:, c, :], ac[:, 5 + c, :], ACT.Copy).then_inc(o_hi.sem, 1)

            def x3_high(k):
                for c in range(CT):
                    act.wait_ge(x3_turned.sem, x3_turned.nth(k, c))
                    act.wait_ge(ff_z.sem, ff_z.nth(k, FT - 1))
                    act.activation(ffn_h[:, c, :], M[c][:], ACT.Copy).then_inc(x3_hi.sem, 1)

            def ffn(r, j, tail=False):
                act.wait_ge(ff_z.sem, ff_z.nth(r, j))
                if j < 3 and not tail:
                    act.wait_ge(hid_lo.sem, hid_lo.nth(r, NT - 1))
                act.wait_ge(ff_lo.sem, ff_lo.nth(r, j - 3))
                act.activation(hid[:, j % 3, :], R[2 * (j % 2)][:], ACT.Tanh, scale=0.5).then_inc(ff_tanh.sem, 1)

            def experts(r):
                more = more_chunks(r)
                if later(r):
                    x3_high(r - 1)
                for t in range(AHEAD, NT):
                    hidden(r, t)
                    if more:
                        if t in (6, 7):
                            x_high(r + 1, t - 6)
                        if t in GATE_TILES:
                            gates(r + 1, GATE_TILES.index(t))
                        if t == GATE_TILES[1] + 1:
                            decays(r + 1, 0)
                            decays(r + 1, 1)
                        if t in (GATE_TILES[1] + 2, GATE_TILES[1] + 3):
                            decay_parts(r + 1, t - GATE_TILES[1] - 2)
                        if t == ROOT_TILE:
                            root(r + 1)

            def rest(r, has_ffn):
                more = more_chunks(r)

                def ff(j):
                    if has_ffn:
                        ffn(r, j)
                    else:
                        weights_high(EARLY + j)
                        if j < W2_PIECES:
                            had_high(j)
                        if j == FT - 1:
                            act.sem_inc(ff_tanh.sem, FT)
                            act.sem_inc(out_stored.sem, 16)
                ff(0)
                if more:
                    y_copy(r + 1)
                ff(1)
                x2_norm(r)
                x2_high(r)
                if more:
                    x1_norm(r + 1)
                ff(2)
                ff(3)
                if more:
                    x1_high(r + 1)
                ff(4)
                key_exp(r, 0)
                ff(5)
                query_exp(r, 0)
                if more:
                    logit_copy(r + 1)
                key_exp(r, 1)
                if more:
                    route_e(r + 1)
                query_exp(r, 1)
                if more:
                    down_copy(r + 1)
                ff(6)
                den_copy(r)
                if more:
                    route_t(r + 1)
                den_expand(r)
                ff(7)
                if more:
                    gate_copy(r + 1)
                o_high(r, 0)
                o_high(r, 1)
                if more:
                    h_gelu(r + 1)
                    for t in range(4):
                        hidden(r + 1, t)
                        if t in (1, 2):
                            g1_gelu(r + 1, t - 1)
                x3_norm(r)
                if more:
                    hidden(r + 1, 4)
                    hidden(r + 1, 5)
                if has_ffn:
                    out_norm(r)

            flat = hid[:].rearrange("p a n -> p (a n)")

            def weights_high(m):
                signal, count = piece_signal(m)
                act.wait_ge(signal.sem, count)
                c = EXPERTS + m * PIECE
                act.activation(wh[:, c:c + PIECE], raw_piece(m), ACT.Copy).then_inc(piece_hi.sem, 1)

            def had_high(q):
                act.wait_ge(had_z.sem, had_z.nth(q))
                act.activation(wh[:, W2 + q * PIECE:W2 + (q + 1) * PIECE], R[q][:], ACT.Copy).then_inc(had_hi.sem, 1)

            act.dma_start(vec[:], vectors).then_inc(vec_loaded.sem, 16)
            act.dma_start(cst[:], consts).then_inc(small_loaded.sem, 16)
            act.dma_start(ac[:, 0:2, :].rearrange("p a n -> p (a n)")[:, 0:rows.shape[0]], rows.partition_broadcast(128)).then_inc(rows_loaded.sem, 16)
            act.wait_ge(vec_loaded.sem, 16)
            act.activation(ser[:, 0, :], vec[:, V_LAM:V_LAM + CT], ACT.Abs).then_inc(setup_act.sem, 1)
            act.wait_ge(setup_act.sem, setup_act.nth(0))
            act.activation(ser[:, 1, :], ser[:, 0, :], ACT.Exp, scale=-1.0).then_inc(setup_act.sem, 1)
            act.activation(decay[:, :], vec[:, V_DEC:V_DEC + CT], ACT.Tanh, scale=0.5).then_inc(setup_act.sem, 1)
            for m in range(6):
                weights_high(m)
            act.wait_ge(setup_dve.sem, setup_dve.nth(SET_ROWS))
            act.wait_ge(setup_dve.sem, setup_dve.nth(SET_C2))
            gates(0, 0)
            decays(0, 0)
            decay_parts(0, 0)
            weights_high(6)
            weights_high(7)
            gates(0, 1)
            decays(0, 1)
            decay_parts(0, 1)
            root(0)
            act.wait_ge(w1_loaded.sem, 16)
            act.activation(wh[:, DOWN:EXPERTS], flat[:, DOWN:EXPERTS], ACT.Copy).then_inc(dense_hi.sem, 1)
            weights_high(8)
            weights_high(9)
            act.activation(b1g[:, :], vec[:, V_E1:V_E1 + NT - 1], ACT.Gelu).then_inc(setup_act.sem, 1)
            y_copy(0)
            weights_high(10)
            weights_high(11)
            x1_norm(0)
            x1_high(0)
            down_copy(0)
            h_gelu(0)
            logit_copy(0)
            hidden(0, 0)
            hidden(0, 1)
            hidden(0, 2)
            route_e(0)
            g1_gelu(0, 0)
            hidden(0, 3)
            route_t(0)
            g1_gelu(0, 1)
            hidden(0, 4)
            gate_copy(0)
            hidden(0, 5)
            weights_high(12)
            weights_high(13)
            experts(0)
            rest(0, False)
            with act.Fori(1, chunks - 1) as r:
                experts(r)
                rest(r, True)
            experts(chunks - 1)
            rest(chunks - 1, True)
            x3_high(chunks - 1)
            for j in range(FT):
                ffn(chunks, j, tail=True)
            out_norm(chunks)

        @block.vector
        def _(dve):
            def x_low(k, c):
                dve.wait_ge(x_hi.sem, x_hi.nth(k, c))
                dve.tensor_tensor(chan_l[:, c, :], xy[:, c, :], chan_h[:, c, :].bitcast(f32), ALU.subtract).then_inc(x_lo.sem, 1)

            def roots(k, c):
                dve.wait_ge(a_sq.sem, a_sq.nth(k, c))
                dve.wait_ge(a_tanh.sem, a_tanh.nth(k, c))
                dve.scalar_tensor_tensor(out=ac[:, c, :], in0=ac[:, 6, :], scalar=1.0, in1=ac[:, c, :], op0=ALU.add, op1=ALU.mult)\
                    .then_inc(w_ready.sem, 1)

            def gated_input(k, c):
                dve.wait_ge(tanh_i.sem, tanh_i.nth(k, c))
                dve.scalar_tensor_tensor(out=ac[:, 2 + c, :], in0=ac[:, 2 + c, :], scalar=1.0, in1=xy[:, c, :], op0=ALU.add, op1=ALU.mult)\
                    .then_inc(ix_ready.sem, 1)

            def cut_decay(k, c):
                dve.wait_ge(a_sq.sem, a_sq.nth(k, c))
                dve.memset(ac[:, 4 + c, :].rearrange("p (s t) -> p s t", t=SEQ)[:, :, 0:1], 0.0).then_inc(a_cut.sem, 1)

            def step_input(k, c):
                dve.wait_ge(w_root.sem, w_root.nth(k))
                dve.wait_ge(ix_ready.sem, ix_ready.nth(k, c))
                dve.scalar_tensor_tensor(out=ac[:, 2 + c, :], in0=ac[:, c, :], scalar=0.5, in1=ac[:, 2 + c, :], op0=ALU.mult, op1=ALU.mult)\
                    .then_inc(u_ready.sem, 1)

            def states(k, c):
                dve.wait_ge(u_ready.sem, u_ready.nth(k, c))
                dve.wait_ge(a_cut.sem, a_cut.nth(k, c))
                dve.tensor_tensor_scan(ac[:, c, :], ac[:, 4 + c, :], ac[:, 2 + c, :], 0.0, ALU.mult, ALU.add).then_inc(state_ready.sem, 1)

            def add_x(k, c):
                dve.wait_ge(state_ready.sem, state_ready.nth(k, c))
                dve.tensor_tensor(xy[:, c, :], ac[:, c, :], xy[:, c, :], ALU.add).then_inc(y_ready.sem, 1)

            def stats(i, k, src, ready, halves=(0, 1)):
                for b in range(NB):
                    if b // 2 in halves:
                        ready(b)
                        dve.bn_stats(st[i][:, b, :], src(b)).then_inc(ln_stats[i].sem, 1)
                if 1 not in halves:
                    return
                dve.wait_ge(ln_stats[i].sem, ln_stats[i].nth(k, NB - 1))
                if later(k):
                    apart(dve)
                    dve.wait_ge(ln_done[i].sem, ln_done[i].nth(k - 1, NB - 1))
                apart(dve)
                for b in range(NB):
                    dve.bn_aggr(mv[i][:, b, :], st[i][:, b, :]).then_inc(ln_mv[i].sem, 1)
                dve.wait_ge(ln_mv[i].sem, ln_mv[i].nth(k, NB - 1))
                apart(dve)
                dve.tensor_scalar(rs[i][:, 0, :], mv[i][:, :, 1], EPS, None, ALU.add).then_inc(ln_var[i].sem, 1)
                dve.tensor_scalar(rs[i][:, 2, :], mv[i][:, :, 0], -1.0, None, ALU.mult).then_inc(ln_var[i].sem, 1)

            gate_tok = gate[:].rearrange("p a (b n) -> p (a b) n", n=D)

            def x1_stats(k):
                stats(0, k, lambda b: gate_tok[:, b, :], lambda b: dve.wait_ge(y_copied.sem, y_copied.nth(k, b // 2)))

            def residual1(k, i):
                dve.wait_ge(ln_done[0].sem, ln_done[0].nth(k, NB - 1))
                if later(k):
                    dve.wait_ge(y3_ready.sem, y3_ready.nth(k - 1, 1))
                dve.tensor_tensor(tok[:, 2 * i:2 * i + 2, :], gate_tok[:, 2 * i:2 * i + 2, :], bias_uc[:].unsqueeze(1).broadcast_to([128, 2, D]), ALU.add)\
                    .then_inc(resid1.sem, 1)

            def x1_low(k):
                for c in range(CT):
                    dve.wait_ge(x1_hi.sem, x1_hi.nth(k, c))
                    dve.tensor_tensor(chan_l[:, c, :], M[c][:], chan_h[:, c, :].bitcast(f32), ALU.subtract).then_inc(x1_lo.sem, 1)

            def grid(ap):
                return ap.rearrange("p (b e) -> p b e", e=E)

            def over(ap):
                return ap.unsqueeze(2).broadcast_to([128, NB, E])

            def routing(k, part):
                at = [(0, 3, 12, 17)[part]]

                def step(ins):
                    ins.then_inc(route.sem, 1)
                    dve.wait_ge(route.sem, route.nth(k, at[0]))
                    at[0] += 1

                shifted, expd, t0, k1, l2, k2, t1, first = (grid(rt[:, i, :]) for i in range(1, 9))
                rev = grid(cst[:, C_REV:C_REV + NB * E])
                m1, i1, m2, i2, z, d, th, g1, g2, rz, e2 = (r4[:, i, :] for i in (0, 1, 2, 3, 4, 5, 6, 7, 8, 9, 10))
                if part == 0:
                    dve.wait_ge(logit_turned.sem, logit_turned.nth(k))
                    if later(k):
                        dve.wait_ge(gate_turned.sem, gate_turned.nth(k - 1))
                    step(dve.tensor_tensor(rt[:, 0, :], M[1][:, 0:NB * E], bias_r[:, :], ALU.add))
                    step(dve.reduce_max(m1, grid(rt[:, 0, :]), AX.X))
                    step(dve.tensor_tensor(shifted, grid(rt[:, 0, :]), over(m1), ALU.subtract))
                elif part == 1:
                    step(dve.scalar_tensor_tensor(out=rt[:, 3, :], in0=rt[:, 1, :], scalar=0.0, in1=cst[:, C_REV:C_REV + NB * E], op0=ALU.is_ge, op1=ALU.mult))
                    step(dve.reduce_max(i1, t0, AX.X))
                    step(dve.tensor_tensor(k1, rev, over(i1), ALU.is_equal))
                    step(dve.scalar_tensor_tensor(out=rt[:, 5, :], in0=rt[:, 4, :], scalar=-3e38, in1=rt[:, 1, :], op0=ALU.mult, op1=ALU.add))
                    step(dve.reduce_max(m2, l2, AX.X))
                    step(dve.tensor_tensor(t0, l2, over(m2), ALU.is_equal))
                    step(dve.tensor_tensor(t0, t0, rev, ALU.mult))
                    step(dve.reduce_max(i2, t0, AX.X))
                    step(dve.tensor_tensor(k2, rev, over(i2), ALU.is_equal))
                elif part == 2:
                    dve.wait_ge(route_exp.sem, route_exp.nth(k))
                    step(dve.reduce_sum(z, expd, AX.X))
                    step(dve.reciprocal(rz, z))
                    step(dve.tensor_tensor(t1, expd, k2, ALU.mult))
                    step(dve.reduce_sum(e2, t1, AX.X))
                    step(dve.scalar_tensor_tensor(out=d, in0=e2, scalar=-1.0, in1=rz, op0=ALU.add, op1=ALU.mult))
                else:
                    dve.wait_ge(route_tanh.sem, route_tanh.nth(k))
                    step(dve.tensor_scalar(g1, th, 0.5, 0.5, ALU.mult, ALU.add))
                    step(dve.tensor_scalar(g2, th, -0.5, 0.5, ALU.mult, ALU.add))
                    step(dve.tensor_tensor(k1, k1, over(g1), ALU.mult))
                    step(dve.tensor_tensor(k2, k2, over(g2), ALU.mult))
                    step(dve.tensor_tensor(rt[:, 8, :].rearrange("p (e b) -> p b e", b=NB), k1, k2, ALU.add))

            def h_low(k):
                dve.wait_ge(h_act.sem, h_act.nth(k))
                dve.tensor_tensor(sl3[:], h_raw[:], sh[:, 3, :].bitcast(f32), ALU.subtract).then_inc(h_lo.sem, 1)

            def split_g1(k, c):
                dve.wait_ge(g1_act.sem, g1_act.nth(k, c))
                if later(k):
                    dve.wait_ge(attn_out.sem, attn_out.nth(k - 1, 1))
                else:
                    dve.wait_ge(piece_lo.sem, piece_lo.nth(SLOTS - 1))
                dve.tensor_copy(mid_h[:, c, :], ac[:, 5 + c, :]).then_inc(g1_hi.sem, 1)
                dve.wait_ge(g1_hi.sem, g1_hi.nth(k, c))
                dve.tensor_tensor(mid_l[:, c, :], ac[:, 5 + c, :], mid_h[:, c, :].bitcast(f32), ALU.subtract).then_inc(g1_lo.sem, 1)

            def hidden_high(k, t):
                dve.wait_ge(hid_act.sem, hid_act.nth(k, t))
                if t < 3:
                    if later(k):
                        dve.wait_ge(ff_used.sem, ff_used.nth(k - 1, FT - 1))
                else:
                    dve.wait_ge(hid_used.sem, hid_used.nth(k, t - 3))
                dve.tensor_copy(sh[:, t % 3, :], hid[:, t % 3, :]).then_inc(hid_hi.sem, 1)

            def combine(k, o):
                dve.wait_ge(hid_used.sem, hid_used.nth(k, last_tile(o)))
                if o == 0:
                    if later(k):
                        dve.wait_ge(den_z.sem, den_z.nth(k - 1))
                    dve.tensor_scalar(ac[:, 4, :], R[3][:], 0.1, s2b[:, 0:1], ALU.mult, ALU.add).then_inc(combined.sem, 1)
                    return
                e = o - 1
                dve.wait_ge(row_loaded[e % 2].sem, row_loaded[e % 2].nth(k, e // 2))
                if o > 1:
                    dve.wait_ge(summed.sem, summed.nth(k, e - 1))
                else:
                    if later(k):
                        dve.wait_ge(out_stored.sem, out_stored.nth(k - 1))
                    dve.wait_ge(gates_stored.sem, gates_stored.nth(k))
                    dve.wait_ge(combined.sem, combined.nth(k))
                dve.scalar_tensor_tensor(out=hid[:, 4, :], in0=R[3 + o % 3][:], scalar=idle[:, e:e + 1], in1=gate[:, e % 2, :],
                                         op0=ALU.subtract, op1=ALU.mult).then_inc(combined.sem, 1)
                dve.wait_ge(combined.sem, combined.nth(k, o))
                so_far = ac[:, 4, :] if o == 1 else hid[:, 3, :]
                dve.tensor_tensor(hid[:, 3, :], so_far, hid[:, 4, :], ALU.add).then_inc(summed.sem, 1)

            def mixture(k):
                dve.wait_ge(summed.sem, summed.nth(k, E - 1))
                dve.wait_ge(hid_z.sem, hid_z.nth(k, NT - 1))
                dve.tensor_scalar(sh[:, 3, :], hid[:, 3, :], idle_sum[:, 0:1], None, ALU.add).then_inc(m_hi.sem, 1)
                dve.wait_ge(m_hi.sem, m_hi.nth(k))
                dve.scalar_tensor_tensor(out=sl3[:], in0=hid[:, 3, :], scalar=idle_sum[:, 0:1], in1=sh[:, 3, :].bitcast(f32),
                                         op0=ALU.add, op1=ALU.subtract).then_inc(m_lo.sem, 1)

            def flat2(t, i):
                return t[:, 2 * i:2 * i + 2, :].rearrange("p b n -> p (b n)")

            def x2_stats(k):
                for i in range(2):
                    dve.wait_ge(moe_out.sem, moe_out.nth(k, i))
                    dve.wait_ge(resid1.sem, resid1.nth(k, i))
                    dve.tensor_tensor(flat2(tok, i), M[i][:], flat2(tok, i), ALU.add).then_inc(y2_ready.sem, 1)
                stats(1, k, lambda b: tok[:, b, :], lambda b: dve.wait_ge(y2_ready.sem, y2_ready.nth(k, b // 2)))

            def x2_low(k):
                for c in range(CT):
                    dve.wait_ge(x2_hi.sem, x2_hi.nth(k, c))
                    dve.tensor_tensor(mid_l[:, c, :], M[c][:], mid_h[:, c, :].bitcast(f32), ALU.subtract).then_inc(x2_lo.sem, 1)

            def elu1(k, c, exp, low, phi, slot):
                dve.wait_ge(exp.sem, exp.nth(k, c))
                dve.tensor_scalar(ac[:, slot, :], ac[:, slot, :], 1.0, None, ALU.min).then_inc(low.sem, 1)
                dve.wait_ge(low.sem, low.nth(k, c))
                dve.scalar_tensor_tensor(out=ac[:, slot, :], in0=M[0][:], scalar=0.0, in1=ac[:, slot, :], op0=ALU.max, op1=ALU.add)\
                    .then_inc(phi.sem, 1)

            def keys(k, c):
                elu1(k, c, k_exp, k_min, k_phi, 0)

            def key_scans(k, c):
                dve.wait_ge(k_phi.sem, k_phi.nth(k, c))
                dve.wait_ge(v_z.sem, v_z.nth(k, c))
                dve.tensor_tensor(ac[:, 1, :], M[1][:], ac[:, 0, :], ALU.mult).then_inc(kv_ready.sem, 1)
                dve.wait_ge(kv_ready.sem, kv_ready.nth(k, c))
                for what, dst in ((0, 3 + c), (1, 5 + c)):
                    for s in range(CHUNK // SEQ):
                        at = slice(s * SEQ, (s + 1) * SEQ)
                        dve.tensor_tensor_scan(ac[:, dst, at], decay[:, c:c + 1].broadcast_to([128, SEQ]), ac[:, what, at], 0.0,
                                               ALU.mult, ALU.add).then_inc(scanned.sem, 1)

            def queries(k, c):
                elu1(k, c, q_exp, q_min, q_phi, 2)

            def inverses(k):
                dve.wait_ge(den_turned.sem, den_turned.nth(k))
                dve.tensor_scalar(rden[:, :], M[1][:, 0:NB * HEADS], 1e-6, None, ALU.max).then_inc(den_max.sem, 1)
                dve.wait_ge(den_max.sem, den_max.nth(k))
                dve.reciprocal(rden[:, :], rden[:, :]).then_inc(den_inv.sem, 1)

            def attention(k):
                for c in range(CT):
                    dve.wait_ge(inv_turned.sem, inv_turned.nth(k, c))
                    dve.wait_ge(num_ready.sem, num_ready.nth(k, c))
                    dve.tensor_tensor(ac[:, 5 + c, :], M[c][:], ac[:, 5 + c, :], ALU.mult).then_inc(o_ready.sem, 1)
                for c in range(CT):
                    dve.wait_ge(o_hi.sem, o_hi.nth(k, c))
                    dve.tensor_tensor(mid_l[:, c, :], ac[:, 5 + c, :], mid_h[:, c, :].bitcast(f32), ALU.subtract).then_inc(o_lo.sem, 1)

            def x3_sum(k):
                if isinstance(k, int) and k == 0:
                    dve.wait_ge(piece_lo.sem, piece_lo.nth(PIECES - 1))
                for i in range(2):
                    dve.wait_ge(attn_out.sem, attn_out.nth(k, i))
                    dve.wait_ge(y4_ready.sem, y4_ready.nth(k, 1))
                    dve.tensor_tensor(flat2(tok3, i), M[i][:], flat2(tok, i), ALU.add).then_inc(y3_ready.sem, 1)

            def x3_stats(k, half):
                stats(2, k, lambda b: tok3[:, b, :], lambda b: dve.wait_ge(y3_ready.sem, y3_ready.nth(k, b // 2)), (half,))

            def x3_low(k):
                for c in range(CT):
                    dve.wait_ge(x3_hi.sem, x3_hi.nth(k, c))
                    dve.tensor_tensor(ffn_l[:, c, :], M[c][:], ffn_h[:, c, :].bitcast(f32), ALU.subtract).then_inc(x3_lo.sem, 1)

            def ffn(r, j, tail=False):
                dve.wait_ge(ff_tanh.sem, ff_tanh.nth(r, j))
                p = 2 * (j % 2)
                h = hid[:, j % 3, :]
                dve.scalar_tensor_tensor(out=h, in0=h, scalar=1.0, in1=R[p][:], op0=ALU.add, op1=ALU.mult).then_inc(ff_silu.sem, 1)
                dve.wait_ge(ff_silu.sem, ff_silu.nth(r, j))
                dve.tensor_tensor(h, R[p + 1][:], h, ALU.mult).then_inc(ff_hid.sem, 1)
                dve.wait_ge(ff_hid.sem, ff_hid.nth(r, j))
                if j < 3 and not tail:
                    dve.wait_ge(hid_used.sem, hid_used.nth(r, NT - 1))
                dve.wait_ge(ff_used.sem, ff_used.nth(r, j - 3))
                dve.tensor_copy(sh[:, j % 3, :], h).then_inc(ff_hi.sem, 1)

            y4 = hid[:, 3:5, :].rearrange("p a (b n) -> p (a b) n", n=D)

            def out_sum(r, tail=False):
                for i in range(2):
                    dve.wait_ge(ff_used.sem, ff_used.nth(r, FT - 1))
                    if tail:
                        if later(r):
                            dve.wait_ge(out_stored.sem, out_stored.nth(r - 1))
                    else:
                        dve.wait_ge(m_lo.sem, m_lo.nth(r))
                        if more_chunks(r):
                            dve.wait_ge(logit_turned.sem, logit_turned.nth(r + 1))
                            dve.wait_ge(gates_stored.sem, gates_stored.nth(r + 1))
                    dve.tensor_tensor(hid[:, 3 + i, :], R[4 + i][:], flat2(tok3, i), ALU.add).then_inc(y4_ready.sem, 1)

            def out_stats(r, half):
                stats(3, r - 1, lambda b: y4[:, b, :], lambda b: dve.wait_ge(y4_ready.sem, y4_ready.nth(r, b // 2)), (half,))

            def had_combine(j):
                s, second = 1 << (j // 2), j % 2
                v = w2_raw[:].rearrange("p (g two m) -> p g two m", two=2, m=s * D)
                a, b = v[:, :, 0, :], v[:, :, 1, :]
                if j == 0:
                    dve.wait_ge(w2_loaded.sem, 16)
                else:
                    dve.wait_ge(had_step.sem, had_step.nth(j - 1))
                if second:
                    dve.scalar_tensor_tensor(out=a, in0=a, scalar=2.0, in1=b, op0=ALU.mult, op1=ALU.subtract).then_inc(had_step.sem, 1)
                else:
                    dve.tensor_tensor(b, a, b, ALU.subtract).then_inc(had_step.sem, 1)

            def had_low(q):
                dve.wait_ge(had_hi.sem, had_hi.nth(q))
                c = W2 + q * PIECE
                dve.tensor_tensor(wl[:, c:c + PIECE], R[q][:], wh[:, c:c + PIECE].bitcast(f32), ALU.subtract).then_inc(had_lo.sem, 1)

            flat = hid[:].rearrange("p a n -> p (a n)")

            def experts(r):
                more = more_chunks(r)
                done = 1
                if later(r):
                    x3_low(r - 1)
                for t in range(AHEAD, NT + LAG):
                    if t < NT:
                        hidden_high(r, t)
                    if t in (6, 7) and more:
                        x_low(r + 1, t - 6)
                    if t in (9, 10):
                        split_g1(r, t - 9)
                    if t in (ROOT_TILE - 1, ROOT_TILE) and more:
                        roots(r + 1, t - ROOT_TILE + 1)
                        cut_decay(r + 1, t - ROOT_TILE + 1)
                    if t >= SUMS_TILE and done <= E and last_tile(done) <= t - LAG - 1:
                        combine(r, done)
                        done += 1
                    if more:
                        if t in (GATE_TILES[0] + 1, GATE_TILES[1] + 1):
                            gated_input(r + 1, (t - GATE_TILES[0]) // 2)
                        if t in (17, 18):
                            step_input(r + 1, t - 17)
                        if t in (19, 20):
                            states(r + 1, t - 19)
                        if t in (21, 22):
                            add_x(r + 1, t - 21)
                while done <= E:
                    combine(r, done)
                    done += 1
                mixture(r)

            def rest(r, has_ffn):
                more = more_chunks(r)

                def ff(j):
                    if has_ffn:
                        ffn(r, j)
                    elif j < W2_PIECES:
                        had_low(j)
                    elif j == FT - 1:
                        dve.sem_inc(ff_silu.sem, FT)
                        dve.sem_inc(ff_hid.sem, FT)
                        dve.sem_inc(ff_hi.sem, FT)
                ff(0)
                x2_stats(r)
                ff(1)
                if more:
                    x1_stats(r + 1)
                x2_low(r)
                ff(2)
                ff(3)
                if more:
                    x1_low(r + 1)
                ff(4)
                keys(r, 0)
                key_scans(r, 0)
                ff(5)
                queries(r, 0)
                if more:
                    routing(r + 1, 0)
                keys(r, 1)
                key_scans(r, 1)
                queries(r, 1)
                if more:
                    routing(r + 1, 1)
                ff(6)
                if more:
                    routing(r + 1, 2)
                inverses(r)
                if more:
                    routing(r + 1, 3)
                ff(7)
                attention(r)
                if has_ffn:
                    out_sum(r)
                else:
                    dve.sem_inc(y4_ready.sem, 2)
                if more:
                    h_low(r + 1)
                x3_sum(r)
                if more:
                    hidden_high(r + 1, 0)
                x3_stats(r, 0)
                if more:
                    hidden_high(r + 1, 1)
                x3_stats(r, 1)
                if more:
                    hidden_high(r + 1, 2)
                if has_ffn:
                    out_stats(r, 0)
                if more:
                    hidden_high(r + 1, 3)
                if has_ffn:
                    out_stats(r, 1)
                if more:
                    hidden_high(r + 1, 4)
                    residual1(r + 1, 0)
                    combine(r + 1, 0)
                    hidden_high(r + 1, 5)
                    residual1(r + 1, 1)

            n = [0]

            def link(ins):
                ins.then_inc(setup_dve.sem, 1)
                dve.wait_ge(setup_dve.sem, setup_dve.nth(n[0]))
                n[0] += 1
                return n[0] - 1

            link(dve.memset(neg_half[:, :], -0.5))
            dve.wait_ge(vec_loaded.sem, 16)
            link(dve.tensor_scalar(half_b[:, :], vec[:, V_BA:V_BA + 2 * CT], 0.5, None, ALU.mult))
            dve.wait_ge(w0_loaded.sem, 16)
            dve.tensor_copy(wh[:, 0:DOWN], flat[:, 0:DOWN]).then_inc(dense_hi.sem, 1)
            dve.wait_ge(x_loaded.sem, x_loaded.nth(0))
            for c in range(CT):
                dve.tensor_copy(chan_h[:, c, :], xy[:, c, :]).then_inc(x_hi.sem, 1)
            dve.wait_ge(dense_hi.sem, dense_hi.nth(0))
            dve.tensor_tensor(wl[:, 0:DOWN], flat[:, 0:DOWN], wh[:, 0:DOWN].bitcast(f32), ALU.subtract).then_inc(dense_lo.sem, 1)
            x_low(0, 0)
            x_low(0, 1)
            dve.wait_ge(setup_act.sem, setup_act.nth(1))
            e_, ratio, sq, acc = ser[:, 1, :], ser[:, 2, :], ser[:, 3, :], ser[:, 4, :]
            link(dve.tensor_scalar(ratio, e_, 2.0, None, ALU.add))
            link(dve.reciprocal(ratio, ratio))
            link(dve.tensor_tensor(ratio, ratio, e_, ALU.mult))
            link(dve.tensor_tensor(sq, ratio, ratio, ALU.mult))
            link(dve.tensor_scalar(acc, sq, 1.0 / 17, None, ALU.mult))
            for d in (15, 13, 11, 9, 7, 5, 3):
                link(dve.scalar_tensor_tensor(out=acc, in0=acc, scalar=1.0 / d, in1=sq, op0=ALU.add, op1=ALU.mult))
            link(dve.scalar_tensor_tensor(out=acc, in0=acc, scalar=1.0, in1=ratio, op0=ALU.add, op1=ALU.mult))
            link(dve.tensor_scalar(sq, vec[:, V_LAM:V_LAM + CT], -1.0, 0.0, ALU.mult, ALU.max))
            link(dve.scalar_tensor_tensor(out=sq, in0=acc, scalar=2.0, in1=sq, op0=ALU.mult, op1=ALU.add))
            link(dve.tensor_scalar(c2[:, :], sq, -4.0, None, ALU.mult))
            link(dve.tensor_scalar(nc2[:, :], sq, 4.0, None, ALU.mult))
            assert link(dve.tensor_scalar(s2b[:, :], vec[:, V_S2:V_S2 + 1], 0.1, None, ALU.mult)) == SET_C2
            dve.wait_ge(setup_act.sem, setup_act.nth(2))
            link(dve.tensor_scalar(decay[:, :], decay[:, :], 0.5, 0.5, ALU.mult, ALU.add))
            dve.wait_ge(rows_loaded.sem, 16)
            dve.wait_ge(small_loaded.sem, 16)
            rw = ac[:, 0:2, :].rearrange("p a n -> p (a n)")
            link(dve.tensor_tensor(bias_uc[:, :], rw[:, 0:D], rw[:, D:2 * D], ALU.add))
            assert link(dve.tensor_tensor(bias_r[:, :], rw[:, 2 * D:2 * D + NB * E], cst[:, C_COST:C_COST + NB * E], ALU.subtract)) == SET_ROWS
            gated_input(0, 0)
            had_combine(0)
            had_combine(1)
            gated_input(0, 1)
            for c in range(CT):
                roots(0, c)
                cut_decay(0, c)
            for c in range(CT):
                step_input(0, c)
                states(0, c)
                add_x(0, c)
            dve.wait_ge(dense_hi.sem, dense_hi.nth(1))
            dve.tensor_tensor(wl[:, DOWN:EXPERTS], flat[:, DOWN:EXPERTS], wh[:, DOWN:EXPERTS].bitcast(f32), ALU.subtract).then_inc(dense_lo.sem, 1)
            dve.wait_ge(setup_act.sem, setup_act.nth(3))
            link(dve.tensor_copy(b1s[:, :, 0], b1g[:, :]))
            assert link(dve.tensor_tensor(b1s[:, :, 1], b1g[:, :], b1s[:, :, 0].bitcast(f32), ALU.subtract)) == IDLE_SPLIT
            x1_stats(0)
            for j in range(2, 2 * HAD_STEPS):
                had_combine(j)
            x1_low(0)
            h_low(0)
            routing(0, 0)
            hidden_high(0, 0)
            hidden_high(0, 1)
            routing(0, 1)
            dve.wait_ge(idle_z.sem, idle_z.nth(0, 1))
            assert link(dve.tensor_copy(idle2[:, :], R[5][:, 0:2 * E])) == IDLE_COPIED
            parts = idle2[:, :].rearrange("p (e two) -> p e two", two=2)
            link(dve.tensor_tensor(idle[:, :], parts[:, :, 0], parts[:, :, 1], ALU.add))
            link(dve.reduce_sum(idle_sum[:, 0:1], idle[:, :], AX.X))
            link(dve.reduce_sum(idle_sum[:, 1:2], vec[:, V_E2:V_E2 + E], AX.X))
            link(dve.tensor_tensor(idle_sum[:, 0:1], idle_sum[:, 0:1], idle_sum[:, 1:2], ALU.add))
            hidden_high(0, 2)
            routing(0, 2)
            hidden_high(0, 3)
            routing(0, 3)
            hidden_high(0, 4)
            combine(0, 0)
            hidden_high(0, 5)
            dve.wait_ge(piece_lo.sem, piece_lo.nth(SLOTS - 1))
            residual1(0, 0)
            residual1(0, 1)
            experts(0)
            rest(0, False)
            with dve.Fori(1, chunks - 1) as r:
                experts(r)
                rest(r, True)
            experts(chunks - 1)
            rest(chunks - 1, True)
            x3_low(chunks - 1)
            for j in range(FT):
                ffn(chunks, j, tail=True)
            out_sum(chunks, tail=True)
            out_stats(chunks, 0)
            out_stats(chunks, 1)

        @block.gpsimd
        def _(pool):
            def rstd(i, k):
                pool.wait_ge(ln_var[i].sem, ln_var[i].nth(k, 1))
                pool.tensor_tensor(rs[i][:, 1, :], rs[i][:, 0, :], neg_half[:, :], ALU.pow).then_inc(ln_rstd[i].sem, 1)
                pool.wait_ge(ln_rstd[i].sem, ln_rstd[i].nth(k))
                pool.tensor_tensor(rs[i][:, 3, :], rs[i][:, 1, :], rs[i][:, 2, :], ALU.mult).then_inc(ln_shift[i].sem, 1)

            gate_tok = gate[:].rearrange("p a (b n) -> p (a b) n", n=D)

            def x1_whole(k):
                pool.wait_ge(x1_lo.sem, x1_lo.nth(k, CT - 1))
                if later(k):
                    pool.wait_ge(o_lo.sem, o_lo.nth(k - 1, CT - 1))
                pool.wait_ge(y_ready.sem, y_ready.nth(k, CT - 1))
                pool.tensor_tensor(ac[:, 5:7, :], chan_h[:].bitcast(f32), chan_l[:].bitcast(f32), ALU.add).then_inc(x1_sum.sem, 1)

            def hidden_low(k, t):
                pool.wait_ge(hid_hi.sem, hid_hi.nth(k, t))
                pool.tensor_tensor(sl[:, t % 3, :], hid[:, t % 3, :], sh[:, t % 3, :].bitcast(f32), ALU.subtract).then_inc(hid_lo.sem, 1)

            def ffn_low(r, j):
                pool.wait_ge(ff_hi.sem, ff_hi.nth(r, j))
                pool.tensor_tensor(sl[:, j % 3, :], hid[:, j % 3, :], sh[:, j % 3, :].bitcast(f32), ALU.subtract).then_inc(ff_lo.sem, 1)

            def numerators(k, c):
                pool.wait_ge(q_phi.sem, q_phi.nth(k, c))
                pool.wait_ge(scanned.sem, scanned.nth(k, 4 * c + 3))
                pool.tensor_tensor(ac[:, 3 + c, :], ac[:, 2, :], ac[:, 3 + c, :], ALU.mult).then_inc(qk_ready.sem, 1)
                pool.tensor_tensor(ac[:, 5 + c, :], ac[:, 2, :], ac[:, 5 + c, :], ALU.mult).then_inc(num_ready.sem, 1)

            def weights_low(m):
                pool.wait_ge(piece_hi.sem, piece_hi.nth(m))
                c = EXPERTS + m * PIECE
                pool.tensor_tensor(wl[:, c:c + PIECE], raw_piece(m), wh[:, c:c + PIECE].bitcast(f32), ALU.subtract).then_inc(piece_lo.sem, 1)

            def experts(r):
                for t in range(AHEAD, NT):
                    hidden_low(r, t)

            def rest(r, has_ffn):
                more = more_chunks(r)

                def ff(j):
                    if has_ffn:
                        ffn_low(r, j)
                    else:
                        weights_low(EARLY + j)
                        if j == FT - 1:
                            pool.sem_inc(ff_lo.sem, FT)
                ff(0)
                rstd(1, r)
                if more:
                    rstd(0, r + 1)
                ff(1)
                ff(2)
                ff(3)
                ff(4)
                ff(5)
                numerators(r, 0)
                numerators(r, 1)
                ff(6)
                ff(7)
                if more:
                    x1_whole(r + 1)
                    hidden_low(r + 1, 0)
                    hidden_low(r + 1, 1)
                rstd(2, r)
                if more:
                    hidden_low(r + 1, 2)
                    hidden_low(r + 1, 3)
                if has_ffn:
                    rstd(3, r - 1)
                if more:
                    hidden_low(r + 1, 4)
                    hidden_low(r + 1, 5)

            for m in range(10):
                weights_low(m)
            rstd(0, 0)
            weights_low(10)
            weights_low(11)
            x1_whole(0)
            for t in range(AHEAD):
                hidden_low(0, t)
            weights_low(12)
            weights_low(13)
            experts(0)
            rest(0, False)
            with pool.Fori(1, chunks - 1) as r:
                experts(r)
                rest(r, True)
            experts(chunks - 1)
            rest(chunks - 1, True)
            for j in range(FT):
                ffn_low(chunks, j)
            rstd(3, chunks - 1)


SET_C2 = 19
SET_ROWS = 22
IDLE_SPLIT = 24
IDLE_COPIED = 25


def kernel(**inputs):
    import numpy as np
    import concourse.bacc as bacc
    from concourse import mybir
    from concourse.bass_utils import run_bass_kernel_spmd as run

    g = {n: np.asarray(a) for n, a in inputs.items()}
    x = g["L0_attn_x"]
    batch, seq, d = x.shape

    def rows_first(a):
        k, n = a.shape
        return a.reshape(k // 128, 128, n).transpose(1, 0, 2).reshape(128, -1)

    parts = [g["L0_attn_Wa"].T, g["L0_attn_Wx"].T, g["L0_ffn_down_w"], g["L0_ffn_router_w"], g["L0_ffn_shared_w1"],
             g["L0_ffn_shared_w2"], g["L0_ffn_core_w"], g["L0_ffn_up_w"]]
    for e in range(E):
        parts += [g[f"L0_ffn_e{e}_w1"], g[f"L0_ffn_e{e}_w2"]]
    parts += [g["L1_attn_w_qkv"], g["L1_attn_w_out"], g["L1_ffn_W1"].T, g["L1_ffn_W3"].T, g["L1_ffn_W2"].T]
    weights = np.concatenate([rows_first(a) for a in parts], axis=1)

    cols = [g["L0_attn_ba"], g["L0_attn_bx"], g["L0_attn_Lam"], g["L0_ffn_down_b"], g["L0_ffn_shared_b1"], g["L0_ffn_shared_b2"]]
    cols += [g[f"L0_ffn_e{e}_b1"] for e in range(E)] + [g[f"L0_ffn_e{e}_b2"] for e in range(E)]
    cols += [np.repeat(g["L1_attn_decay_param"], HEAD)]
    vectors = np.concatenate([a.reshape(-1, 128).T for a in cols], axis=1)
    rows = np.concatenate([g["L0_ffn_up_b"], g["L0_ffn_core_b"], np.tile(g["L0_ffn_router_b"], NB)])

    had = np.array([[1.0]])
    while had.shape[0] < 128:
        had = np.block([[had, had], [had, -had]])
    head = np.zeros((128, CT, HEADS))
    for p in range(128):
        for c in range(CT):
            head[p, c, (c * 128 + p) // HEAD] = 1.0
    consts = np.concatenate([np.eye(128), had / (2 * FF ** 0.5), head.reshape(128, -1),
                             np.tile(np.arange(E, 0, -1.0), (128, NB)), np.tile(np.array(COST), (128, NB))], axis=1).astype(np.float32)

    arrays = {"x_t": x.reshape(batch * seq, d).T, "weights": weights, "vectors": vectors, "rows": rows, "consts": consts}
    arrays = {n: np.ascontiguousarray(a) for n, a in arrays.items()}
    nc = bacc.Bacc("TRN2", target_bir_lowering=False, num_devices=1)
    aps = [nc.dram_tensor("in_" + n, a.shape, mybir.dt.from_np(a.dtype), kind="ExternalInput").ap() for n, a in arrays.items()]
    out = nc.dram_tensor("out", (batch * seq, d), mybir.dt.float32, kind="ExternalOutput").ap()
    program(nc, *aps, out)
    r = run(nc, [{"in_" + n: a for n, a in arrays.items()}], core_ids=[0])
    return r.results[0]["out"].reshape(batch, seq, d)
```

```python
import concourse.bass as bass
from concourse import mybir
from contextlib import ExitStack

HID = [128, 256, 384, 512, 128, 256, 384, 512]
E = len(HID)
D = 256
L = 128
FF = 1024
SEQ = 256
CHUNK = 512
CT = D // 128
NB = CHUNK // 128
HALF = CHUNK // 2
HEADS, HEAD = 16, 16
FT = FF // 128
TILES = [(-1, 0)] + [(e, j) for e in range(E) for j in range(HID[e] // 128)]
NT = len(TILES)
AHEAD = 6
LAG = 3
X3_TILE = 6
GATE_TILES = (9, 11)
CORE_TILES = (13, 18)
GATES_TURN = 5
EXP_TILE = 12
PARTS_TILES = (13, 14)
ROOT_TILE = 15
SUMS_TILE = 8
G1_TILES = (8, 9)
INPUT_TILES = (10, 12)
ROOT_TILES = (14, 15)
STEP_TILES = (17, 18)
STATE_TILES = (19, 20)
Y_TILES = (21, 22)
X3_STEP = 4
OUT_NORM_STEP = 2
OUT_DVE = 10
OUT_POOL = 11
OUT_ACT = 13
HAD_STEPS = 3
EPS = 1e-5
COST = [1e-7 * 2 * L * h for h in HID]

_at = 0


def _cols(n):
    global _at
    _at += n
    return _at - n


WA = _cols(CT * D)
WX = _cols(CT * D)
DOWN = _cols(CT * L)
ROUTER = _cols(CT * E)
SW1 = _cols(L)
SW2 = _cols(L)
CORE = _cols(CT * D)
UP = _cols(D)
EXPERTS = _at
EW1, EW2 = [], []
for _h in HID:
    EW1.append(_cols(_h))
    EW2.append(_cols(_h))
QKV = _cols(CT * 3 * D)
WOUT = _cols(CT * D)
W1 = _cols(CT * FF)
W3 = _cols(CT * FF)
W2 = _cols(FT * D)
WCOLS = _at
PIECE = 512
PIECES = (W2 - EXPERTS) // PIECE
EARLY = (W1 - EXPERTS) // PIECE
W2_PIECES = FT * D // PIECE
SLOTS = 8

V_BA, V_BX, V_LAM, V_DOWN, V_S1, V_S2, V_E1, V_E2, V_DEC = 0, 2, 4, 6, 7, 8, 9, 9 + NT - 1, 9 + NT - 1 + E
VCOLS = V_DEC + CT
C_ID, C_HAD, C_HEAD, C_REV, C_COST = 0, 128, 256, 256 + CT * HEADS, 256 + CT * HEADS + NB * E
CCOLS = C_COST + NB * E


def program(nc, x_in, weights, vectors, rows, consts, out):
    f32, f32r = mybir.dt.float32, mybir.dt.float32r
    ALU, ACT, AX = mybir.AluOpType, mybir.ActivationFunctionType, mybir.AxisListType
    chunks = x_in.shape[1] // CHUNK
    LAST = chunks - 1
    x_chunks = x_in.rearrange("(c p) (k t) -> k p c t", p=128, t=CHUNK)
    out_chunks = out.rearrange("(k b p) n -> k p b n", b=NB, p=128)
    gates_dram = nc.dram_tensor("gates_scratch", (chunks, E, CHUNK), f32, kind="Internal").ap()

    with ExitStack() as ctx:
        def sb(name, shape, dt=f32):
            return ctx.enter_context(nc.sbuf_tensor(name, shape, dt))

        def before(name, shape):
            with nc.sbuf_tensor(name, shape, f32) as t:
                return t

        wh = sb("weights_hi", [128, WCOLS], f32r)
        wl = sb("weights_lo", [128, WCOLS], f32r)
        xy = sb("x_then_y", [128, CT, CHUNK])
        chan_h = sb("chan_hi", [128, CT, CHUNK], f32r)
        chan_l = sb("chan_lo", [128, CT, CHUNK], f32r)
        mid_raw = before("mid_raw", [128, 2 * CT, CHUNK])
        mid_h = sb("mid_hi", [128, CT, CHUNK], f32r)
        mid_l = sb("mid_lo", [128, CT, CHUNK], f32r)
        w2_raw = before("w2_raw", [128, FT * D])
        ffn_h = sb("ffn_hi", [128, CT, CHUNK], f32r)
        ffn_l = sb("ffn_lo", [128, CT, CHUNK], f32r)
        tok = sb("tok", [128, NB, D])
        tok3 = sb("tok3", [128, NB, D])
        gate = sb("gate_rows", [128, 2, CHUNK])
        ac = sb("gate_attn_work", [128, 7, CHUNK])
        hid = sb("hidden", [128, 5, CHUNK])
        sh = sb("hidden_hi", [128, 4, CHUNK], f32r)
        sl = sb("hidden_lo", [128, 3, CHUNK], f32r)
        h_raw = before("h_raw", [128, CHUNK])
        sl3 = sb("input_lo", [128, CHUNK], f32r)
        cst = sb("consts", [128, CCOLS])
        vec = sb("vectors", [128, VCOLS])
        bias_uc = sb("bias_up_core", [128, D])
        bias_r = sb("bias_router", [128, NB * E])
        half_b = sb("half_gate_bias", [128, 2 * CT])
        c2 = sb("half_log_decay", [128, CT])
        nc2 = sb("neg_half_log_decay", [128, CT])
        ser = sb("softplus_work", [128, 5, CT])
        s2b = sb("shared_bias_tenth", [128, 1])
        decay = sb("attn_decay", [128, CT])
        b1g = sb("gelu_of_bias", [128, NT - 1])
        b1s = sb("gelu_of_bias_split", [128, NT - 1, 2], f32r)
        idle2 = sb("idle_parts", [128, 2 * E])
        idle = sb("idle_expert", [128, E])
        idle_sum = sb("idle_sum", [128, 2])
        neg_half = sb("neg_half", [128, NB])
        rt = sb("routing", [128, 9, NB * E])
        r4 = sb("routing_per_token", [128, 12, NB])
        gate_tok = gate[:].rearrange("p a (b n) -> p (a b) n", n=D)
        y4 = hid[:, 3:5, :].rearrange("p a (b n) -> p (a b) n", n=D)
        dense_raw = hid[:].rearrange("p a n -> p (a n)")
        gt = hid[0:NB * E, 3, 0:128]
        lg = hid[0:E, 4, :]
        rden = sb("denominators", [128, NB * HEADS])
        st = [sb(f"ln{i}_stats", [128, NB, 6]) for i in range(4)]
        mv = [sb(f"ln{i}_mean_var", [128, NB, 2]) for i in range(4)]
        rs = [sb(f"ln{i}_rstd", [128, 4, NB]) for i in range(4)]
        ident = cst[:, C_ID:C_ID + 128]
        R = [ctx.enter_context(nc.psum_tensor(f"R{i}", [128, CHUNK], f32)) for i in range(6)]
        M = [ctx.enter_context(nc.psum_tensor(f"M{i}", [128, CHUNK], f32)) for i in range(2)]

        class Signal:

            def __init__(self, name, per=1, by=1):
                self.sem, self.per, self.by = ctx.enter_context(nc.semaphore(name)), per, by

            def nth(self, k, i=0):
                return (k * self.per + i + 1) * self.by

        def later(k):
            return not isinstance(k, int) or k > 0

        def more_chunks(k):
            return not isinstance(k, int) or k < LAST

        wait_carried = Signal("wait_carried")

        def apart(eng):
            eng.sem_inc(wait_carried.sem, 1)

        S = Signal
        x_loaded, gates_stored = S("x_loaded", 1, 16), S("gates_stored", 1, 16)
        row_loaded = [S(f"gate_row_loaded{i}", E // 2, 16) for i in range(2)]
        out_stored = S("out_stored", 1, 16)
        small_loaded, w0_loaded, w1_loaded = S("small_loaded", 1, 16), S("w_gates_loaded", 1, 16), S("w_dense_loaded", 1, 16)
        rows_loaded, vec_loaded = S("rows_loaded", 1, 16), S("vec_loaded", 1, 16)
        piece_loaded = [S(f"piece_loaded{i}", 1, 16) for i in range(SLOTS)]
        w2_loaded = S("w2_loaded", 1, 16)
        dense_hi, dense_lo = S("dense_hi"), S("dense_lo")
        piece_hi, piece_lo = S("piece_hi"), S("piece_lo")
        had_step, had_z, had_hi, had_lo = S("had_step"), S("had_z"), S("had_hi"), S("had_lo")
        setup_act, setup_dve, idle_z = S("setup_act"), S("setup_dve"), S("idle_z", 2)
        x_hi, x_lo, gate_z = S("x_hi", CT), S("x_lo", CT), S("gate_z", 4)
        tanh_r, tanh_i, a_exp, a_tanh, a_sq = (S(n, CT) for n in ("tanh_r", "tanh_i", "a_exp", "a_tanh", "a_square"))
        a_cut, w_ready, w_root = S("a_cut", CT), S("w_ready", CT), S("w_root", CT)
        ix_ready, u_ready, state_ready, y_ready = (S(n, CT) for n in ("ix_ready", "u_ready", "state_ready", "y_ready"))
        y_turned, y_copied, x1_turned = (S(n, 2) for n in ("y_turned", "y_copied", "x1_turned"))
        x1_hi, x1_lo, resid1 = S("x1_hi", 2), S("x1_lo", 2), S("resid1", 2)
        ln_stats = [S(f"ln{i}_stats_s", NB) for i in range(4)]
        ln_mv = [S(f"ln{i}_mv_s", NB) for i in range(4)]
        ln_var = [S(f"ln{i}_var_s", 2) for i in range(4)]
        ln_rstd = [S(f"ln{i}_rstd_s") for i in range(4)]
        ln_shift = [S(f"ln{i}_shift_s") for i in range(4)]
        ln_done = [S(f"ln{i}_done", NB) for i in range(4)]
        logit_z, logit_copied, logit_turned = S("logit_z"), S("logit_copied"), S("logit_turned")
        ROUTE = 22
        route, route_exp, route_tanh = S("route", ROUTE), S("route_exp"), S("route_tanh")
        gate_turned, gate_copied = S("gate_turned"), S("gate_copied")
        down_z, down_copied, h_act, h_hi, h_lo = (S(n) for n in ("down_z", "down_copied", "h_act", "h_hi", "h_lo"))
        x1_sum, g1_act, g1_hi, g1_lo = S("x1_sum"), S("g1_act", CT), S("g1_hi", CT), S("g1_lo", CT)
        hid_z, hid_act, hid_hi, hid_lo, hid_used = (S(n, NT) for n in ("hid_z", "hid_act", "hid_hi", "hid_lo", "hid_used"))
        combined, summed = S("combined", E + 1), S("summed", E)
        m_hi, m_lo, moe_out, y2_ready = S("m_hi"), S("m_lo"), S("moe_out", 2), S("y2_ready", 2)
        x2_turned, x2_hi, x2_lo = S("x2_turned", 2), S("x2_hi", 2), S("x2_lo", 2)
        k_z, v_z, q_z = (S(n, CT) for n in ("k_z", "v_z", "q_z"))
        k_exp, k_min, k_phi, kv_ready, q_exp, q_min, q_phi = (S(n, CT) for n in ("k_exp", "k_min", "k_phi", "kv_ready", "q_exp", "q_min", "q_phi"))
        scanned, qk_ready, num_ready = S("scanned", 4 * CT), S("qk_ready", CT), S("num_ready", CT)
        den_z, den_copied, den_turned, den_max, den_inv, den_wide = (S(n) for n in ("den_z", "den_copied", "den_turned", "den_max", "den_inv", "den_wide"))
        inv_turned, o_ready, o_hi, o_lo = (S(n, CT) for n in ("inv_turned", "o_ready", "o_hi", "o_lo"))
        attn_out, y3_ready = S("attn_out", 2), S("y3_ready", 2)
        x3_turned, x3_hi, x3_lo = S("x3_turned", 2), S("x3_hi", 2), S("x3_lo", 2)
        ff_z, ff_tanh, ff_silu, ff_hid, ff_hi, ff_lo, ff_used = (S(n, FT) for n in ("ff_z", "ff_tanh", "ff_silu", "ff_hid", "ff_hi", "ff_lo", "ff_used"))
        y4_ready = S("y4_ready", 2)
        half_var = {i: S(f"ln{i}_half_var", 4) for i in (2, 3)}
        half_rstd, half_shift = ({i: S(f"ln{i}_half_{n}", 2) for i in (2, 3)} for n in ("rstd", "shift"))

        def raw_piece(m):
            if m < SLOTS and m >= 2:
                if m < 2 + 2 * CT:
                    return mid_raw[:, m - 2, :]
                return tok[:, (m % 2) * 2:(m % 2) * 2 + 2, :].rearrange("p b n -> p (b n)")
            return tok3[:, (m % 2) * 2:(m % 2) * 2 + 2, :].rearrange("p b n -> p (b n)")

        def piece_signal(m):
            if m < SLOTS:
                return piece_loaded[m], 16
            return piece_loaded[m % 2], 16 * ((m - SLOTS) // 2 + 2)

        block = ctx.enter_context(nc.Block())

        def last_tile(o):
            return max(t for t, (e, _) in enumerate(TILES) if e == o - 1)

        @block.sync
        def _(sp):
            def piece(m):
                if m >= SLOTS:
                    sp.wait_ge(piece_lo.sem, piece_lo.nth(m - (SLOTS if m < SLOTS + 2 else 2)))
                c = EXPERTS + m * PIECE
                sp.dma_start(raw_piece(m), weights[:, c:c + PIECE]).then_inc(piece_signal(m)[0].sem, 16)

            def load_x(k):
                if later(k):
                    sp.wait_ge(y_turned.sem, y_turned.nth(k - 1, 1))
                    apart(sp)
                sp.dma_start(xy[:], x_chunks[k]).then_inc(x_loaded.sem, 16)

            def store_gates(k):
                sp.wait_ge(gate_copied.sem, gate_copied.nth(k))
                sp.dma_start(gates_dram[k].rearrange("e (b t) -> (e b) t", t=128), gt).then_inc(gates_stored.sem, 16)

            def gate_row(k, e):
                if e == 0:
                    sp.wait_ge(gates_stored.sem, gates_stored.nth(k))
                    apart(sp)
                    sp.wait_ge(x1_turned.sem, x1_turned.nth(k, 1))
                    apart(sp)
                    sp.wait_ge(resid1.sem, resid1.nth(k, 1))
                elif e >= 2:
                    sp.wait_ge(combined.sem, combined.nth(k, e + 1 - 2))
                sp.dma_start(gate[:, e % 2, :], gates_dram[k][e].partition_broadcast(128)).then_inc(row_loaded[e % 2].sem, 16)

            sp.dma_start(dense_raw[:, 0:DOWN], weights[:, 0:DOWN]).then_inc(w0_loaded.sem, 16)
            sp.dma_start(xy[:], x_chunks[0]).then_inc(x_loaded.sem, 16)
            sp.dma_start(dense_raw[:, DOWN:EXPERTS], weights[:, DOWN:EXPERTS]).then_inc(w1_loaded.sem, 16)
            for m in range(SLOTS):
                piece(m)
            sp.dma_start(w2_raw[:], weights[:, W2:WCOLS]).then_inc(w2_loaded.sem, 16)
            for m in range(SLOTS, EARLY):
                piece(m)
            load_x(1)
            store_gates(0)
            for e in range(E):
                gate_row(0, e)
            for m in range(EARLY, PIECES):
                piece(m)
            store_gates(1)
            with sp.Fori(1, LAST) as r:
                load_x(r + 1)
                for e in range(E):
                    gate_row(r, e)
                store_gates(r + 1)
            for e in range(E):
                gate_row(LAST, e)
            sp.wait_ge(out_stored.sem, out_stored.nth(chunks + 1))
            sp.wait_ge(gates_stored.sem, gates_stored.nth(LAST))

        @block.tensor
        def _(pe):
            def product(out, a, b, start=True, stop=True, shared=False):
                (ah, al), (bh, bl) = a, b
                pe.matmul(out, ah, bh, start=start, stop=False, skip_group_check=shared)
                pe.matmul(out, ah, bl, start=False, stop=False, skip_group_check=shared)
                return pe.matmul(out, al, bh, start=False, stop=stop, skip_group_check=shared)

            def w(c, n=128):
                return wh[:, c:c + n], wl[:, c:c + n]

            def two(h, l, i, lo=0, n=CHUNK):
                return h[:, i, lo:lo + n], l[:, i, lo:lo + n]

            def gates(k, c):
                pe.wait_ge(x_lo.sem, x_lo.nth(k, CT - 1))
                for g, base in enumerate((WA, WX)):
                    if c:
                        pe.wait_ge((tanh_r, tanh_i)[g].sem, (tanh_r, tanh_i)[g].nth(k, c - 1))
                    for kt in range(CT):
                        last = product(M[g][:], w(base + kt * D + c * 128), two(chan_h, chan_l, kt), kt == 0, kt == CT - 1)
                    last.then_inc(gate_z.sem, 1)

            def to_tokens(src, done):
                for b in range(NB):
                    for c in range(CT):
                        last = pe.transpose(M[b // 2][:, (b % 2) * D + c * 128:(b % 2) * D + (c + 1) * 128],
                                            src[:, c, b * 128:(b + 1) * 128], ident)
                    if b % 2:
                        last.then_inc(done.sem, 1)

            def to_channels(src, done):
                for c in range(CT):
                    for b in range(NB):
                        last = pe.transpose(M[c][:, b * 128:(b + 1) * 128], src[:, b, c * 128:(c + 1) * 128], ident)
                    last.then_inc(done.sem, 1)

            def turn_y(k):
                pe.wait_ge(y_ready.sem, y_ready.nth(k, CT - 1))
                to_tokens(xy, y_turned)

            def turn_x1(k):
                pe.wait_ge(ln_done[0].sem, ln_done[0].nth(k, NB - 1))
                to_channels(gate_tok, x1_turned)

            def logits(k):
                pe.wait_ge(x1_lo.sem, x1_lo.nth(k, CT - 1))
                for kt in range(CT):
                    last = product(M[1][:], w(ROUTER + kt * E), two(chan_h, chan_l, kt), kt == 0, kt == CT - 1)
                last.then_inc(logit_z.sem, 1)

            def turn_logits(k):
                pe.wait_ge(logit_copied.sem, logit_copied.nth(k))
                apart(pe)
                for b in range(NB):
                    last = pe.transpose(M[1][:, b * E:(b + 1) * E], lg[:, b * 128:(b + 1) * 128], ident[0:E, 0:E])
                last.then_inc(logit_turned.sem, 1)

            def turn_gates(k):
                pe.wait_ge(route.sem, route.nth(k, ROUTE - 1))
                pe.transpose(M[0][0:NB * E, 0:128], rt[:, 8, :], ident).then_inc(gate_turned.sem, 1)

            def down(k):
                pe.wait_ge(x1_lo.sem, x1_lo.nth(k, CT - 1))
                for kt in range(CT):
                    last = product(M[1][:], w(DOWN + kt * L), two(chan_h, chan_l, kt), kt == 0, kt == CT - 1)
                last.then_inc(down_z.sem, 1)

            def idle_experts(some):
                pe.wait_ge(setup_dve.sem, setup_dve.nth(IDLE_SPLIT))
                for t, (e, j) in enumerate(TILES[1:]):
                    if e not in some:
                        continue
                    if j == 0:
                        pe.wait_ge(piece_lo.sem, piece_lo.nth((EW2[e] + HID[e] - EXPERTS - 1) // PIECE))
                    pe.matmul(R[5][:, 2 * e:2 * e + 2], wh[:, EW2[e] + j * 128:EW2[e] + (j + 1) * 128], b1s[:, t, :],
                              start=j == 0, stop=False)
                    last = pe.matmul(R[5][:, 2 * e:2 * e + 2], wl[:, EW2[e] + j * 128:EW2[e] + (j + 1) * 128], b1s[:, t, :],
                                     start=False, stop=j == HID[e] // 128 - 1)
                last.then_inc(idle_z.sem, 1)

            def first(k, t):
                e, j = TILES[t]
                if t == 0:
                    pe.wait_ge(h_lo.sem, h_lo.nth(k))
                if t < 3:
                    if later(k):
                        pe.wait_ge(ff_hid.sem, ff_hid.nth(k - 1, FT - 1))
                else:
                    pe.wait_ge(hid_act.sem, hid_act.nth(k, t - 3))
                product(R[t % 3][:], w(SW1 if e < 0 else EW1[e] + j * 128), (sh[:, 3, :], sl3[:])).then_inc(hid_z.sem, 1)

            def second(k, t):
                e, j = TILES[t]
                o = e + 1
                pe.wait_ge(hid_lo.sem, hid_lo.nth(k, t))
                if j == 0:
                    if o < 3:
                        if later(k):
                            pe.wait_ge(y4_ready.sem, y4_ready.nth(k - 1, 1))
                        if isinstance(k, int) and k == 0 and o == 2:
                            pe.wait_ge(setup_dve.sem, setup_dve.nth(IDLE_COPIED))
                    else:
                        pe.wait_ge(combined.sem, combined.nth(k, o - 3))
                n = 1 if e < 0 else HID[e] // 128
                product(R[3 + o % 3][:], w(SW2 if e < 0 else EW2[e] + j * 128), two(sh, sl, t % 3), j == 0, j == n - 1)\
                    .then_inc(hid_used.sem, 1)

            def core_product(k, half):
                pe.wait_ge(g1_lo.sem, g1_lo.nth(k, CT - 1))
                for b in (2 * half, 2 * half + 1):
                    for kt in range(CT):
                        product(M[half][:, (b % 2) * D:(b % 2 + 1) * D], two(mid_h, mid_l, kt, b * 128, 128),
                                w(CORE + kt * D, D), b % 2 == 0 and kt == 0, False, shared=True)

            def up_product(k):
                pe.wait_ge(m_lo.sem, m_lo.nth(k))
                for b in range(NB):
                    last = product(M[b // 2][:, (b % 2) * D:(b % 2 + 1) * D], (sh[:, 3, b * 128:(b + 1) * 128], sl3[:, b * 128:(b + 1) * 128]), w(UP, D),
                                   False, True, shared=True)
                    if b % 2:
                        last.then_inc(moe_out.sem, 1)

            def turn_x2(k):
                pe.wait_ge(ln_done[1].sem, ln_done[1].nth(k, NB - 1))
                to_channels(tok, x2_turned)

            def qkv(k, which, c):
                bank = which // 2
                for kt in range(CT):
                    last = product(M[bank][:], w(QKV + kt * 3 * D + which * D + c * 128), two(mid_h, mid_l, kt), kt == 0, kt == CT - 1)
                last.then_inc((q_z, k_z, v_z)[which].sem, 1)

            def denominators(k):
                for c in range(CT):
                    pe.wait_ge(qk_ready.sem, qk_ready.nth(k, c))
                    last = pe.matmul(M[0][0:HEADS, :], cst[:, C_HEAD + c * HEADS:C_HEAD + (c + 1) * HEADS], ac[:, 3 + c, :],
                                     start=c == 0, stop=c == CT - 1)
                last.then_inc(den_z.sem, 1)

            def turn_denominators(k):
                pe.wait_ge(den_copied.sem, den_copied.nth(k))
                apart(pe)
                for b in range(NB):
                    last = pe.transpose(M[1][:, b * HEADS:(b + 1) * HEADS], ac[0:HEADS, 2, b * 128:(b + 1) * 128],
                                        ident[0:HEADS, 0:HEADS])
                last.then_inc(den_turned.sem, 1)

            def turn_inverses(k):
                pe.wait_ge(den_wide.sem, den_wide.nth(k))
                wide = ac[:, 0:2, :].rearrange("p a (b n) -> p (a b) n", n=D)
                to_channels(wide, inv_turned)

            def attention_product(k):
                pe.wait_ge(o_lo.sem, o_lo.nth(k, CT - 1))
                for b in range(NB):
                    for kt in range(CT):
                        last = product(M[b // 2][:, (b % 2) * D:(b % 2 + 1) * D], two(mid_h, mid_l, kt, b * 128, 128),
                                       w(WOUT + kt * D, D), kt == 0, kt == CT - 1)
                    if b % 2:
                        last.then_inc(attn_out.sem, 1)

            def turn_x3(k):
                pe.wait_ge(ln_done[2].sem, ln_done[2].nth(k, NB - 1))
                pe.wait_ge(y3_ready.sem, y3_ready.nth(k, 1))
                to_channels(tok3, x3_turned)

            def ffn_first(r, j):
                if j == 0:
                    if later(r):
                        pe.wait_ge(x3_lo.sem, x3_lo.nth(r - 1, CT - 1))
                p = 2 * (j % 2)
                if j < 2:
                    pe.wait_ge(hid_act.sem, hid_act.nth(r, NT - 1))
                    pe.wait_ge(combined.sem, combined.nth(r, E - 2))
                pe.wait_ge(ff_hid.sem, ff_hid.nth(r, j - 2))
                for g, base in enumerate((W1, W3)):
                    for kt in range(CT):
                        last = product(R[p + g][:], w(base + kt * FF + j * 128), two(ffn_h, ffn_l, kt), kt == 0, kt == CT - 1)
                last.then_inc(ff_z.sem, 1)

            def ffn_second(r, j):
                pe.wait_ge(ff_lo.sem, ff_lo.nth(r, j))
                if j == 0:
                    if later(r):
                        pe.wait_ge(y4_ready.sem, y4_ready.nth(r - 1, 1))
                    pe.wait_ge(combined.sem, combined.nth(r, E))
                for b in range(NB):
                    last = product(R[4 + b // 2][:, (b % 2) * D:(b % 2 + 1) * D], two(sh, sl, j % 3, b * 128, 128),
                                   w(W2 + j * D, D), j == 0 and b % 2 == 0, j == FT - 1, shared=True)
                last.then_inc(ff_used.sem, 1)

            def last_turn_x3(h):
                pe.wait_ge(ln_done[2].sem, ln_done[2].nth(LAST, 2 * h + 1))
                pe.wait_ge(y3_ready.sem, y3_ready.nth(LAST, h))
                for c in range(CT):
                    for b in range(2):
                        last = pe.transpose(M[h][:, c * HALF + b * 128:c * HALF + (b + 1) * 128],
                                            tok[:, 2 * h + b, c * 128:(c + 1) * 128], ident)
                last.then_inc(x3_turned.sem, 1)

            def last_first(n):
                h, j = divmod(n, FT)
                if j == 0:
                    pe.wait_ge(x3_lo.sem, x3_lo.nth(LAST, h))
                pe.wait_ge(ff_hid.sem, ff_hid.nth(chunks, n - 4) if n >= 4 else ff_hid.nth(LAST, FT - 1))
                for g, base in enumerate((W1, W3)):
                    for kt in range(CT):
                        last = product(R[n % 4][:, g * HALF:(g + 1) * HALF], w(base + kt * FF + j * 128),
                                       two(ffn_h, ffn_l, kt, h * HALF, HALF), kt == 0, kt == CT - 1)
                last.then_inc(ff_z.sem, 1)

            def last_second(n):
                h, j = divmod(n, FT)
                pe.wait_ge(ff_lo.sem, ff_lo.nth(chunks, n))
                if n == 0:
                    pe.wait_ge(y4_ready.sem, y4_ready.nth(LAST, 1))
                for b in range(2):
                    last = product(R[4 + h][:, b * D:(b + 1) * D], two(sh, sl, n % 3, b * 128, 128),
                                   w(W2 + j * D, D), j == 0 and b == 0, j == FT - 1, shared=True)
                last.then_inc(ff_used.sem, 1)

            def experts(r):
                more = more_chunks(r)
                for t in range(NT + LAG):
                    if t < NT:
                        first(r, t)
                    if t == X3_TILE and later(r):
                        turn_x3(r - 1)
                    if t == 2 and not later(r):
                        idle_experts(range(5, E))
                    if t == GATES_TURN and not later(r):
                        turn_gates(0)
                        pe.wait_ge(gate_copied.sem, gate_copied.nth(0))
                    if t in GATE_TILES and more:
                        if t == GATE_TILES[0] and later(r):
                            pe.wait_ge(x3_lo.sem, x3_lo.nth(r - 1, CT - 1))
                        gates(r + 1, GATE_TILES.index(t))
                    if t in CORE_TILES:
                        half = CORE_TILES.index(t)
                        if more:
                            pe.wait_ge((tanh_r, tanh_i)[half].sem, (tanh_r, tanh_i)[half].nth(r + 1, CT - 1))
                        else:
                            pe.wait_ge(x3_lo.sem, x3_lo.nth(r - 1, CT - 1))
                        core_product(r, half)
                    if t >= LAG:
                        second(r, t - LAG)

            def rest(r, has_ffn):
                more = more_chunks(r)

                def ff(j):
                    if has_ffn:
                        ffn_first(r, j)
                        if 2 <= j < FT - 3:
                            ffn_second(r, j - 2)
                    elif j < W2_PIECES:
                        pe.wait_ge(had_step.sem, had_step.nth(2 * HAD_STEPS - 1))
                        pe.wait_ge(hid_act.sem, hid_act.nth(r, NT - 1))
                        pe.wait_ge(combined.sem, combined.nth(r, E))
                        pe.matmul(R[j][:], cst[:, C_HAD:C_HAD + 128], w2_raw[:, j * PIECE:(j + 1) * PIECE], start=True, stop=True)\
                            .then_inc(had_z.sem, 1)
                    elif j == FT - 1:
                        pe.sem_inc(ff_z.sem, FT)
                        pe.sem_inc(ff_used.sem, FT)
                ff(0)
                up_product(r)
                ff(1)
                pe.wait_ge(y2_ready.sem, y2_ready.nth(r, 1))
                if more:
                    turn_y(r + 1)
                ff(2)
                if more:
                    pe.wait_ge(y_copied.sem, y_copied.nth(r + 1, 1))
                turn_x2(r)
                ff(3)
                pe.wait_ge(x2_lo.sem, x2_lo.nth(r, 1))
                if more:
                    turn_x1(r + 1)
                ff(4)
                if more:
                    pe.wait_ge(x1_lo.sem, x1_lo.nth(r + 1, 1))
                qkv(r, 1, 0)
                qkv(r, 2, 0)
                ff(5)
                pe.wait_ge(k_phi.sem, k_phi.nth(r))
                qkv(r, 0, 0)
                pe.wait_ge(kv_ready.sem, kv_ready.nth(r))
                if more:
                    logits(r + 1)
                if has_ffn:
                    ffn_second(r, FT - 5)
                if more:
                    turn_logits(r + 1)
                pe.wait_ge(q_phi.sem, q_phi.nth(r))
                qkv(r, 1, 1)
                if more:
                    pe.wait_ge(route.sem, route.nth(r + 1))
                qkv(r, 2, 1)
                if has_ffn:
                    ffn_second(r, FT - 4)
                pe.wait_ge(k_phi.sem, k_phi.nth(r, 1))
                qkv(r, 0, 1)
                pe.wait_ge(kv_ready.sem, kv_ready.nth(r, 1))
                if more:
                    down(r + 1)
                ff(6)
                pe.wait_ge(q_phi.sem, q_phi.nth(r, 1))
                denominators(r)
                if has_ffn:
                    ffn_second(r, FT - 3)
                if more:
                    pe.wait_ge(down_copied.sem, down_copied.nth(r + 1))
                turn_denominators(r)
                ff(7)
                if more:
                    turn_gates(r + 1)
                    pe.wait_ge(gate_copied.sem, gate_copied.nth(r + 1))
                pe.wait_ge(den_max.sem, den_max.nth(r))
                turn_inverses(r)
                if has_ffn:
                    ffn_second(r, FT - 2)
                if has_ffn and more:
                    ffn_second(r, FT - 1)
                attention_product(r)
                if not more:
                    ffn_second(r, FT - 1)

            pe.wait_ge(small_loaded.sem, 16)
            pe.wait_ge(dense_lo.sem, dense_lo.nth(0))
            gates(0, 0)
            gates(0, 1)
            pe.wait_ge(tanh_r.sem, tanh_r.nth(0, 1))
            pe.wait_ge(tanh_i.sem, tanh_i.nth(0, 1))
            turn_y(0)
            idle_experts(range(0, 5))
            pe.wait_ge(y_copied.sem, y_copied.nth(0, 1))
            turn_x1(0)
            pe.wait_ge(dense_lo.sem, dense_lo.nth(1))
            down(0)
            pe.wait_ge(down_copied.sem, down_copied.nth(0))
            logits(0)
            turn_logits(0)
            experts(0)
            pe.wait_ge(piece_lo.sem, piece_lo.nth(EARLY - 1))
            rest(0, False)
            pe.wait_ge(piece_lo.sem, piece_lo.nth(PIECES - 1))
            pe.wait_ge(had_lo.sem, had_lo.nth(3))
            with pe.Fori(1, LAST) as r:
                experts(r)
                rest(r, True)
            experts(LAST)
            rest(LAST, True)
            last_turn_x3(0)
            for n in range(2 * FT + 2):
                if n < 2 * FT:
                    last_first(n)
                if n == X3_STEP:
                    last_turn_x3(1)
                if n >= 2:
                    last_second(n - 2)

        @block.scalar
        def _(act):
            def gate_r(k, c):
                if c == 0:
                    if later(k):
                        act.wait_ge(y_ready.sem, y_ready.nth(k - 1, CT - 1))
                    if later(k - 1):
                        act.wait_ge(inv_turned.sem, inv_turned.nth(k - 2, 1))
                        act.wait_ge(o_lo.sem, o_lo.nth(k - 2, CT - 1))
                act.wait_ge(gate_z.sem, gate_z.nth(k, 2 * c))
                act.activation(ac[:, c, :], M[0][:], ACT.Tanh, bias=half_b[:, c:c + 1], scale=0.5).then_inc(tanh_r.sem, 1)

            def gate_i(k, c):
                act.wait_ge(gate_z.sem, gate_z.nth(k, 2 * c + 1))
                act.activation(ac[:, 2 + c, :], M[1][:], ACT.Tanh, bias=half_b[:, CT + c:CT + c + 1], scale=0.5).then_inc(tanh_i.sem, 1)

            def decays(k, c):
                act.wait_ge(tanh_r.sem, tanh_r.nth(k, c))
                if c == 0 and later(k):
                    act.wait_ge(summed.sem, summed.nth(k - 1))
                    act.wait_ge(g1_lo.sem, g1_lo.nth(k - 1, CT - 1))
                act.activation(ac[:, 4 + c, :], ac[:, c, :], ACT.Exp, bias=c2[:, c:c + 1], scale=c2[:, c:c + 1]).then_inc(a_exp.sem, 1)

            def decay_parts(k, c):
                act.wait_ge(a_exp.sem, a_exp.nth(k, c))
                act.activation(ac[:, c, :], ac[:, c, :], ACT.Tanh, bias=nc2[:, c:c + 1], scale=nc2[:, c:c + 1]).then_inc(a_tanh.sem, 1)
                if c:
                    act.wait_ge(w_ready.sem, w_ready.nth(k, c - 1))
                act.activation(ac[:, 6, :], ac[:, 4 + c, :], ACT.Square).then_inc(a_sq.sem, 1)

            def root(k):
                act.wait_ge(w_ready.sem, w_ready.nth(k, CT - 1))
                for c in range(CT):
                    act.activation(ac[:, c, :], ac[:, c, :], ACT.Sqrt).then_inc(w_root.sem, 1)

            def x_high(k, c):
                act.wait_ge(x_loaded.sem, x_loaded.nth(k))
                if later(k):
                    act.wait_ge(down_z.sem, down_z.nth(k - 1))
                    act.wait_ge(logit_z.sem, logit_z.nth(k - 1))
                    act.wait_ge(x1_sum.sem, x1_sum.nth(k - 1))
                act.activation(chan_h[:, c, :], xy[:, c, :], ACT.Copy).then_inc(x_hi.sem, 1)

            def normed(i, k, buf):
                act.wait_ge(ln_shift[i].sem, ln_shift[i].nth(k))
                for b in range(NB):
                    act.activation(buf[:, b, :], buf[:, b, :], ACT.Identity, bias=rs[i][:, 3, b:b + 1], scale=rs[i][:, 1, b:b + 1])\
                        .then_inc(ln_done[i].sem, 1)

            def y_copy(k):
                if later(k):
                    act.wait_ge(combined.sem, combined.nth(k - 1, E))
                for i in range(2):
                    act.wait_ge(y_turned.sem, y_turned.nth(k, i))
                    act.activation(gate[:, i, :], M[i][:], ACT.Copy).then_inc(y_copied.sem, 1)

            def x1_norm(k):
                normed(0, k, gate_tok)

            def x2_norm(k):
                normed(1, k, tok)

            def x3_norm(k):
                normed(2, k, tok3)

            def out_norm(r):
                normed(3, r - 1, y4)
                act.wait_ge(ln_done[3].sem, ln_done[3].nth(r - 1, NB - 1))
                apart(act)
                act.dma_start(out_chunks[r - 1], y4).then_inc(out_stored.sem, 16)

            def x1_high(k):
                for c in range(CT):
                    act.wait_ge(x1_turned.sem, x1_turned.nth(k, c))
                    act.wait_ge(gate_z.sem, gate_z.nth(k, 3))
                    act.activation(chan_h[:, c, :], M[c][:], ACT.Copy).then_inc(x1_hi.sem, 1)

            def logit_copy(k):
                act.wait_ge(logit_z.sem, logit_z.nth(k))
                if later(k):
                    act.wait_ge(m_lo.sem, m_lo.nth(k - 1))
                act.activation(lg, M[1][0:E, :], ACT.Copy).then_inc(logit_copied.sem, 1)

            def route_e(k):
                act.wait_ge(route.sem, route.nth(k, 2))
                act.activation(rt[:, 2, :], rt[:, 1, :], ACT.Exp).then_inc(route_exp.sem, 1)

            def route_t(k):
                act.wait_ge(route.sem, route.nth(k, 16))
                act.activation(r4[:, 6, :], r4[:, 5, :], ACT.Tanh, scale=-0.5).then_inc(route_tanh.sem, 1)

            def gate_copy(k):
                act.wait_ge(gate_turned.sem, gate_turned.nth(k))
                if later(k):
                    act.wait_ge(m_lo.sem, m_lo.nth(k - 1))
                act.activation(gt, M[0][0:NB * E, 0:128], ACT.Copy).then_inc(gate_copied.sem, 1)

            def down_copy(k):
                act.wait_ge(down_z.sem, down_z.nth(k))
                if later(k):
                    act.wait_ge(moe_out.sem, moe_out.nth(k - 1, 1))
                act.activation(h_raw[:], M[1][:], ACT.Identity, bias=vec[:, V_DOWN:V_DOWN + 1]).then_inc(down_copied.sem, 1)

            def h_gelu(k):
                act.wait_ge(down_copied.sem, down_copied.nth(k))
                act.activation(sh[:, 3, :], h_raw[:], ACT.Gelu).then_inc(h_hi.sem, 1)
                act.wait_ge(h_hi.sem, h_hi.nth(k))
                act.activation(h_raw[:], h_raw[:], ACT.Gelu).then_inc(h_act.sem, 1)

            def g1_gelu(k, c):
                act.wait_ge(x1_sum.sem, x1_sum.nth(k))
                act.activation(ac[:, 5 + c, :], ac[:, 5 + c, :], ACT.Gelu).then_inc(g1_act.sem, 1)

            def hidden(k, t):
                act.wait_ge(hid_z.sem, hid_z.nth(k, t))
                if t < 3:
                    if later(k):
                        act.wait_ge(ff_lo.sem, ff_lo.nth(k - 1, FT - 1))
                else:
                    act.wait_ge(hid_lo.sem, hid_lo.nth(k, t - 3))
                b = vec[:, V_S1:V_S1 + 1] if t == 0 else vec[:, V_E1 + t - 1:V_E1 + t]
                act.activation(hid[:, t % 3, :], R[t % 3][:], ACT.Gelu, bias=b).then_inc(hid_act.sem, 1)

            def x2_high(k):
                for c in range(CT):
                    act.wait_ge(x2_turned.sem, x2_turned.nth(k, c))
                    act.activation(mid_h[:, c, :], M[c][:], ACT.Copy).then_inc(x2_hi.sem, 1)

            def key_exp(k, c):
                act.wait_ge(k_z.sem, k_z.nth(k, c))
                if c == 0:
                    if more_chunks(k):
                        act.wait_ge(y_ready.sem, y_ready.nth(k + 1, CT - 1))
                else:
                    act.wait_ge(scanned.sem, scanned.nth(k, 4 * c - 1))
                act.activation(ac[:, 0, :], M[0][:], ACT.Exp).then_inc(k_exp.sem, 1)

            def query_exp(k, c):
                act.wait_ge(q_z.sem, q_z.nth(k, c))
                if c:
                    act.wait_ge(num_ready.sem, num_ready.nth(k, c - 1))
                act.activation(ac[:, 2, :], M[0][:], ACT.Exp).then_inc(q_exp.sem, 1)

            def den_copy(k):
                act.wait_ge(den_z.sem, den_z.nth(k))
                act.wait_ge(num_ready.sem, num_ready.nth(k, CT - 1))
                act.activation(ac[0:HEADS, 2, :], M[0][0:HEADS, :], ACT.Copy).then_inc(den_copied.sem, 1)

            def den_expand(k):
                act.wait_ge(den_inv.sem, den_inv.nth(k))
                act.wait_ge(scanned.sem, scanned.nth(k, 4 * CT - 1))
                act.activation(ac[:, 0:2, :].rearrange("p a (n d) -> p (a n) d", d=HEAD),
                               rden[:].unsqueeze(2).broadcast_to([128, NB * HEADS, HEAD]), ACT.Copy).then_inc(den_wide.sem, 1)

            def o_high(k, c):
                act.wait_ge(o_ready.sem, o_ready.nth(k, c))
                act.wait_ge(q_z.sem, q_z.nth(k, CT - 1))
                act.wait_ge(v_z.sem, v_z.nth(k, CT - 1))
                act.activation(mid_h[:, c, :], ac[:, 5 + c, :], ACT.Copy).then_inc(o_hi.sem, 1)

            def x3_high(k):
                for c in range(CT):
                    act.wait_ge(x3_turned.sem, x3_turned.nth(k, c))
                    act.wait_ge(ff_z.sem, ff_z.nth(k, FT - 1))
                    act.activation(ffn_h[:, c, :], M[c][:], ACT.Copy).then_inc(x3_hi.sem, 1)

            def ffn(r, j):
                act.wait_ge(ff_z.sem, ff_z.nth(r, j))
                if j < 3:
                    act.wait_ge(hid_lo.sem, hid_lo.nth(r, NT - 1))
                act.wait_ge(ff_lo.sem, ff_lo.nth(r, j - 3))
                act.activation(hid[:, j % 3, :], R[2 * (j % 2)][:], ACT.Tanh, scale=0.5).then_inc(ff_tanh.sem, 1)

            def last_normed(i, h, buf):
                act.wait_ge(half_shift[i].sem, half_shift[i].nth(0, h))
                for b in (2 * h, 2 * h + 1):
                    act.activation(buf[:, b, :], buf[:, b, :], ACT.Identity, bias=rs[i][:, 3, b:b + 1], scale=rs[i][:, 1, b:b + 1])\
                        .then_inc(ln_done[i].sem, 1)

            def last_x3_high(h):
                act.wait_ge(x3_turned.sem, x3_turned.nth(LAST, h))
                act.wait_ge(ff_z.sem, ff_z.nth(LAST, FT - 1))
                act.activation(ffn_h[:, :, h * HALF:(h + 1) * HALF], M[h][:].rearrange("p (c n) -> p c n", c=CT), ACT.Copy)\
                    .then_inc(x3_hi.sem, 1)

            def last_ffn(n):
                act.wait_ge(ff_z.sem, ff_z.nth(chunks, n))
                act.wait_ge(ff_lo.sem, ff_lo.nth(chunks, n - 3))
                act.activation(hid[:, n % 3, 0:HALF], R[n % 4][:, 0:HALF], ACT.Tanh, scale=0.5).then_inc(ff_tanh.sem, 1)

            def last_out(h):
                last_normed(3, h, y4)
                act.wait_ge(ln_done[3].sem, ln_done[3].nth(LAST, 2 * h + 1))
                act.dma_start(out_chunks[LAST][:, 2 * h:2 * h + 2, :], y4[:, 2 * h:2 * h + 2, :]).then_inc(out_stored.sem, 16)

            def experts(r):
                more = more_chunks(r)
                if later(r):
                    x3_high(r - 1)
                for t in range(AHEAD, NT):
                    hidden(r, t)
                    if more:
                        if t in (6, 7):
                            x_high(r + 1, t - 6)
                        if t in GATE_TILES:
                            gate_r(r + 1, GATE_TILES.index(t))
                            gate_i(r + 1, GATE_TILES.index(t))
                        if t == EXP_TILE:
                            decays(r + 1, 0)
                            decays(r + 1, 1)
                        if t in PARTS_TILES:
                            decay_parts(r + 1, PARTS_TILES.index(t))
                        if t == ROOT_TILE:
                            root(r + 1)

            def rest(r, has_ffn):
                more = more_chunks(r)

                def ff(j):
                    if has_ffn:
                        ffn(r, j)
                    else:
                        weights_high(EARLY + j)
                        if j < W2_PIECES:
                            had_high(j)
                        if j == FT - 1:
                            act.sem_inc(ff_tanh.sem, FT)
                            act.sem_inc(out_stored.sem, 16)
                ff(0)
                if more:
                    y_copy(r + 1)
                ff(1)
                x2_norm(r)
                if not has_ffn:
                    x1_norm(r + 1)
                x2_high(r)
                if has_ffn and more:
                    x1_norm(r + 1)
                ff(2)
                if has_ffn:
                    ff(3)
                if more:
                    x1_high(r + 1)
                if not has_ffn:
                    ff(3)
                if has_ffn:
                    ff(4)
                key_exp(r, 0)
                if not has_ffn:
                    ff(4)
                ff(5)
                query_exp(r, 0)
                if more:
                    logit_copy(r + 1)
                key_exp(r, 1)
                if more:
                    route_e(r + 1)
                query_exp(r, 1)
                if more:
                    down_copy(r + 1)
                ff(6)
                den_copy(r)
                if more:
                    route_t(r + 1)
                den_expand(r)
                ff(7)
                if more:
                    gate_copy(r + 1)
                o_high(r, 0)
                o_high(r, 1)
                if more:
                    h_gelu(r + 1)
                    for t in range(4):
                        hidden(r + 1, t)
                        if t in (1, 2):
                            g1_gelu(r + 1, t - 1)
                    x3_norm(r)
                    hidden(r + 1, 4)
                    hidden(r + 1, 5)
                else:
                    last_normed(2, 0, tok)
                    last_x3_high(0)
                    last_normed(2, 1, tok)
                if has_ffn and more:
                    out_norm(r)

            def weights_high(m):
                signal, count = piece_signal(m)
                act.wait_ge(signal.sem, count)
                c = EXPERTS + m * PIECE
                act.activation(wh[:, c:c + PIECE], raw_piece(m), ACT.Copy).then_inc(piece_hi.sem, 1)

            def had_high(q):
                act.wait_ge(had_z.sem, had_z.nth(q))
                act.activation(wh[:, W2 + q * PIECE:W2 + (q + 1) * PIECE], R[q][:], ACT.Copy).then_inc(had_hi.sem, 1)

            act.dma_start(vec[:], vectors).then_inc(vec_loaded.sem, 16)
            act.dma_start(cst[:], consts).then_inc(small_loaded.sem, 16)
            act.dma_start(ac[:, 5:7, :].rearrange("p a n -> p (a n)")[:, 0:rows.shape[0]], rows.partition_broadcast(128)).then_inc(rows_loaded.sem, 16)
            act.wait_ge(vec_loaded.sem, 16)
            act.activation(ser[:, 0, :], vec[:, V_LAM:V_LAM + CT], ACT.Abs).then_inc(setup_act.sem, 1)
            act.wait_ge(setup_act.sem, setup_act.nth(0))
            act.activation(ser[:, 1, :], ser[:, 0, :], ACT.Exp, scale=-1.0).then_inc(setup_act.sem, 1)
            act.activation(decay[:, :], vec[:, V_DEC:V_DEC + CT], ACT.Tanh, scale=0.5).then_inc(setup_act.sem, 1)
            for m in range(3):
                weights_high(m)
            act.wait_ge(setup_dve.sem, setup_dve.nth(SET_BIAS))
            gate_r(0, 0)
            act.wait_ge(setup_dve.sem, setup_dve.nth(SET_C2))
            decays(0, 0)
            act.wait_ge(setup_dve.sem, setup_dve.nth(SET_ROWS))
            decay_parts(0, 0)
            gate_i(0, 0)
            gate_r(0, 1)
            decays(0, 1)
            weights_high(3)
            gate_i(0, 1)
            decay_parts(0, 1)
            weights_high(4)
            root(0)
            for m in range(5, SLOTS):
                weights_high(m)
            act.wait_ge(w1_loaded.sem, 16)
            act.activation(wh[:, DOWN:EXPERTS], dense_raw[:, DOWN:EXPERTS], ACT.Copy).then_inc(dense_hi.sem, 1)
            weights_high(8)
            weights_high(9)
            act.activation(b1g[:, :], vec[:, V_E1:V_E1 + NT - 1], ACT.Gelu).then_inc(setup_act.sem, 1)
            y_copy(0)
            weights_high(10)
            weights_high(11)
            x1_norm(0)
            x1_high(0)
            down_copy(0)
            h_gelu(0)
            logit_copy(0)
            hidden(0, 0)
            hidden(0, 1)
            hidden(0, 2)
            route_e(0)
            g1_gelu(0, 0)
            hidden(0, 3)
            route_t(0)
            g1_gelu(0, 1)
            hidden(0, 4)
            gate_copy(0)
            hidden(0, 5)
            weights_high(12)
            weights_high(13)
            experts(0)
            rest(0, False)
            with act.Fori(1, LAST) as r:
                experts(r)
                rest(r, True)
            experts(LAST)
            rest(LAST, True)
            for n in range(2 * FT):
                last_ffn(n)
                if n == OUT_NORM_STEP:
                    out_norm(LAST)
                if n == X3_STEP:
                    last_x3_high(1)
                if n == OUT_ACT:
                    last_out(0)
            last_out(1)

        @block.vector
        def _(dve):
            def x_low(k, c):
                dve.wait_ge(x_hi.sem, x_hi.nth(k, c))
                dve.tensor_tensor(chan_l[:, c, :], xy[:, c, :], chan_h[:, c, :].bitcast(f32), ALU.subtract).then_inc(x_lo.sem, 1)

            def roots(k, c):
                dve.wait_ge(a_sq.sem, a_sq.nth(k, c))
                dve.wait_ge(a_tanh.sem, a_tanh.nth(k, c))
                dve.scalar_tensor_tensor(out=ac[:, c, :], in0=ac[:, 6, :], scalar=1.0, in1=ac[:, c, :], op0=ALU.add, op1=ALU.mult)\
                    .then_inc(w_ready.sem, 1)

            def gated_input(k, c):
                dve.wait_ge(tanh_i.sem, tanh_i.nth(k, c))
                dve.scalar_tensor_tensor(out=ac[:, 2 + c, :], in0=ac[:, 2 + c, :], scalar=1.0, in1=xy[:, c, :], op0=ALU.add, op1=ALU.mult)\
                    .then_inc(ix_ready.sem, 1)

            def cut_decay(k, c):
                dve.wait_ge(a_sq.sem, a_sq.nth(k, c))
                dve.memset(ac[:, 4 + c, :].rearrange("p (s t) -> p s t", t=SEQ)[:, :, 0:1], 0.0).then_inc(a_cut.sem, 1)

            def step_input(k, c):
                dve.wait_ge(w_root.sem, w_root.nth(k, c))
                dve.wait_ge(ix_ready.sem, ix_ready.nth(k, c))
                dve.scalar_tensor_tensor(out=ac[:, 2 + c, :], in0=ac[:, c, :], scalar=0.5, in1=ac[:, 2 + c, :], op0=ALU.mult, op1=ALU.mult)\
                    .then_inc(u_ready.sem, 1)

            def states(k, c):
                dve.wait_ge(u_ready.sem, u_ready.nth(k, c))
                dve.wait_ge(a_cut.sem, a_cut.nth(k, c))
                dve.tensor_tensor_scan(ac[:, c, :], ac[:, 4 + c, :], ac[:, 2 + c, :], 0.0, ALU.mult, ALU.add).then_inc(state_ready.sem, 1)

            def add_x(k, c):
                dve.wait_ge(state_ready.sem, state_ready.nth(k, c))
                dve.tensor_tensor(xy[:, c, :], ac[:, c, :], xy[:, c, :], ALU.add).then_inc(y_ready.sem, 1)

            def stats(i, k, buf, ready, halves=(0, 1)):
                for b in range(NB):
                    if b // 2 in halves:
                        ready(b)
                        dve.bn_stats(st[i][:, b, :], buf[:, b, :]).then_inc(ln_stats[i].sem, 1)
                if 1 not in halves:
                    return
                dve.wait_ge(ln_stats[i].sem, ln_stats[i].nth(k, NB - 1))
                if later(k):
                    apart(dve)
                    dve.wait_ge(ln_done[i].sem, ln_done[i].nth(k - 1, NB - 1))
                apart(dve)
                for b in range(NB):
                    dve.bn_aggr(mv[i][:, b, :], st[i][:, b, :]).then_inc(ln_mv[i].sem, 1)
                dve.wait_ge(ln_mv[i].sem, ln_mv[i].nth(k, NB - 1))
                apart(dve)
                dve.tensor_scalar(rs[i][:, 0, :], mv[i][:, :, 1], EPS, None, ALU.add).then_inc(ln_var[i].sem, 1)
                dve.tensor_scalar(rs[i][:, 2, :], mv[i][:, :, 0], -1.0, None, ALU.mult).then_inc(ln_var[i].sem, 1)

            def x1_stats(k):
                stats(0, k, gate_tok, lambda b: dve.wait_ge(y_copied.sem, y_copied.nth(k, b // 2)))

            def residual1(k, i):
                dve.wait_ge(ln_done[0].sem, ln_done[0].nth(k, NB - 1))
                if later(k):
                    dve.wait_ge(y3_ready.sem, y3_ready.nth(k - 1, 1))
                dve.tensor_tensor(tok[:, 2 * i:2 * i + 2, :], gate_tok[:, 2 * i:2 * i + 2, :], bias_uc[:].unsqueeze(1).broadcast_to([128, 2, D]), ALU.add)\
                    .then_inc(resid1.sem, 1)

            def x1_low(k):
                for c in range(CT):
                    dve.wait_ge(x1_hi.sem, x1_hi.nth(k, c))
                    dve.tensor_tensor(chan_l[:, c, :], M[c][:], chan_h[:, c, :].bitcast(f32), ALU.subtract).then_inc(x1_lo.sem, 1)

            def grid(ap):
                return ap.rearrange("p (b e) -> p b e", e=E)

            def over(ap):
                return ap.unsqueeze(2).broadcast_to([128, NB, E])

            def routing(k, part):
                at = [(0, 3, 12, 17)[part]]

                def step(ins):
                    ins.then_inc(route.sem, 1)
                    dve.wait_ge(route.sem, route.nth(k, at[0]))
                    at[0] += 1

                shifted, expd, t0, k1, l2, k2, t1 = (grid(rt[:, i, :]) for i in range(1, 8))
                rev = grid(cst[:, C_REV:C_REV + NB * E])
                m1, i1, m2, i2, z, d, th, g1, g2, rz, e2 = (r4[:, i, :] for i in (0, 1, 2, 3, 4, 5, 6, 7, 8, 9, 10))
                if part == 0:
                    dve.wait_ge(logit_turned.sem, logit_turned.nth(k))
                    if later(k):
                        dve.wait_ge(gate_turned.sem, gate_turned.nth(k - 1))
                    step(dve.tensor_tensor(rt[:, 0, :], M[1][:, 0:NB * E], bias_r[:, :], ALU.add))
                    step(dve.reduce_max(m1, grid(rt[:, 0, :]), AX.X))
                    step(dve.tensor_tensor(shifted, grid(rt[:, 0, :]), over(m1), ALU.subtract))
                elif part == 1:
                    step(dve.scalar_tensor_tensor(out=rt[:, 3, :], in0=rt[:, 1, :], scalar=0.0, in1=cst[:, C_REV:C_REV + NB * E], op0=ALU.is_ge, op1=ALU.mult))
                    step(dve.reduce_max(i1, t0, AX.X))
                    step(dve.tensor_tensor(k1, rev, over(i1), ALU.is_equal))
                    step(dve.scalar_tensor_tensor(out=rt[:, 5, :], in0=rt[:, 4, :], scalar=-3e38, in1=rt[:, 1, :], op0=ALU.mult, op1=ALU.add))
                    step(dve.reduce_max(m2, l2, AX.X))
                    step(dve.tensor_tensor(t0, l2, over(m2), ALU.is_equal))
                    step(dve.tensor_tensor(t0, t0, rev, ALU.mult))
                    step(dve.reduce_max(i2, t0, AX.X))
                    step(dve.tensor_tensor(k2, rev, over(i2), ALU.is_equal))
                elif part == 2:
                    dve.wait_ge(route_exp.sem, route_exp.nth(k))
                    step(dve.reduce_sum(z, expd, AX.X))
                    step(dve.reciprocal(rz, z))
                    step(dve.tensor_tensor(t1, expd, k2, ALU.mult))
                    step(dve.reduce_sum(e2, t1, AX.X))
                    step(dve.scalar_tensor_tensor(out=d, in0=e2, scalar=-1.0, in1=rz, op0=ALU.add, op1=ALU.mult))
                else:
                    dve.wait_ge(route_tanh.sem, route_tanh.nth(k))
                    step(dve.tensor_scalar(g1, th, 0.5, 0.5, ALU.mult, ALU.add))
                    step(dve.tensor_scalar(g2, th, -0.5, 0.5, ALU.mult, ALU.add))
                    step(dve.tensor_tensor(k1, k1, over(g1), ALU.mult))
                    step(dve.tensor_tensor(k2, k2, over(g2), ALU.mult))
                    step(dve.tensor_tensor(rt[:, 8, :].rearrange("p (e b) -> p b e", b=NB), k1, k2, ALU.add))

            def h_low(k):
                dve.wait_ge(h_act.sem, h_act.nth(k))
                dve.tensor_tensor(sl3[:], h_raw[:], sh[:, 3, :].bitcast(f32), ALU.subtract).then_inc(h_lo.sem, 1)

            def split_g1(k, c):
                dve.wait_ge(g1_act.sem, g1_act.nth(k, c))
                if later(k):
                    dve.wait_ge(attn_out.sem, attn_out.nth(k - 1, 1))
                else:
                    dve.wait_ge(piece_lo.sem, piece_lo.nth(SLOTS - 1))
                dve.tensor_copy(mid_h[:, c, :], ac[:, 5 + c, :]).then_inc(g1_hi.sem, 1)
                dve.wait_ge(g1_hi.sem, g1_hi.nth(k, c))
                dve.tensor_tensor(mid_l[:, c, :], ac[:, 5 + c, :], mid_h[:, c, :].bitcast(f32), ALU.subtract).then_inc(g1_lo.sem, 1)

            def hidden_high(k, t):
                dve.wait_ge(hid_act.sem, hid_act.nth(k, t))
                if t < 3:
                    if later(k):
                        dve.wait_ge(ff_used.sem, ff_used.nth(k - 1, FT - 1))
                else:
                    dve.wait_ge(hid_used.sem, hid_used.nth(k, t - 3))
                dve.tensor_copy(sh[:, t % 3, :], hid[:, t % 3, :]).then_inc(hid_hi.sem, 1)

            def combine(k, o):
                dve.wait_ge(hid_used.sem, hid_used.nth(k, last_tile(o)))
                if o == 0:
                    if later(k):
                        dve.wait_ge(den_z.sem, den_z.nth(k - 1))
                    dve.tensor_scalar(ac[:, 4, :], R[3][:], 0.1, s2b[:, 0:1], ALU.mult, ALU.add).then_inc(combined.sem, 1)
                    return
                e = o - 1
                dve.wait_ge(row_loaded[e % 2].sem, row_loaded[e % 2].nth(k, e // 2))
                if o > 1:
                    dve.wait_ge(summed.sem, summed.nth(k, e - 1))
                else:
                    if later(k):
                        dve.wait_ge(out_stored.sem, out_stored.nth(k - 1))
                    dve.wait_ge(gates_stored.sem, gates_stored.nth(k))
                    dve.wait_ge(combined.sem, combined.nth(k))
                dve.scalar_tensor_tensor(out=hid[:, 4, :], in0=R[3 + o % 3][:], scalar=idle[:, e:e + 1], in1=gate[:, e % 2, :],
                                         op0=ALU.subtract, op1=ALU.mult).then_inc(combined.sem, 1)
                dve.wait_ge(combined.sem, combined.nth(k, o))
                so_far = ac[:, 4, :] if o == 1 else hid[:, 3, :]
                dve.tensor_tensor(hid[:, 3, :], so_far, hid[:, 4, :], ALU.add).then_inc(summed.sem, 1)

            def mixture(k):
                dve.wait_ge(summed.sem, summed.nth(k, E - 1))
                dve.wait_ge(hid_z.sem, hid_z.nth(k, NT - 1))
                dve.tensor_scalar(sh[:, 3, :], hid[:, 3, :], idle_sum[:, 0:1], None, ALU.add).then_inc(m_hi.sem, 1)
                dve.wait_ge(m_hi.sem, m_hi.nth(k))
                dve.scalar_tensor_tensor(out=sl3[:], in0=hid[:, 3, :], scalar=idle_sum[:, 0:1], in1=sh[:, 3, :].bitcast(f32),
                                         op0=ALU.add, op1=ALU.subtract).then_inc(m_lo.sem, 1)

            def flat2(t, i):
                return t[:, 2 * i:2 * i + 2, :].rearrange("p b n -> p (b n)")

            def x2_stats(k):
                for i in range(2):
                    dve.wait_ge(moe_out.sem, moe_out.nth(k, i))
                    dve.wait_ge(resid1.sem, resid1.nth(k, i))
                    dve.tensor_tensor(flat2(tok, i), M[i][:], flat2(tok, i), ALU.add).then_inc(y2_ready.sem, 1)
                stats(1, k, tok, lambda b: dve.wait_ge(y2_ready.sem, y2_ready.nth(k, b // 2)))

            def x2_low(k):
                for c in range(CT):
                    dve.wait_ge(x2_hi.sem, x2_hi.nth(k, c))
                    dve.tensor_tensor(mid_l[:, c, :], M[c][:], mid_h[:, c, :].bitcast(f32), ALU.subtract).then_inc(x2_lo.sem, 1)

            def elu1(k, c, exp, low, phi, slot):
                dve.wait_ge(exp.sem, exp.nth(k, c))
                dve.tensor_scalar(ac[:, slot, :], ac[:, slot, :], 1.0, None, ALU.min).then_inc(low.sem, 1)
                dve.wait_ge(low.sem, low.nth(k, c))
                dve.scalar_tensor_tensor(out=ac[:, slot, :], in0=M[0][:], scalar=0.0, in1=ac[:, slot, :], op0=ALU.max, op1=ALU.add)\
                    .then_inc(phi.sem, 1)

            def keys(k, c):
                elu1(k, c, k_exp, k_min, k_phi, 0)

            def key_scans(k, c):
                dve.wait_ge(k_phi.sem, k_phi.nth(k, c))
                dve.wait_ge(v_z.sem, v_z.nth(k, c))
                dve.tensor_tensor(ac[:, 1, :], M[1][:], ac[:, 0, :], ALU.mult).then_inc(kv_ready.sem, 1)
                dve.wait_ge(kv_ready.sem, kv_ready.nth(k, c))
                for what, dst in ((0, 3 + c), (1, 5 + c)):
                    for s in range(CHUNK // SEQ):
                        at = slice(s * SEQ, (s + 1) * SEQ)
                        dve.tensor_tensor_scan(ac[:, dst, at], decay[:, c:c + 1].broadcast_to([128, SEQ]), ac[:, what, at], 0.0,
                                               ALU.mult, ALU.add).then_inc(scanned.sem, 1)

            def queries(k, c):
                elu1(k, c, q_exp, q_min, q_phi, 2)

            def inverses(k):
                dve.wait_ge(den_turned.sem, den_turned.nth(k))
                dve.tensor_scalar(rden[:, :], M[1][:, 0:NB * HEADS], 1e-6, None, ALU.max).then_inc(den_max.sem, 1)
                dve.wait_ge(den_max.sem, den_max.nth(k))
                dve.reciprocal(rden[:, :], rden[:, :]).then_inc(den_inv.sem, 1)

            def attention(k):
                for c in range(CT):
                    dve.wait_ge(inv_turned.sem, inv_turned.nth(k, c))
                    dve.wait_ge(num_ready.sem, num_ready.nth(k, c))
                    dve.tensor_tensor(ac[:, 5 + c, :], M[c][:], ac[:, 5 + c, :], ALU.mult).then_inc(o_ready.sem, 1)
                for c in range(CT):
                    dve.wait_ge(o_hi.sem, o_hi.nth(k, c))
                    dve.tensor_tensor(mid_l[:, c, :], ac[:, 5 + c, :], mid_h[:, c, :].bitcast(f32), ALU.subtract).then_inc(o_lo.sem, 1)

            def x3_sum(k):
                if isinstance(k, int) and k == 0:
                    dve.wait_ge(piece_lo.sem, piece_lo.nth(PIECES - 1))
                for i in range(2):
                    dve.wait_ge(attn_out.sem, attn_out.nth(k, i))
                    dve.wait_ge(y4_ready.sem, y4_ready.nth(k, 1))
                    dve.tensor_tensor(flat2(tok3, i), M[i][:], flat2(tok, i), ALU.add).then_inc(y3_ready.sem, 1)

            def last_x3_sum(h):
                dve.wait_ge(attn_out.sem, attn_out.nth(LAST, h))
                dve.tensor_tensor(flat2(tok, h), M[h][:], flat2(tok, h), ALU.add).then_inc(y3_ready.sem, 1)

            def x3_stats(k, half):
                stats(2, k, tok3, lambda b: dve.wait_ge(y3_ready.sem, y3_ready.nth(k, b // 2)), (half,))

            def x3_low(k):
                for c in range(CT):
                    dve.wait_ge(x3_hi.sem, x3_hi.nth(k, c))
                    dve.tensor_tensor(ffn_l[:, c, :], M[c][:], ffn_h[:, c, :].bitcast(f32), ALU.subtract).then_inc(x3_lo.sem, 1)

            def ffn(r, j):
                dve.wait_ge(ff_tanh.sem, ff_tanh.nth(r, j))
                p = 2 * (j % 2)
                h = hid[:, j % 3, :]
                dve.scalar_tensor_tensor(out=h, in0=h, scalar=1.0, in1=R[p][:], op0=ALU.add, op1=ALU.mult).then_inc(ff_silu.sem, 1)
                dve.wait_ge(ff_silu.sem, ff_silu.nth(r, j))
                dve.tensor_tensor(h, R[p + 1][:], h, ALU.mult).then_inc(ff_hid.sem, 1)
                dve.wait_ge(ff_hid.sem, ff_hid.nth(r, j))
                if j < 3:
                    dve.wait_ge(hid_used.sem, hid_used.nth(r, NT - 1))
                dve.wait_ge(ff_used.sem, ff_used.nth(r, j - 3))
                dve.tensor_copy(sh[:, j % 3, :], h).then_inc(ff_hi.sem, 1)

            def last_ffn(n):
                dve.wait_ge(ff_tanh.sem, ff_tanh.nth(chunks, n))
                h = hid[:, n % 3, 0:HALF]
                dve.scalar_tensor_tensor(out=h, in0=h, scalar=1.0, in1=R[n % 4][:, 0:HALF], op0=ALU.add, op1=ALU.mult).then_inc(ff_silu.sem, 1)
                dve.wait_ge(ff_silu.sem, ff_silu.nth(chunks, n))
                dve.tensor_tensor(h, R[n % 4][:, HALF:CHUNK], h, ALU.mult).then_inc(ff_hid.sem, 1)
                dve.wait_ge(ff_hid.sem, ff_hid.nth(chunks, n))
                dve.wait_ge(ff_used.sem, ff_used.nth(chunks, n - 3))
                dve.tensor_copy(sh[:, n % 3, 0:HALF], h).then_inc(ff_hi.sem, 1)

            def last_x3_low(h):
                dve.wait_ge(x3_hi.sem, x3_hi.nth(LAST, h))
                at = slice(h * HALF, (h + 1) * HALF)
                dve.tensor_tensor(ffn_l[:, :, at], M[h][:].rearrange("p (c n) -> p c n", c=CT), ffn_h[:, :, at].bitcast(f32), ALU.subtract)\
                    .then_inc(x3_lo.sem, 1)

            def last_stats(i, h, buf):
                at = slice(2 * h, 2 * h + 2)
                for b in (2 * h, 2 * h + 1):
                    dve.wait_ge((y3_ready, y4_ready)[i - 2].sem, (y3_ready, y4_ready)[i - 2].nth((LAST, chunks)[i - 2], h))
                    dve.bn_stats(st[i][:, b, :], buf[:, b, :]).then_inc(ln_stats[i].sem, 1)
                dve.wait_ge(ln_stats[i].sem, ln_stats[i].nth(LAST, 2 * h + 1))
                dve.wait_ge(ln_done[i].sem, ln_done[i].nth(LAST - 1, NB - 1))
                apart(dve)
                for b in (2 * h, 2 * h + 1):
                    dve.bn_aggr(mv[i][:, b, :], st[i][:, b, :]).then_inc(ln_mv[i].sem, 1)
                dve.wait_ge(ln_mv[i].sem, ln_mv[i].nth(LAST, 2 * h + 1))
                dve.tensor_scalar(rs[i][:, 0, at], mv[i][:, at, 1], EPS, None, ALU.add).then_inc(half_var[i].sem, 1)
                dve.tensor_scalar(rs[i][:, 2, at], mv[i][:, at, 0], -1.0, None, ALU.mult).then_inc(half_var[i].sem, 1)

            def last_out(h):
                dve.wait_ge(ff_used.sem, ff_used.nth(chunks, (h + 1) * FT - 1))
                dve.wait_ge(out_stored.sem, out_stored.nth(LAST))
                dve.tensor_tensor(hid[:, 3 + h, :], R[4 + h][:], flat2(tok, h), ALU.add).then_inc(y4_ready.sem, 1)
                last_stats(3, h, y4)

            def out_sum(r):
                for i in range(2):
                    dve.wait_ge(ff_used.sem, ff_used.nth(r, FT - 1))
                    dve.wait_ge(m_lo.sem, m_lo.nth(r))
                    if more_chunks(r):
                        dve.wait_ge(logit_turned.sem, logit_turned.nth(r + 1))
                        dve.wait_ge(gates_stored.sem, gates_stored.nth(r + 1))
                    dve.tensor_tensor(hid[:, 3 + i, :], R[4 + i][:], flat2(tok3, i), ALU.add).then_inc(y4_ready.sem, 1)

            def out_stats(r, half):
                stats(3, r - 1, y4, lambda b: dve.wait_ge(y4_ready.sem, y4_ready.nth(r, b // 2)), (half,))

            def had_combine(j):
                s, second = 1 << (j // 2), j % 2
                v = w2_raw[:].rearrange("p (g two m) -> p g two m", two=2, m=s * D)
                a, b = v[:, :, 0, :], v[:, :, 1, :]
                if j == 0:
                    dve.wait_ge(w2_loaded.sem, 16)
                else:
                    dve.wait_ge(had_step.sem, had_step.nth(j - 1))
                if second:
                    dve.scalar_tensor_tensor(out=a, in0=a, scalar=2.0, in1=b, op0=ALU.mult, op1=ALU.subtract).then_inc(had_step.sem, 1)
                else:
                    dve.tensor_tensor(b, a, b, ALU.subtract).then_inc(had_step.sem, 1)

            def had_low(q):
                dve.wait_ge(had_hi.sem, had_hi.nth(q))
                c = W2 + q * PIECE
                dve.tensor_tensor(wl[:, c:c + PIECE], R[q][:], wh[:, c:c + PIECE].bitcast(f32), ALU.subtract).then_inc(had_lo.sem, 1)

            def experts(r):
                more = more_chunks(r)
                done = 1
                if later(r):
                    x3_low(r - 1)
                for t in range(AHEAD, NT + LAG):
                    if t < NT:
                        hidden_high(r, t)
                    if t in (6, 7) and more:
                        x_low(r + 1, t - 6)
                    if t in G1_TILES:
                        split_g1(r, G1_TILES.index(t))
                    if t in ROOT_TILES and more:
                        roots(r + 1, ROOT_TILES.index(t))
                        cut_decay(r + 1, ROOT_TILES.index(t))
                    if t >= SUMS_TILE and done <= E and last_tile(done) <= t - LAG - 1:
                        combine(r, done)
                        done += 1
                    if more:
                        if t in INPUT_TILES:
                            gated_input(r + 1, INPUT_TILES.index(t))
                        if t in STEP_TILES:
                            step_input(r + 1, STEP_TILES.index(t))
                        if t in STATE_TILES:
                            states(r + 1, STATE_TILES.index(t))
                        if t in Y_TILES:
                            add_x(r + 1, Y_TILES.index(t))
                while done <= E:
                    combine(r, done)
                    done += 1
                mixture(r)

            def rest(r, has_ffn):
                more = more_chunks(r)

                def ff(j):
                    if has_ffn:
                        ffn(r, j)
                    elif j < W2_PIECES:
                        had_low(j)
                    elif j == FT - 1:
                        dve.sem_inc(ff_silu.sem, FT)
                        dve.sem_inc(ff_hid.sem, FT)
                        dve.sem_inc(ff_hi.sem, FT)
                ff(0)
                x2_stats(r)
                if has_ffn:
                    ff(1)
                if more:
                    x1_stats(r + 1)
                if not has_ffn:
                    ff(1)
                x2_low(r)
                ff(2)
                if has_ffn:
                    ff(3)
                if more:
                    x1_low(r + 1)
                if not has_ffn:
                    ff(3)
                ff(4)
                keys(r, 0)
                key_scans(r, 0)
                ff(5)
                queries(r, 0)
                if more:
                    routing(r + 1, 0)
                if not has_ffn:
                    routing(r + 1, 1)
                keys(r, 1)
                key_scans(r, 1)
                queries(r, 1)
                if has_ffn and more:
                    routing(r + 1, 1)
                ff(6)
                if more:
                    routing(r + 1, 2)
                inverses(r)
                if more:
                    routing(r + 1, 3)
                ff(7)
                attention(r)
                if not more:
                    last_x3_sum(0)
                    last_stats(2, 0, tok)
                    last_x3_sum(1)
                    last_stats(2, 1, tok)
                    out_sum(r)
                    last_x3_low(0)
                    out_stats(r, 0)
                    out_stats(r, 1)
                    return
                if has_ffn:
                    out_sum(r)
                else:
                    dve.sem_inc(y4_ready.sem, 2)
                h_low(r + 1)
                x3_sum(r)
                hidden_high(r + 1, 0)
                x3_stats(r, 0)
                hidden_high(r + 1, 1)
                x3_stats(r, 1)
                hidden_high(r + 1, 2)
                if has_ffn:
                    out_stats(r, 0)
                hidden_high(r + 1, 3)
                if has_ffn:
                    out_stats(r, 1)
                hidden_high(r + 1, 4)
                residual1(r + 1, 0)
                combine(r + 1, 0)
                hidden_high(r + 1, 5)
                residual1(r + 1, 1)

            n = [0]

            def link(ins):
                ins.then_inc(setup_dve.sem, 1)
                dve.wait_ge(setup_dve.sem, setup_dve.nth(n[0]))
                n[0] += 1
                return n[0] - 1

            link(dve.memset(neg_half[:, :], -0.5))
            dve.wait_ge(vec_loaded.sem, 16)
            link(dve.tensor_scalar(half_b[:, :], vec[:, V_BA:V_BA + 2 * CT], 0.5, None, ALU.mult))
            dve.wait_ge(w0_loaded.sem, 16)
            dve.tensor_copy(wh[:, 0:DOWN], dense_raw[:, 0:DOWN]).then_inc(dense_hi.sem, 1)
            dve.wait_ge(x_loaded.sem, x_loaded.nth(0))
            for c in range(CT):
                dve.tensor_copy(chan_h[:, c, :], xy[:, c, :]).then_inc(x_hi.sem, 1)
            dve.wait_ge(dense_hi.sem, dense_hi.nth(0))
            dve.tensor_tensor(wl[:, 0:DOWN], dense_raw[:, 0:DOWN], wh[:, 0:DOWN].bitcast(f32), ALU.subtract).then_inc(dense_lo.sem, 1)
            x_low(0, 0)
            x_low(0, 1)
            dve.wait_ge(setup_act.sem, setup_act.nth(1))
            e_, ratio, sq, acc = ser[:, 1, :], ser[:, 2, :], ser[:, 3, :], ser[:, 4, :]
            link(dve.tensor_scalar(ratio, e_, 2.0, None, ALU.add))
            link(dve.reciprocal(ratio, ratio))
            link(dve.tensor_tensor(ratio, ratio, e_, ALU.mult))
            link(dve.tensor_tensor(sq, ratio, ratio, ALU.mult))
            link(dve.tensor_scalar(acc, sq, 1.0 / 17, None, ALU.mult))
            for d in (15, 13, 11, 9, 7, 5, 3):
                link(dve.scalar_tensor_tensor(out=acc, in0=acc, scalar=1.0 / d, in1=sq, op0=ALU.add, op1=ALU.mult))
            link(dve.scalar_tensor_tensor(out=acc, in0=acc, scalar=1.0, in1=ratio, op0=ALU.add, op1=ALU.mult))
            link(dve.tensor_scalar(sq, vec[:, V_LAM:V_LAM + CT], -1.0, 0.0, ALU.mult, ALU.max))
            link(dve.scalar_tensor_tensor(out=sq, in0=acc, scalar=2.0, in1=sq, op0=ALU.mult, op1=ALU.add))
            link(dve.tensor_scalar(c2[:, :], sq, -4.0, None, ALU.mult))
            link(dve.tensor_scalar(nc2[:, :], sq, 4.0, None, ALU.mult))
            assert link(dve.tensor_scalar(s2b[:, :], vec[:, V_S2:V_S2 + 1], 0.1, None, ALU.mult)) == SET_C2
            dve.wait_ge(setup_act.sem, setup_act.nth(2))
            link(dve.tensor_scalar(decay[:, :], decay[:, :], 0.5, 0.5, ALU.mult, ALU.add))
            dve.wait_ge(rows_loaded.sem, 16)
            dve.wait_ge(small_loaded.sem, 16)
            rw = ac[:, 5:7, :].rearrange("p a n -> p (a n)")
            link(dve.tensor_tensor(bias_uc[:, :], rw[:, 0:D], rw[:, D:2 * D], ALU.add))
            assert link(dve.tensor_tensor(bias_r[:, :], rw[:, 2 * D:2 * D + NB * E], cst[:, C_COST:C_COST + NB * E], ALU.subtract)) == SET_ROWS
            roots(0, 0)
            cut_decay(0, 0)
            gated_input(0, 0)
            had_combine(0)
            gated_input(0, 1)
            roots(0, 1)
            cut_decay(0, 1)
            had_combine(1)
            for c in range(CT):
                step_input(0, c)
            for c in range(CT):
                states(0, c)
            for c in range(CT):
                add_x(0, c)
            dve.wait_ge(dense_hi.sem, dense_hi.nth(1))
            dve.tensor_tensor(wl[:, DOWN:EXPERTS], dense_raw[:, DOWN:EXPERTS], wh[:, DOWN:EXPERTS].bitcast(f32), ALU.subtract).then_inc(dense_lo.sem, 1)
            dve.wait_ge(setup_act.sem, setup_act.nth(3))
            link(dve.tensor_copy(b1s[:, :, 0], b1g[:, :]))
            assert link(dve.tensor_tensor(b1s[:, :, 1], b1g[:, :], b1s[:, :, 0].bitcast(f32), ALU.subtract)) == IDLE_SPLIT
            x1_stats(0)
            for j in range(2, 2 * HAD_STEPS):
                had_combine(j)
            x1_low(0)
            h_low(0)
            routing(0, 0)
            hidden_high(0, 0)
            hidden_high(0, 1)
            routing(0, 1)
            dve.wait_ge(idle_z.sem, idle_z.nth(0, 1))
            assert link(dve.tensor_copy(idle2[:, :], R[5][:, 0:2 * E])) == IDLE_COPIED
            parts = idle2[:, :].rearrange("p (e two) -> p e two", two=2)
            link(dve.tensor_tensor(idle[:, :], parts[:, :, 0], parts[:, :, 1], ALU.add))
            link(dve.reduce_sum(idle_sum[:, 0:1], idle[:, :], AX.X))
            link(dve.reduce_sum(idle_sum[:, 1:2], vec[:, V_E2:V_E2 + E], AX.X))
            link(dve.tensor_tensor(idle_sum[:, 0:1], idle_sum[:, 0:1], idle_sum[:, 1:2], ALU.add))
            hidden_high(0, 2)
            routing(0, 2)
            hidden_high(0, 3)
            routing(0, 3)
            hidden_high(0, 4)
            combine(0, 0)
            hidden_high(0, 5)
            dve.wait_ge(piece_lo.sem, piece_lo.nth(SLOTS - 1))
            residual1(0, 0)
            residual1(0, 1)
            experts(0)
            rest(0, False)
            with dve.Fori(1, LAST) as r:
                experts(r)
                rest(r, True)
            experts(LAST)
            rest(LAST, True)
            for n in range(2 * FT):
                last_ffn(n)
                if n == X3_STEP:
                    last_x3_low(1)
                if n == OUT_DVE:
                    last_out(0)
            last_out(1)

        @block.gpsimd
        def _(pool):
            def rstd(i, k):
                pool.wait_ge(ln_var[i].sem, ln_var[i].nth(k, 1))
                pool.tensor_tensor(rs[i][:, 1, :], rs[i][:, 0, :], neg_half[:, :], ALU.pow).then_inc(ln_rstd[i].sem, 1)
                pool.wait_ge(ln_rstd[i].sem, ln_rstd[i].nth(k))
                pool.tensor_tensor(rs[i][:, 3, :], rs[i][:, 1, :], rs[i][:, 2, :], ALU.mult).then_inc(ln_shift[i].sem, 1)

            def last_rstd(i, h):
                at = slice(2 * h, 2 * h + 2)
                pool.wait_ge(half_var[i].sem, half_var[i].nth(0, 2 * h + 1))
                pool.tensor_tensor(rs[i][:, 1, at], rs[i][:, 0, at], neg_half[:, 0:2], ALU.pow).then_inc(half_rstd[i].sem, 1)
                pool.wait_ge(half_rstd[i].sem, half_rstd[i].nth(0, h))
                pool.tensor_tensor(rs[i][:, 3, at], rs[i][:, 1, at], rs[i][:, 2, at], ALU.mult).then_inc(half_shift[i].sem, 1)

            def last_ffn_low(n):
                pool.wait_ge(ff_hi.sem, ff_hi.nth(chunks, n))
                pool.tensor_tensor(sl[:, n % 3, 0:HALF], hid[:, n % 3, 0:HALF], sh[:, n % 3, 0:HALF].bitcast(f32), ALU.subtract)\
                    .then_inc(ff_lo.sem, 1)

            def x1_whole(k):
                pool.wait_ge(x1_lo.sem, x1_lo.nth(k, CT - 1))
                if later(k):
                    pool.wait_ge(o_lo.sem, o_lo.nth(k - 1, CT - 1))
                pool.wait_ge(y_ready.sem, y_ready.nth(k, CT - 1))
                pool.tensor_tensor(ac[:, 5:7, :], chan_h[:].bitcast(f32), chan_l[:].bitcast(f32), ALU.add).then_inc(x1_sum.sem, 1)

            def hidden_low(k, t):
                pool.wait_ge(hid_hi.sem, hid_hi.nth(k, t))
                pool.tensor_tensor(sl[:, t % 3, :], hid[:, t % 3, :], sh[:, t % 3, :].bitcast(f32), ALU.subtract).then_inc(hid_lo.sem, 1)

            def ffn_low(r, j):
                pool.wait_ge(ff_hi.sem, ff_hi.nth(r, j))
                pool.tensor_tensor(sl[:, j % 3, :], hid[:, j % 3, :], sh[:, j % 3, :].bitcast(f32), ALU.subtract).then_inc(ff_lo.sem, 1)

            def numerators(k, c):
                pool.wait_ge(q_phi.sem, q_phi.nth(k, c))
                pool.wait_ge(scanned.sem, scanned.nth(k, 4 * c + 3))
                pool.tensor_tensor(ac[:, 3 + c, :], ac[:, 2, :], ac[:, 3 + c, :], ALU.mult).then_inc(qk_ready.sem, 1)
                pool.tensor_tensor(ac[:, 5 + c, :], ac[:, 2, :], ac[:, 5 + c, :], ALU.mult).then_inc(num_ready.sem, 1)

            def weights_low(m):
                pool.wait_ge(piece_hi.sem, piece_hi.nth(m))
                c = EXPERTS + m * PIECE
                pool.tensor_tensor(wl[:, c:c + PIECE], raw_piece(m), wh[:, c:c + PIECE].bitcast(f32), ALU.subtract).then_inc(piece_lo.sem, 1)

            def experts(r):
                for t in range(AHEAD, NT):
                    hidden_low(r, t)

            def rest(r, has_ffn):
                more = more_chunks(r)

                def ff(j):
                    if has_ffn:
                        ffn_low(r, j)
                    else:
                        weights_low(EARLY + j)
                        if j == FT - 1:
                            pool.sem_inc(ff_lo.sem, FT)
                ff(0)
                rstd(1, r)
                if more:
                    rstd(0, r + 1)
                ff(1)
                ff(2)
                ff(3)
                ff(4)
                ff(5)
                numerators(r, 0)
                numerators(r, 1)
                ff(6)
                ff(7)
                if more:
                    x1_whole(r + 1)
                    hidden_low(r + 1, 0)
                    hidden_low(r + 1, 1)
                if more:
                    rstd(2, r)
                else:
                    last_rstd(2, 0)
                    last_rstd(2, 1)
                if more:
                    hidden_low(r + 1, 2)
                    hidden_low(r + 1, 3)
                if has_ffn:
                    rstd(3, r - 1)
                if more:
                    hidden_low(r + 1, 4)
                    hidden_low(r + 1, 5)

            for m in range(10):
                weights_low(m)
            rstd(0, 0)
            weights_low(10)
            weights_low(11)
            x1_whole(0)
            for t in range(AHEAD):
                hidden_low(0, t)
            weights_low(12)
            weights_low(13)
            experts(0)
            rest(0, False)
            with pool.Fori(1, LAST) as r:
                experts(r)
                rest(r, True)
            experts(LAST)
            rest(LAST, True)
            for n in range(2 * FT):
                last_ffn_low(n)
                if n == OUT_POOL:
                    last_rstd(3, 0)
            last_rstd(3, 1)


SET_BIAS = 1
SET_C2 = 19
SET_ROWS = 22
IDLE_SPLIT = 24
IDLE_COPIED = 25


def kernel(**inputs):
    import numpy as np
    import concourse.bacc as bacc
    from concourse import mybir
    from concourse.bass_utils import run_bass_kernel_spmd as run

    g = {n: np.asarray(a) for n, a in inputs.items()}
    x = g["L0_attn_x"]
    batch, seq, d = x.shape

    def rows_first(a):
        k, n = a.shape
        return a.reshape(k // 128, 128, n).transpose(1, 0, 2).reshape(128, -1)

    parts = [g["L0_attn_Wa"].T, g["L0_attn_Wx"].T, g["L0_ffn_down_w"], g["L0_ffn_router_w"], g["L0_ffn_shared_w1"],
             g["L0_ffn_shared_w2"], g["L0_ffn_core_w"], g["L0_ffn_up_w"]]
    for e in range(E):
        parts += [g[f"L0_ffn_e{e}_w1"], g[f"L0_ffn_e{e}_w2"]]
    parts += [g["L1_attn_w_qkv"], g["L1_attn_w_out"], g["L1_ffn_W1"].T, g["L1_ffn_W3"].T, g["L1_ffn_W2"].T]
    weights = np.concatenate([rows_first(a) for a in parts], axis=1)

    cols = [g["L0_attn_ba"], g["L0_attn_bx"], g["L0_attn_Lam"], g["L0_ffn_down_b"], g["L0_ffn_shared_b1"], g["L0_ffn_shared_b2"]]
    cols += [g[f"L0_ffn_e{e}_b1"] for e in range(E)] + [g[f"L0_ffn_e{e}_b2"] for e in range(E)]
    cols += [np.repeat(g["L1_attn_decay_param"], HEAD)]
    vectors = np.concatenate([a.reshape(-1, 128).T for a in cols], axis=1)
    rows = np.concatenate([g["L0_ffn_up_b"], g["L0_ffn_core_b"], np.tile(g["L0_ffn_router_b"], NB)])

    had = np.array([[1.0]])
    while had.shape[0] < 128:
        had = np.block([[had, had], [had, -had]])
    head = np.zeros((128, CT, HEADS))
    for p in range(128):
        for c in range(CT):
            head[p, c, (c * 128 + p) // HEAD] = 1.0
    consts = np.concatenate([np.eye(128), had / (2 * FF ** 0.5), head.reshape(128, -1),
                             np.tile(np.arange(E, 0, -1.0), (128, NB)), np.tile(np.array(COST), (128, NB))], axis=1).astype(np.float32)

    arrays = {"x_t": x.reshape(batch * seq, d).T, "weights": weights, "vectors": vectors, "rows": rows, "consts": consts}
    arrays = {n: np.ascontiguousarray(a) for n, a in arrays.items()}
    nc = bacc.Bacc("TRN2", target_bir_lowering=False, num_devices=1)
    aps = [nc.dram_tensor("in_" + n, a.shape, mybir.dt.from_np(a.dtype), kind="ExternalInput").ap() for n, a in arrays.items()]
    out = nc.dram_tensor("out", (batch * seq, d), mybir.dt.float32, kind="ExternalOutput").ap()
    program(nc, *aps, out)
    r = run(nc, [{"in_" + n: a for n, a in arrays.items()}], core_ids=[0])
    return r.results[0]["out"].reshape(batch, seq, d)
```
